# Optimizing a Trainium2 kernel written in Bass

```python
import numpy as np
import jax
import jax.numpy as jnp

def _softmax(x, axis=-1):
    return jax.nn.softmax(x, axis=axis)

def _gelu(x):
    return jax.nn.gelu(x, approximate=True)

def _silu(x):
    return jax.nn.silu(x)

def _sigmoid(x):
    return jax.nn.sigmoid(x)

def _layernorm(x, axis=-1, eps=1e-05):
    m = jnp.mean(x, axis=axis, keepdims=True)
    v = jnp.var(x, axis=axis, keepdims=True)
    return (x - m) / jnp.sqrt(v + eps)

def _scatter_add(tgt, idx, src, axis=0):
    return tgt.at[idx].add(src)

def _segment_sum(src, seg, n):
    return jax.ops.segment_sum(src, seg, n)
kernel_name = 'mk_xattn_ffn_d4_seqx_r8_88ec3f'

def setup_inputs(seed: int=0):
    np.random.seed(seed)
    _w = jnp.asarray

    def _rec_inputs():
        import jax
        import jax.numpy as jnp
        _rk = jax.random.key(seed)
        x = 7.22e-05 + 1 * jax.random.normal(jax.random.fold_in(_rk, 1), (4, 256, 128), jnp.float32)
        _lenS = 256 - jax.random.randint(jax.random.fold_in(_rk, 7), (4,), 0, max(1, 256 // 4) + 1, jnp.int32)
        _lenS2 = 64 - jax.random.randint(jax.random.fold_in(_rk, 8), (4,), 0, max(1, 64 // 4) + 1, jnp.int32)
        _ctx_1024P = jax.random.normal(jax.random.fold_in(_rk, 11), (4, 16, 128), jnp.float32)
        _ctx_1024c = jax.random.dirichlet(jax.random.fold_in(_rk, 511), 0.3 * jnp.ones((16,), jnp.float32), (4, 64))
        _ctx_1024t = jnp.einsum('bsk,bkd->bsd', _ctx_1024c, _ctx_1024P)
        _ctx_1024t = _ctx_1024t * jax.lax.rsqrt(jnp.mean(jnp.square(_ctx_1024t)) + 1e-12) * 0.953939
        ctx_1024 = 4.13588e-05 + 0.999923 * (_ctx_1024t + 0.3 * jax.random.normal(jax.random.fold_in(_rk, 611), (4, 64, 128), jnp.float32))
        _validS = jnp.arange(256)[None, :] < _lenS[:, None]
        _validS2 = jnp.arange(64)[None, :] < _lenS2[:, None]
        _causal = jnp.tril(jnp.ones((256, 256), dtype=bool))
        mask_BxS2_bk0 = jnp.logical_not(jnp.broadcast_to(_validS2[:, :], (4, 64)))
        mask_1x1xSxS2_ik0 = jnp.where(jnp.broadcast_to(_validS2[0:1, None, None, :], (1, 1, 256, 64)), 0, 1).astype(jnp.int32)
        mask_BxS2_ik1 = jnp.where(jnp.broadcast_to(_validS2[:, :], (4, 64)), 1, 0).astype(jnp.int32)
        return (x, ctx_1024, mask_BxS2_bk0, mask_1x1xSxS2_ik0, mask_BxS2_ik1)
    x, ctx_1024, mask_BxS2_bk0, mask_1x1xSxS2_ik0, mask_BxS2_ik1 = _rec_inputs()

    def _L0_xattn_setup():
        import jax, jax.numpy as jnp
        import numpy as np
        import math
        D_MODEL = 128
        D_K = 64
        D_V = 64
        N_HEADS = 16
        key = jax.random.key(seed)
        ks = jax.random.split(key, 12)
        bz, sq = (4, 256)
        std = math.sqrt(1.0 / D_MODEL)
        inp = {'q': jax.random.normal(ks[0], (bz, sq, D_MODEL), jnp.float32), 'k': jax.random.normal(ks[1], (bz, sq, D_MODEL), jnp.float32), 'v': jax.random.normal(ks[2], (bz, sq, D_MODEL), jnp.float32), 'att_mask': jax.random.randint(ks[3], (bz, sq), 0, 2).astype(bool), 'Wq': std * jax.random.normal(ks[4], (D_K * N_HEADS, D_MODEL), jnp.float32), 'bq': jnp.zeros((D_K * N_HEADS,), jnp.float32), 'Wk': std * jax.random.normal(ks[5], (D_K * N_HEADS, D_MODEL), jnp.float32), 'bk': jnp.zeros((D_K * N_HEADS,), jnp.float32), 'Wv': std * jax.random.normal(ks[6], (D_V * N_HEADS, D_MODEL), jnp.float32), 'bv': jnp.zeros((D_V * N_HEADS,), jnp.float32), 'Wo': std * jax.random.normal(ks[7], (D_MODEL, D_V * N_HEADS), jnp.float32), 'bo': jnp.zeros((D_MODEL,), jnp.float32)}
        return inp
    _L0_xattn_all = _L0_xattn_setup()
    _L0_xattn_in = {k: v for k, v in _L0_xattn_all.items() if k in ('Wq', 'bq', 'Wk', 'bk', 'Wv', 'bv', 'Wo', 'bo')}
    del _L0_xattn_all

    def _L0_ffn_setup():
        import jax, jax.numpy as jnp
        import numpy as np
        EPS = 1e-05

        def rmsnorm(x):
            return x * jax.lax.rsqrt(jnp.mean(x * x, axis=-1, keepdims=True) + EPS)

        def act_quant(x):
            scale = 127.0 / jnp.clip(jnp.max(jnp.abs(x), axis=-1, keepdims=True), 1e-05)
            q = jnp.clip(jnp.round(x * scale), -128.0, 127.0) / scale
            return x + jax.lax.stop_gradient(q - x)

        def weight_quant(w):
            scale = 1.0 / jnp.clip(jnp.mean(jnp.abs(w)), 1e-05)
            q = jnp.clip(jnp.round(w * scale), -1.0, 1.0) / scale
            return w + jax.lax.stop_gradient(q - w)

        def bitlinear(x, w, b):
            xq = act_quant(rmsnorm(x))
            wq = weight_quant(w)
            return jnp.einsum('bsd,fd->bsf', xq, wq) + b
        key = jax.random.key(seed)
        k0, k1, k2 = jax.random.split(key, 3)
        B, S, D, F = (2, 1024, 128, 512)
        x = jax.random.normal(k0, (B, S, D), dtype=jnp.float32)
        w1 = jax.random.normal(k1, (F, D), dtype=jnp.float32) * (1.0 / np.sqrt(D))
        b1 = jnp.zeros((F,), dtype=jnp.float32)
        w2 = jax.random.normal(k2, (D, F), dtype=jnp.float32) * (1.0 / np.sqrt(F))
        b2 = jnp.zeros((D,), dtype=jnp.float32)
        return {'x': x, 'w1': w1, 'b1': b1, 'w2': w2, 'b2': b2}
    _L0_ffn_all = _L0_ffn_setup()
    _L0_ffn_in = {k: v for k, v in _L0_ffn_all.items() if k in ('w1', 'b1', 'w2', 'b2')}
    del _L0_ffn_all

    def _L1_xattn_setup():
        import jax, jax.numpy as jnp
        import numpy as np
        B, L, E, H = (2, 256, 128, 16)
        Dh = E // H
        key = jax.random.key(seed)
        ks = jax.random.split(key, 12)
        s = 0.02
        inp = {'x_q': jax.random.normal(ks[0], (B, L, E), jnp.float32), 'x_k': jax.random.normal(ks[1], (B, L, E), jnp.float32), 'x_v': jax.random.normal(ks[2], (B, L, E), jnp.float32), 'mask': jnp.tril(jnp.ones((L, L), jnp.int32))[None, None], 'Wq': jax.random.normal(ks[3], (E, E), jnp.float32) * s, 'bq': jnp.zeros((E,), jnp.float32), 'Wk': jax.random.normal(ks[4], (E, E), jnp.float32) * s, 'bk': jnp.zeros((E,), jnp.float32), 'Wv': jax.random.normal(ks[5], (E, E), jnp.float32) * s, 'bv': jnp.zeros((E,), jnp.float32), 'Wo': jax.random.normal(ks[6], (E, E), jnp.float32) * s, 'bo': jnp.zeros((E,), jnp.float32)}
        return inp
    _L1_xattn_all = _L1_xattn_setup()
    _L1_xattn_in = {k: v for k, v in _L1_xattn_all.items() if k in ('Wq', 'bq', 'Wk', 'bk', 'Wv', 'bv', 'Wo', 'bo')}
    del _L1_xattn_all

    def _L1_ffn_setup():
        import jax, jax.numpy as jnp
        import numpy as np
        BITS = 8
        LORA_RANK = 16
        LORA_ALPHA = 32
        SCALING = LORA_ALPHA / LORA_RANK

        def fake_quant_weight(w, bits=BITS):
            qmax = 2.0 ** (bits - 1) - 1
            scale = jnp.max(jnp.abs(w)) / qmax
            wq = jnp.clip(jnp.round(w / scale), -qmax - 1, qmax) * scale
            return w + jax.lax.stop_gradient(wq - w)

        def qat_lora_linear(x, W, b, A, B):
            Wq = fake_quant_weight(W)
            base = jnp.einsum('bsi,oi->bso', x, Wq) + b
            lora = jnp.einsum('bsr,or->bso', jnp.einsum('bsi,ri->bsr', x, A), B)
            return base + SCALING * lora
        key = jax.random.key(seed)
        ks = jax.random.split(key, 9)
        d, f = (128, 512)
        s_in = 1.0 / np.sqrt(d)
        s_ff = 1.0 / np.sqrt(f)
        return {'hidden_states': jax.random.normal(ks[0], (4, 256, d), jnp.float32), 'W_fc': jax.random.normal(ks[1], (f, d), jnp.float32) * s_in, 'b_fc': jnp.zeros((f,), jnp.float32), 'A_fc': jax.random.normal(ks[2], (LORA_RANK, d), jnp.float32) * s_in, 'B_fc': jnp.zeros((f, LORA_RANK), jnp.float32), 'W_proj': jax.random.normal(ks[3], (d, f), jnp.float32) * s_ff, 'b_proj': jnp.zeros((d,), jnp.float32), 'A_proj': jax.random.normal(ks[4], (LORA_RANK, f), jnp.float32) * s_ff, 'B_proj': jnp.zeros((d, LORA_RANK), jnp.float32)}
    _L1_ffn_all = _L1_ffn_setup()
    _L1_ffn_in = {k: v for k, v in _L1_ffn_all.items() if k in ('W_fc', 'b_fc', 'A_fc', 'B_fc', 'W_proj', 'b_proj', 'A_proj', 'B_proj')}
    del _L1_ffn_all

    def _L2_xattn_setup():
        import jax, jax.numpy as jnp
        import numpy as np
        import math
        B, T, EMB = (4, 256, 128)
        PAD_TAIL = 32
        key = jax.random.key(seed)
        kq, kk, kv = jax.random.split(key, 3)
        query = jax.random.normal(kq, (B, T, EMB), dtype=jnp.float32)
        k = jax.random.normal(kk, (B, T, EMB), dtype=jnp.float32)
        value = jax.random.normal(kv, (B, T, EMB), dtype=jnp.float32)
        attention_mask = jnp.concatenate([jnp.ones((B, T - PAD_TAIL), dtype=jnp.int32), jnp.zeros((B, PAD_TAIL), dtype=jnp.int32)], axis=1)
        return {'query': query, 'key': k, 'value': value, 'attention_mask': attention_mask}
    _L2_xattn_all = _L2_xattn_setup()
    _L2_xattn_in = {k: v for k, v in _L2_xattn_all.items() if k in ()}
    del _L2_xattn_all

    def _L2_ffn_setup():
        import jax, jax.numpy as jnp
        import numpy as np
        B, T, D = (4, 256, 128)
        H, DH, E, SEL = (8, 64, 5, 2)

        def _topk_mask(logits, k):
            _, idx = jax.lax.top_k(logits, k)
            return jnp.sum(jax.nn.one_hot(idx, logits.shape[-1], dtype=logits.dtype), axis=-2)
        key = jax.random.key(seed)
        ks = jax.random.split(key, 7)
        s = 0.02
        x = jax.random.normal(ks[0], (B, T, D), dtype=jnp.float32)
        Wq = jax.random.normal(ks[1], (D, H * DH), dtype=jnp.float32) * s
        Wk = jax.random.normal(ks[2], (D, H * DH), dtype=jnp.float32) * s
        Ws = jax.random.normal(ks[3], (D, H * E), dtype=jnp.float32) * s
        Wd = jax.random.normal(ks[4], (D, H * E), dtype=jnp.float32) * s
        Wv = jax.random.normal(ks[5], (E, D, DH), dtype=jnp.float32) * s
        Wo = jax.random.normal(ks[6], (E, DH, D), dtype=jnp.float32) * s
        return {'x': x, 'Wq': Wq, 'Wk': Wk, 'Ws': Ws, 'Wd': Wd, 'Wv': Wv, 'Wo': Wo}
    _L2_ffn_all = _L2_ffn_setup()
    _L2_ffn_in = {k: v for k, v in _L2_ffn_all.items() if k in ('Wq', 'Wk', 'Ws', 'Wd', 'Wv', 'Wo')}
    del _L2_ffn_all

    def _L3_xattn_setup():
        import jax, jax.numpy as jnp
        import numpy as np
        import math
        D_MODEL = 128
        N_HEADS = 16
        D_K = D_MODEL // N_HEADS
        ROPE_BASE = 10000.0

        def rope_cos_sin(seq_len, d_k, base=ROPE_BASE, dtype=jnp.float32):
            inv_freq = 1.0 / base ** (jnp.arange(0, d_k, 2, dtype=dtype) / d_k)
            pos = jnp.arange(seq_len, dtype=dtype)
            freqs = jnp.outer(pos, inv_freq)
            return (jnp.cos(freqs), jnp.sin(freqs))

        def apply_rope(x, cos, sin):
            x1 = x[..., 0::2]
            x2 = x[..., 1::2]
            c = cos[None, None]
            s = sin[None, None]
            r1 = x1 * c - x2 * s
            r2 = x1 * s + x2 * c
            return jnp.stack([r1, r2], axis=-1).reshape(x.shape)
        key = jax.random.key(seed)
        ks = jax.random.split(key, 7)
        B, T = (2, 256)
        scale = 1.0 / math.sqrt(D_MODEL)
        return {'query': jax.random.normal(ks[0], (B, T, D_MODEL), jnp.float32), 'key': jax.random.normal(ks[1], (B, T, D_MODEL), jnp.float32), 'value': jax.random.normal(ks[2], (B, T, D_MODEL), jnp.float32), 'Wq': jax.random.normal(ks[3], (D_MODEL, D_MODEL), jnp.float32) * scale, 'Wk': jax.random.normal(ks[4], (D_MODEL, D_MODEL), jnp.float32) * scale, 'Wv': jax.random.normal(ks[5], (D_MODEL, D_MODEL), jnp.float32) * scale, 'Wo': jax.random.normal(ks[6], (D_MODEL, D_MODEL), jnp.float32) * scale}
    _L3_xattn_all = _L3_xattn_setup()
    _L3_xattn_in = {k: v for k, v in _L3_xattn_all.items() if k in ('Wq', 'Wk', 'Wv', 'Wo')}
    del _L3_xattn_all

    def _L3_ffn_setup():
        import jax, jax.numpy as jnp
        import numpy as np
        H = 128
        I = 352
        E = 8
        TOP_K = 2

        def _moe(hidden_states, router_w, gate_w, up_w, down_w):
            B, S, Hd = hidden_states.shape
            x = hidden_states.reshape(-1, Hd)
            logits = x @ router_w.T
            probs = jax.nn.softmax(logits.astype(jnp.float32), axis=-1)
            top_w, top_idx = jax.lax.top_k(probs, TOP_K)
            top_w = top_w.astype(x.dtype)
            onehot = jax.nn.one_hot(top_idx, E, dtype=x.dtype)
            w_te = jnp.einsum('tk,tke->te', top_w, onehot)
            g = jnp.einsum('th,eih->tei', x, gate_w)
            u = jnp.einsum('th,eih->tei', x, up_w)
            h = jax.nn.silu(g) * u
            y = jnp.einsum('tei,ehi,te->th', h, down_w, w_te)
            return y.reshape(B, S, Hd)
        key = jax.random.key(seed)
        ks = jax.random.split(key, 5)
        s = 0.02
        return {'hidden_states': jax.random.normal(ks[0], (2, 128, H), dtype=jnp.float32), 'router_w': jax.random.normal(ks[1], (E, H), dtype=jnp.float32) * s, 'gate_w': jax.random.normal(ks[2], (E, I, H), dtype=jnp.float32) * s, 'up_w': jax.random.normal(ks[3], (E, I, H), dtype=jnp.float32) * s, 'down_w': jax.random.normal(ks[4], (E, H, I), dtype=jnp.float32) * s}
    _L3_ffn_all = _L3_ffn_setup()
    _L3_ffn_in = {k: v for k, v in _L3_ffn_all.items() if k in ('router_w', 'gate_w', 'up_w', 'down_w')}
    del _L3_ffn_all
    return {'x': x, 'ctx_1024': ctx_1024, 'mask_BxS2_bk0': mask_BxS2_bk0, 'mask_1x1xSxS2_ik0': mask_1x1xSxS2_ik0, 'mask_BxS2_ik1': mask_BxS2_ik1, 'L0_xattn_Wq': _L0_xattn_in['Wq'], 'L0_xattn_bq': _L0_xattn_in['bq'], 'L0_xattn_Wk': _L0_xattn_in['Wk'], 'L0_xattn_bk': _L0_xattn_in['bk'], 'L0_xattn_Wv': _L0_xattn_in['Wv'], 'L0_xattn_bv': _L0_xattn_in['bv'], 'L0_xattn_Wo': _L0_xattn_in['Wo'], 'L0_xattn_bo': _L0_xattn_in['bo'], 'L0_ffn_w1': _L0_ffn_in['w1'], 'L0_ffn_b1': _L0_ffn_in['b1'], 'L0_ffn_w2': _L0_ffn_in['w2'], 'L0_ffn_b2': _L0_ffn_in['b2'], 'L1_xattn_Wq': _L1_xattn_in['Wq'], 'L1_xattn_bq': _L1_xattn_in['bq'], 'L1_xattn_Wk': _L1_xattn_in['Wk'], 'L1_xattn_bk': _L1_xattn_in['bk'], 'L1_xattn_Wv': _L1_xattn_in['Wv'], 'L1_xattn_bv': _L1_xattn_in['bv'], 'L1_xattn_Wo': _L1_xattn_in['Wo'], 'L1_xattn_bo': _L1_xattn_in['bo'], 'L1_ffn_W_fc': _L1_ffn_in['W_fc'], 'L1_ffn_b_fc': _L1_ffn_in['b_fc'], 'L1_ffn_A_fc': _L1_ffn_in['A_fc'], 'L1_ffn_B_fc': _L1_ffn_in['B_fc'], 'L1_ffn_W_proj': _L1_ffn_in['W_proj'], 'L1_ffn_b_proj': _L1_ffn_in['b_proj'], 'L1_ffn_A_proj': _L1_ffn_in['A_proj'], 'L1_ffn_B_proj': _L1_ffn_in['B_proj'], 'L2_ffn_Wq': _L2_ffn_in['Wq'], 'L2_ffn_Wk': _L2_ffn_in['Wk'], 'L2_ffn_Ws': _L2_ffn_in['Ws'], 'L2_ffn_Wd': _L2_ffn_in['Wd'], 'L2_ffn_Wv': _L2_ffn_in['Wv'], 'L2_ffn_Wo': _L2_ffn_in['Wo'], 'L3_xattn_Wq': _L3_xattn_in['Wq'], 'L3_xattn_Wk': _L3_xattn_in['Wk'], 'L3_xattn_Wv': _L3_xattn_in['Wv'], 'L3_xattn_Wo': _L3_xattn_in['Wo'], 'L3_ffn_router_w': _L3_ffn_in['router_w'], 'L3_ffn_gate_w': _L3_ffn_in['gate_w'], 'L3_ffn_up_w': _L3_ffn_in['up_w'], 'L3_ffn_down_w': _L3_ffn_in['down_w']}

def reference(x, ctx_1024, mask_BxS2_bk0, mask_1x1xSxS2_ik0, mask_BxS2_ik1, L0_xattn_Wq, L0_xattn_bq, L0_xattn_Wk, L0_xattn_bk, L0_xattn_Wv, L0_xattn_bv, L0_xattn_Wo, L0_xattn_bo, L0_ffn_w1, L0_ffn_b1, L0_ffn_w2, L0_ffn_b2, L1_xattn_Wq, L1_xattn_bq, L1_xattn_Wk, L1_xattn_bk, L1_xattn_Wv, L1_xattn_bv, L1_xattn_Wo, L1_xattn_bo, L1_ffn_W_fc, L1_ffn_b_fc, L1_ffn_A_fc, L1_ffn_B_fc, L1_ffn_W_proj, L1_ffn_b_proj, L1_ffn_A_proj, L1_ffn_B_proj, L2_ffn_Wq, L2_ffn_Wk, L2_ffn_Ws, L2_ffn_Wd, L2_ffn_Wv, L2_ffn_Wo, L3_xattn_Wq, L3_xattn_Wk, L3_xattn_Wv, L3_xattn_Wo, L3_ffn_router_w, L3_ffn_gate_w, L3_ffn_up_w, L3_ffn_down_w):
    import jax
    import jax.numpy as jnp

    def _L0_xattn_ref(q, k, v, att_mask, Wq, bq, Wk, bk, Wv, bv, Wo, bo):
        import jax, jax.numpy as jnp
        import numpy as np
        import math
        D_MODEL = 128
        D_K = 64
        D_V = 64
        N_HEADS = 16
        bz, len_q, _ = q.shape
        len_k = k.shape[1]
        q_h = (q @ Wq.T + bq).reshape(bz, len_q, N_HEADS, D_K).transpose(0, 2, 1, 3)
        k_h = (k @ Wk.T + bk).reshape(bz, len_k, N_HEADS, D_K).transpose(0, 2, 1, 3)
        v_h = (v @ Wv.T + bv).reshape(bz, len_k, N_HEADS, D_V).transpose(0, 2, 1, 3)
        scores = jnp.einsum('bhqd,bhkd->bhqk', q_h, k_h) / jnp.sqrt(jnp.float32(D_K))
        scores = jnp.where(att_mask[:, None, None, :], jnp.float32(-1000000000.0), scores)
        attn = jax.nn.softmax(scores, axis=-1)
        out = jnp.einsum('bhqk,bhkd->bhqd', attn, v_h)
        out = out.transpose(0, 2, 1, 3).reshape(bz, len_q, N_HEADS * D_V)
        return out @ Wo.T + bo

    def _L0_ffn_ref(x, w1, b1, w2, b2):
        import jax, jax.numpy as jnp
        import numpy as np
        EPS = 1e-05

        def rmsnorm(x):
            return x * jax.lax.rsqrt(jnp.mean(x * x, axis=-1, keepdims=True) + EPS)

        def act_quant(x):
            scale = 127.0 / jnp.clip(jnp.max(jnp.abs(x), axis=-1, keepdims=True), 1e-05)
            q = jnp.clip(jnp.round(x * scale), -128.0, 127.0) / scale
            return x + jax.lax.stop_gradient(q - x)

        def weight_quant(w):
            scale = 1.0 / jnp.clip(jnp.mean(jnp.abs(w)), 1e-05)
            q = jnp.clip(jnp.round(w * scale), -1.0, 1.0) / scale
            return w + jax.lax.stop_gradient(q - w)

        def bitlinear(x, w, b):
            xq = act_quant(rmsnorm(x))
            wq = weight_quant(w)
            return jnp.einsum('bsd,fd->bsf', xq, wq) + b
        h = bitlinear(x, w1, b1)
        h = jax.nn.gelu(h, approximate=False)
        return bitlinear(h, w2, b2)

    def _L1_xattn_ref(x_q, x_k, x_v, mask, Wq, bq, Wk, bk, Wv, bv, Wo, bo):
        import jax, jax.numpy as jnp
        import numpy as np
        B, L, E, H = (2, 256, 128, 16)
        Dh = E // H
        N, Lq, _ = x_q.shape
        Lk = x_k.shape[1]
        q = (x_q @ Wq.T + bq).reshape(N, Lq, H, Dh).transpose(0, 2, 1, 3)
        k = (x_k @ Wk.T + bk).reshape(N, Lk, H, Dh).transpose(0, 2, 1, 3)
        v = (x_v @ Wv.T + bv).reshape(N, Lk, H, Dh).transpose(0, 2, 1, 3)
        scores = jnp.einsum('bhqd,bhkd->bhqk', q, k) / jnp.sqrt(jnp.float32(Dh))
        scores = jnp.where(mask == 0, jnp.float32(-1000000000.0), scores)
        attn = jax.nn.softmax(scores, axis=-1)
        out = jnp.einsum('bhqk,bhkd->bhqd', attn, v)
        out = out.transpose(0, 2, 1, 3).reshape(N, Lq, E)
        return out @ Wo.T + bo

    def _L1_ffn_ref(hidden_states, W_fc, b_fc, A_fc, B_fc, W_proj, b_proj, A_proj, B_proj):
        import jax, jax.numpy as jnp
        import numpy as np
        BITS = 8
        LORA_RANK = 16
        LORA_ALPHA = 32
        SCALING = LORA_ALPHA / LORA_RANK

        def fake_quant_weight(w, bits=BITS):
            qmax = 2.0 ** (bits - 1) - 1
            scale = jnp.max(jnp.abs(w)) / qmax
            wq = jnp.clip(jnp.round(w / scale), -qmax - 1, qmax) * scale
            return w + jax.lax.stop_gradient(wq - w)

        def qat_lora_linear(x, W, b, A, B):
            Wq = fake_quant_weight(W)
            base = jnp.einsum('bsi,oi->bso', x, Wq) + b
            lora = jnp.einsum('bsr,or->bso', jnp.einsum('bsi,ri->bsr', x, A), B)
            return base + SCALING * lora
        h = qat_lora_linear(hidden_states, W_fc, b_fc, A_fc, B_fc)
        h = jax.nn.gelu(h, approximate=False)
        h = qat_lora_linear(h, W_proj, b_proj, A_proj, B_proj)
        return h

    def _L2_xattn_ref(query, key, value, attention_mask):
        import jax, jax.numpy as jnp
        import numpy as np
        import math
        B, T, EMB = (4, 256, 128)
        PAD_TAIL = 32
        Bq, Tq, emb = query.shape
        Tk = key.shape[1]
        scale = 1.0 / math.sqrt(emb)
        scores = jnp.einsum('bqd,bkd->bqk', query, key) * scale
        neg_inf = jnp.float32(-jnp.inf)
        if Tq == Tk:
            causal = jnp.triu(jnp.ones((Tq, Tk), dtype=bool), k=1)
            scores = jnp.where(causal[None, :, :], neg_inf, scores)
        key_pad = (attention_mask == 0)[:, None, :]
        scores = jnp.where(key_pad, neg_inf, scores)
        attn = jax.nn.softmax(scores, axis=-1)
        out = jnp.einsum('bqk,bkd->bqd', attn, value)
        return out

    def _L2_ffn_ref(x, Wq, Wk, Ws, Wd, Wv, Wo):
        import jax, jax.numpy as jnp
        import numpy as np
        B, T, D = (4, 256, 128)
        H, DH, E, SEL = (8, 64, 5, 2)

        def _topk_mask(logits, k):
            _, idx = jax.lax.top_k(logits, k)
            return jnp.sum(jax.nn.one_hot(idx, logits.shape[-1], dtype=logits.dtype), axis=-2)
        e, d, dh = Wv.shape
        h = Wq.shape[1] // dh
        b, t, _ = x.shape
        scale = dh ** (-0.5)
        q = (x @ Wq).reshape(b, t, h, dh).transpose(0, 2, 1, 3)
        k = (x @ Wk).reshape(b, t, h, dh).transpose(0, 2, 1, 3)
        gl_v = (x @ Ws).reshape(b, t, h, e)
        wv = _topk_mask(gl_v, SEL) * jax.nn.sigmoid(gl_v)
        xv = jnp.einsum('btd,edk->btek', x, Wv)
        v = jnp.einsum('bthe,btek->bhtk', wv, xv)
        scores = jnp.einsum('bhid,bhjd->bhij', q * scale, k)
        probs = jax.nn.softmax(scores, axis=-1)
        attn = jnp.einsum('bhij,bhjd->bihd', probs, v)
        gl_o = (x @ Wd).reshape(b, t, h, e)
        mask_o = _topk_mask(gl_o, SEL)
        out = jnp.einsum('bthe,bthk,ekd->btd', mask_o, attn, Wo)
        return out

    def _L3_xattn_ref(query, key, value, Wq, Wk, Wv, Wo):
        import jax, jax.numpy as jnp
        import numpy as np
        import math
        D_MODEL = 128
        N_HEADS = 16
        D_K = D_MODEL // N_HEADS
        ROPE_BASE = 10000.0

        def rope_cos_sin(seq_len, d_k, base=ROPE_BASE, dtype=jnp.float32):
            inv_freq = 1.0 / base ** (jnp.arange(0, d_k, 2, dtype=dtype) / d_k)
            pos = jnp.arange(seq_len, dtype=dtype)
            freqs = jnp.outer(pos, inv_freq)
            return (jnp.cos(freqs), jnp.sin(freqs))

        def apply_rope(x, cos, sin):
            x1 = x[..., 0::2]
            x2 = x[..., 1::2]
            c = cos[None, None]
            s = sin[None, None]
            r1 = x1 * c - x2 * s
            r2 = x1 * s + x2 * c
            return jnp.stack([r1, r2], axis=-1).reshape(x.shape)
        B, Tq, _ = query.shape
        Tk = key.shape[1]
        Q = (query @ Wq.T).reshape(B, Tq, N_HEADS, D_K).transpose(0, 2, 1, 3)
        K = (key @ Wk.T).reshape(B, Tk, N_HEADS, D_K).transpose(0, 2, 1, 3)
        V = (value @ Wv.T).reshape(B, Tk, N_HEADS, D_K).transpose(0, 2, 1, 3)
        cos_q, sin_q = rope_cos_sin(Tq, D_K)
        cos_k, sin_k = rope_cos_sin(Tk, D_K)
        Q = apply_rope(Q, cos_q, sin_q)
        K = apply_rope(K, cos_k, sin_k)
        scores = jnp.einsum('bhqd,bhkd->bhqk', Q, K) / math.sqrt(D_K)
        attn = jax.nn.softmax(scores, axis=-1)
        out = jnp.einsum('bhqk,bhkd->bhqd', attn, V)
        out = out.transpose(0, 2, 1, 3).reshape(B, Tq, D_MODEL)
        return out @ Wo.T

    def _L3_ffn_ref(hidden_states, router_w, gate_w, up_w, down_w):
        import jax, jax.numpy as jnp
        import numpy as np
        H = 128
        I = 352
        E = 8
        TOP_K = 2

        def _moe(hidden_states, router_w, gate_w, up_w, down_w):
            B, S, Hd = hidden_states.shape
            x = hidden_states.reshape(-1, Hd)
            logits = x @ router_w.T
            probs = jax.nn.softmax(logits.astype(jnp.float32), axis=-1)
            top_w, top_idx = jax.lax.top_k(probs, TOP_K)
            top_w = top_w.astype(x.dtype)
            onehot = jax.nn.one_hot(top_idx, E, dtype=x.dtype)
            w_te = jnp.einsum('tk,tke->te', top_w, onehot)
            g = jnp.einsum('th,eih->tei', x, gate_w)
            u = jnp.einsum('th,eih->tei', x, up_w)
            h = jax.nn.silu(g) * u
            y = jnp.einsum('tei,ehi,te->th', h, down_w, w_te)
            return y.reshape(B, S, Hd)
        return _moe(hidden_states, router_w, gate_w, up_w, down_w)
    x = x + _L0_xattn_ref(_layernorm(x, axis=-1), ctx_1024, ctx_1024, mask_BxS2_bk0, L0_xattn_Wq, L0_xattn_bq, L0_xattn_Wk, L0_xattn_bk, L0_xattn_Wv, L0_xattn_bv, L0_xattn_Wo, L0_xattn_bo)
    x = x + _L0_ffn_ref(_layernorm(x, axis=-1), L0_ffn_w1, L0_ffn_b1, L0_ffn_w2, L0_ffn_b2)
    x = x + _L1_xattn_ref(_layernorm(x, axis=-1), ctx_1024, ctx_1024, mask_1x1xSxS2_ik0, L1_xattn_Wq, L1_xattn_bq, L1_xattn_Wk, L1_xattn_bk, L1_xattn_Wv, L1_xattn_bv, L1_xattn_Wo, L1_xattn_bo)
    x = x + _L1_ffn_ref(_layernorm(x, axis=-1), L1_ffn_W_fc, L1_ffn_b_fc, L1_ffn_A_fc, L1_ffn_B_fc, L1_ffn_W_proj, L1_ffn_b_proj, L1_ffn_A_proj, L1_ffn_B_proj)
    x = x + _L2_xattn_ref(_layernorm(x, axis=-1), ctx_1024, ctx_1024, mask_BxS2_ik1)
    x = x + _L2_ffn_ref(_layernorm(x, axis=-1), L2_ffn_Wq, L2_ffn_Wk, L2_ffn_Ws, L2_ffn_Wd, L2_ffn_Wv, L2_ffn_Wo)
    x = x + _L3_xattn_ref(_layernorm(x, axis=-1), ctx_1024, ctx_1024, L3_xattn_Wq, L3_xattn_Wk, L3_xattn_Wv, L3_xattn_Wo)
    x = x + _L3_ffn_ref(_layernorm(x, axis=-1), L3_ffn_router_w, L3_ffn_gate_w, L3_ffn_up_w, L3_ffn_down_w)
    return x

_drawn_inputs = setup_inputs


def setup_inputs(seed=0):
    import zlib

    import numpy as np

    out = dict(_drawn_inputs(seed))
    spreads = {'L0_xattn_bq': (0.0, 0.1),
     'L0_xattn_bk': (0.0, 0.8),
     'L0_xattn_bv': (0.0, 0.1),
     'L0_xattn_bo': (0.0, 0.1),
     'L0_ffn_b1': (0.0, 0.1),
     'L0_ffn_b2': (0.0, 0.1),
     'L1_xattn_bq': (0.0, 0.8),
     'L1_xattn_bk': (0.0, 0.8),
     'L1_xattn_bv': (0.0, 0.8),
     'L1_xattn_bo': (0.0, 0.1),
     'L1_ffn_b_fc': (0.0, 0.1),
     'L1_ffn_B_fc': (0.0, 0.1),
     'L1_ffn_b_proj': (0.0, 0.1),
     'L1_ffn_B_proj': (0.0, 0.1)}
    factors = {'L1_xattn_Wq': 8.0,
     'L1_xattn_Wk': 8.0,
     'L1_xattn_Wv': 4.082,
     'L1_xattn_Wo': 3.471,
     'L2_ffn_Wq': 8.0,
     'L2_ffn_Wk': 8.0,
     'L2_ffn_Ws': 3.022,
     'L3_ffn_router_w': 8.0,
     'L3_ffn_gate_w': 8.0,
     'L3_ffn_up_w': 8.0,
     'L3_ffn_down_w': 8.0}
    for name, (base, spread) in spreads.items():
        noise = np.random.default_rng([zlib.crc32(name.encode()), seed]).standard_normal(out[name].shape)
        drawn = base * np.exp(spread * noise) if base else spread * noise
        out[name] = jnp.asarray(drawn.astype(out[name].dtype))
    for name, factor in factors.items():
        out[name] = (out[name] * factor).astype(out[name].dtype)
    return out
```

```python
from contextlib import ExitStack

import numpy as np

import concourse.bass as bass
from concourse import mybir

F32 = mybir.dt.float32
BF16 = mybir.dt.bfloat16
I32 = mybir.dt.int32
U8 = mybir.dt.uint8
ALU = mybir.AluOpType
ACT = mybir.ActivationFunctionType
X_AXIS = mybir.AxisListType.X
R_ADD = bass.bass_isa.ReduceOp.add
R_MAX = bass.bass_isa.ReduceOp.max

P = 128
D = 128
B, S, CTX = 4, 256, 64
TILES = S // P
NC8 = 8
SIDE = 16
FF = 512
H2, DH2, E2, SEL = 8, 64, 5, 2
G2 = 2 * H2
XV = E2 * DH2
E3, I3 = 8, 352
CHUNKS = [(0, 128), (128, 128), (256, 96)]
UNITS = E3 * len(CHUNKS)
RING = 4
LAG = 2
EPS = 1e-5
RMS_EPS = 1e-5
QMAX = 127.0
ROUND = 12582912.0
MASKED = -1e30
SCALE_L0 = 0.125
SCALE_L1 = float(1.0 / np.sqrt(np.float32(8)))
SCALE_L2X = float(1.0 / np.sqrt(128.0))
SCALE_L2F = 0.125
SCALES = [SCALE_L0, SCALE_L1, SCALE_L1]
CLAMPS = [-1e9 / SCALE_L0, -1e9 / SCALE_L1, None]
LORA_SCALE = 2.0

WA = {"ctxT": (0, 256), "WkT": (256, 1024), "WvT": (1280, 1024), "Wq": (2304, 1024), "WoT": (3328, 1024)}
COLS = {"bq0": (0, 8), "bk0": (8, 8), "bv0": (16, 8), "bq1": (24, 1), "bk1": (25, 1), "bfc": (26, 4)}
ROWS = {"bo0": (0, 128), "b2": (128, 128), "bo1": (256, 128), "bpj": (384, 128), "b1": (512, 512), "bv1": (1024, 128)}
WC = {n: (128 * k, 128) for k, n in enumerate(
    ["Wq1", "Wk1", "Wv1", "Wo1", "Wq3", "Wq3s", "Wk3", "Wk3s", "Wv3", "Wo3"])}
WC["ctxT2"] = (1280, 512)
LORA = {"Afc": (0, 128), "BfcT": (128, 512), "Apj": (640, 512), "BpjT": (1152, 128)}
WE = {"Wq": (0, 512), "Wk": (512, 512), "VSD": (1024, 400), "router": (1424, 8)}
CONST = {"ident": (0, 128), "cos": (128, 256), "sin": (384, 256), "block": (640, 16)}

LN_OF_XT = [0, 2, 3, 4, 5, 6, 7]
POW = {0: 0, 1: 1, "rms1": 2, "rms2": 3, 2: 4, 3: 5, 4: 6, 5: 7, 6: 8, 7: 9}
N_POW = 10
N_XT = 2 * len(LN_OF_XT)
DVE_STEPS = 214


def build(nc, x, wa, cols, rows, wb, wc, wd, lora, we, wo2, ctxn, gateup, down, const, mask0, mask1, mask2, out):
    ctx = ExitStack()
    with ctx:
        def sb(name, shape, dt=F32):
            return ctx.enter_context(nc.sbuf_tensor(name, shape, dt))

        def sem(name):
            return ctx.enter_context(nc.semaphore(name))

        wc_sb = sb("wc_sb", [P, 1792])
        we_sb = sb("we_sb", [P, 1432])
        cols_sb = sb("cols_sb", [P, 30])
        rows_sb = sb("rows_sb", [P, 1152])
        const_sb = sb("const_sb", [P, 656])
        wo2_sb = sb("wo2_sb", [P, 2, D])
        wo2b_sb = sb("wo2b_sb", [XV - 2 * P, D])
        ctxn_sb = sb("ctxn_sb", [CTX, B, D])
        ctxb = sb("ctxb", [CTX, D])
        ctxT_sb = sb("ctxT_sb", [P, B, CTX])
        gu_sb = sb("gu_sb", [P, 2, E3 * I3])
        dn_sb = sb("dn_sb", [P, E3, len(CHUNKS), D])
        ident_bf = sb("ident_bf", [P, P], BF16)
        ones_bf = sb("ones_bf", [4, P], BF16)
        w1q = sb("w1q", [P, FF], BF16)
        w2q = sb("w2q", [P, FF // P, D], BF16)
        wfc = sb("wfc", [P, FF])
        wpj = sb("wpj", [P, FF // P, D])
        wmean = sb("wmean", [P, 2])
        M0 = sb("M0", [P, B, NC8, P])
        VO0 = sb("VO0", [P, B, NC8, D])
        bias0 = sb("bias0", [4, B, NC8 * P], BF16)
        KT = [None, sb("KT1", [P, B, CTX]), sb("KT3", [P, B, CTX])]
        Kbd = [None, sb("Kbd1", [P, 16, CTX]), sb("Kbd3", [P, 16, CTX])]
        Vbd = [None, sb("Vbd1", [P, B, NC8, 18]), sb("Vbd3", [P, B, NC8, 18])]
        mneg1 = sb("mneg1", [P, TILES, CTX], BF16)
        mneg2 = sb("mneg2", [1, B, CTX], BF16)
        xall = sb("xall", [P, B * TILES, D])
        oall = xall
        X = sb("X", [P, TILES, D])
        XB = sb("XB", [P, TILES, D])
        XH = sb("XH", [P, TILES, D])
        XT = sb("XT", [P, TILES * P])
        st = sb("st", [P, TILES, 6])
        mv = sb("mv", [P, TILES, 2])
        ve = sb("ve", [P, TILES])
        rs = sb("rs", [P, TILES])
        mhalf = sb("mhalf", [P, TILES])
        filler = sb("filler", [P, 32])
        work = sb("work", [P, TILES, 2560])
        E = work[:, :, 0:1024]
        PT = work[:, :, 1024:2048]
        prod = work
        PF = work[:, :, 0:2048].rearrange("p t (h q) -> p t h q", h=H2)
        mx = sb("mx", [P, TILES, 16])
        mxc = sb("mxc", [P, TILES, 16])
        sm = sb("sm", [P, TILES, 16])
        rc = sb("rc", [P, TILES, 16])
        QT = sb("QT", [P, TILES, P])
        rope = sb("rope", [P, TILES, 2, P])
        AO = sb("AO", [P, TILES, D])
        AOT = sb("AOT", [P, TILES, P])
        q_small = sb("q_small", [P, 8, TILES])
        qbf = sb("qbf", [P, TILES, FF], BF16)
        qTbf = sb("qTbf", [P, TILES, FF], BF16)
        GT = sb("GT", [P, FF // P, TILES * P])
        QF = GT
        KF = sb("KF", [P, H2 // 2, S])
        XG = sb("XG", [P, TILES, XV + E2 * G2])
        cmp = sb("cmp", [P, TILES * G2, E2, E2])
        cnt = sb("cnt", [P, TILES * G2, E2])
        th = sb("th", [P, TILES, E2 * H2])
        wv = sb("wv", [P, TILES, H2, E2])
        mo = sb("mo", [P, TILES, H2, E2])
        V = sb("V", [P, TILES, FF])
        EF = sb("EF", [P, TILES, H2, S])
        mxf = sb("mxf", [P, TILES, H2])
        nmf = sb("nmf", [P, TILES, H2])
        smf = sb("smf", [P, TILES, H2])
        rcf = sb("rcf", [P, TILES, H2])
        Amix = sb("Amix", [P, TILES, XV])
        AT = sb("AT", [P, TILES, 3, P])
        SG = V[:, :, :].rearrange("p t (r q) -> p (t r) q", q=S)
        HT = sb("HT", [P, RING, S])
        rmx = sb("rmx", [P, TILES, 4])
        pr = sb("pr", [P, TILES, E3])
        cmp3 = sb("cmp3", [P, TILES, E3, E3])
        cnt3 = sb("cnt3", [P, TILES, E3])
        wte = sb("wte", [P, TILES, E3])
        KTbd = EF[:, :, :, :].rearrange("p a b c -> p (a b c)").rearrange("p (c b k) -> p c b k", c=NC8, b=B)
        VTbd = work[:, :, :].rearrange("p a b -> p (a b)")[:, 0:4096].rearrange("p (c b k) -> p c b k", c=NC8, b=B)
        wa_sb = gu_sb[:, :, :].rearrange("p a b -> p (a b)")[:, 0:4352]
        dn_flat = dn_sb[:, :, :, :].rearrange("p a b c -> p (a b c)")
        wb_sb = dn_flat[:, 0:1024]
        wd_sb = dn_flat[:, 1024:2048]
        wtmp = dn_flat[:, 2048:3072]
        wtmp2 = GT[:, :, :].rearrange("p a b -> p (a b)")
        lora_sb = SG[0:16, :, :].rearrange("p a b -> p (a b)")
        loraB_sb = HT[0:16, :, :].rearrange("p a b -> p (a b)")
        KT1 = KT[1][:, :, :].rearrange("p b k -> p (b k)")
        KT3a = KF[:, 1, :]
        KT3b = KF[:, 2, :]
        KT3 = KT[2][:, :, :].rearrange("p b k -> p (b k)")
        bpart = sb("bpart", [P, 3, B, NC8], BF16)
        bres = sb("bres", [P, 2, 32])
        bpT = sb("bpT", [96, P], BF16)
        wstat = sb("wstat", [P, 4])
        wred = sb("wred", [P, 4])
        wsc = sb("wsc", [P, 4])
        m0w = sb("m0w", [1, B * CTX // 4], I32)
        m0row = sb("m0row", [1, B, CTX], BF16)
        m1i = sb("m1i", [P, TILES, CTX], I32)
        m2i = sb("m2i", [1, B, CTX], I32)

        ps = ctx.enter_context(nc.psum_tensor("ps", [P, 8, 512], F32))

        def SC(s, h):
            return ps[:, 4 * s + h, :]

        def TR(s):
            return ps[:, 4 * s + 2, :]

        def OU(s):
            return ps[:, 4 * s + 3, :]

        def part(t, table, name):
            a, n = table[name]
            return t[:, a:a + n]

        def wcol(name):
            return part(wc_sb, WC, name)

        ident = part(const_sb, CONST, "ident")
        cosT = part(const_sb, CONST, "cos")
        sinT = part(const_sb, CONST, "sin")
        blockm = part(const_sb, CONST, "block")

        ld_a = sem("ld_a")
        ld_small = sem("ld_small")
        ld_masks = sem("ld_masks")
        ld_x = sem("ld_x")
        ld_b = sem("ld_b")
        ld_c = sem("ld_c")
        ld_d = sem("ld_d")
        ld_e = sem("ld_e")
        ld_moe = sem("ld_moe")
        bias_rows = sem("bias_rows")
        stored = sem("stored")
        memsets = sem("memsets")
        mrows = sem("mrows")
        prep_mm = sem("prep_mm")
        prep_act = sem("prep_act")
        prep_dve = sem("prep_dve")
        wstat_ready = sem("wstat_ready")
        wred_ready = sem("wred_ready")
        kt_ready = sem("kt_ready")
        kbd_ready = sem("kbd_ready")
        bsplit = sem("bsplit")
        prep_done = sem("prep_done")
        dve_seq = sem("dve_seq")
        var_ready = sem("var_ready")
        rstd_ready = sem("rstd_ready")
        xb_ready = sem("xb_ready")
        xhat_ready = sem("xhat_ready")
        xT_psum = sem("xT_psum")
        xT_ready = sem("xT_ready")
        scores_ready = sem("scores_ready")
        shifted = sem("shifted")
        exp_ready = sem("exp_ready")
        ctxb_ready = sem("ctxb_ready")
        recip_ready = sem("recip_ready")
        norm_ready = sem("norm_ready")
        pT_psum = sem("pT_psum")
        pT_ready = sem("pT_ready")
        attn_out = sem("attn_out")
        quant_ready = sem("quant_ready")
        quantT_psum = sem("quantT_psum")
        quantT_ready = sem("quantT_ready")
        bit_out = sem("bit_out")
        hid_ready = sem("hid_ready")
        gelu_ready = sem("gelu_ready")
        qT_psum = sem("qT_psum")
        qT_ready = sem("qT_ready")
        heads_ready = sem("heads_ready")
        headsT_psum = sem("headsT_psum")
        headsT_ready = sem("headsT_ready")
        proj_out = sem("proj_out")
        fc_psum = sem("fc_psum")
        fc_gelu = sem("fc_gelu")
        pj_out = sem("pj_out")
        sx_psum = sem("sx_psum")
        sx_neg = sem("sx_neg")
        sx_exp = sem("sx_exp")
        sxT_psum = sem("sxT_psum")
        sxT_ready = sem("sxT_ready")
        sx_out = sem("sx_out")
        gate_psum = sem("gate_psum")
        gate_ready = sem("gate_ready")
        tanh_ready = sem("tanh_ready")
        qf_psum = sem("qf_psum")
        qf_ready = sem("qf_ready")
        kf_ready = sem("kf_ready")
        v_ready = sem("v_ready")
        sf_psum = sem("sf_psum")
        nmf_ready = sem("nmf_ready")
        ef_ready = sem("ef_ready")
        pf_psum = sem("pf_psum")
        pfa_ready = sem("pfa_ready")
        pfd_ready = sem("pfd_ready")
        pv_out = sem("pv_out")
        mix_ready = sem("mix_ready")
        mixT_psum = sem("mixT_psum")
        mixT_ready = sem("mixT_ready")
        swo_out = sem("swo_out")
        router_psum = sem("router_psum")
        rneg_ready = sem("rneg_ready")
        rexp_ready = sem("rexp_ready")
        up_psum = sem("up_psum")
        silu_ready = sem("silu_ready")
        h_ready = sem("h_ready")
        down_psum = sem("down_psum")
        comb_done = sem("comb_done")
        out_ready = sem("out_ready")

        JOBS = ([("K0", c, "ad") for c in range(NC8)] + [("M0", c, "a") for c in range(NC8)] + [("b0", 0, "d")]
                + [("V0", c, "ad") for c in range(NC8)] + [("VO", c, "da"[c % 2]) for c in range(NC8)]
                + [("b0T", 0, "a")]
                + [("K1", 0, "d"), ("V1", 0, "d"), ("K3", 0, "d"), ("V3", 0, "d"), ("Lfc", 0, "d"), ("Lpj", 0, "d")])
        JOB = {(k, c): n for n, (k, c, _) in enumerate(JOBS)}

        def read_by(engine, n):
            return sum(engine in r for _, _, r in JOBS[:n + 1])

        block = ctx.enter_context(nc.Block())

        @block.sync
        def _(sp):
            sp.dma_start(wa_sb[:, 0:2304], wa[:, 0:2304]).then_inc(ld_a, 16)
            sp.dma_start(wa_sb[:, 2304:4352], wa[:, 2304:4352]).then_inc(ld_a, 16)
            sp.dma_start(cols_sb[:, :], cols).then_inc(ld_small, 16)
            sp.dma_start(const_sb[:, :], const).then_inc(ld_small, 16)
            sp.dma_start(xall[:, :, :], x.rearrange("(t p) d -> p t d", p=P)).then_inc(ld_x, 16)
            sp.dma_start(wb_sb, wb).then_inc(ld_b, 16)
            sp.dma_start(rows_sb[:, :], rows.to_broadcast([P, 1152])).then_inc(ld_small, 16)
            sp.dma_start(wc_sb[:, :], wc).then_inc(ld_c, 16)
            sp.dma_start(wd_sb, wd).then_inc(ld_d, 16)
            sp.dma_start(lora_sb[:, 0:640], lora[:, 0:640]).then_inc(ld_d, 16)
            sp.dma_start(loraB_sb[:, 0:640], lora[:, 640:1280]).then_inc(ld_d, 16)
            sp.dma_start(we_sb[:, :], we).then_inc(ld_e, 16)
            sp.dma_start(wo2_sb[:, :, :], wo2[0:256, :].rearrange("(c p) d -> p c d", p=P)).then_inc(ld_e, 16)
            sp.dma_start(wo2b_sb[:, :], wo2[256:320, :]).then_inc(ld_e, 16)
            sp.dma_start(ctxT_sb[:, :, :], wa[:, 0:256].rearrange("p (b k) -> p b k", b=B)).then_inc(ld_e, 16)
            sp.dma_start(ctxn_sb[:, :, :], ctxn.rearrange("b k d -> k b d")).then_inc(ld_e, 16)
            sp.wait_ge(mrows, 1)
            for b in range(B):
                sp.dma_start(bias0[0:1, b, :].rearrange("p (n k) -> p n k", k=CTX),
                             m0row[:, b, :].unsqueeze(1).to_broadcast([1, 16, CTX])).then_inc(bias_rows, 16)
            sp.wait_ge(prep_act, read_by("a", JOB["b0T", 0]))
            for r in range(3):
                sp.dma_start(bias0[r + 1:r + 2, :, :].rearrange("p b (c k) -> p (b c) k", k=P),
                             bpT[32 * r:32 * r + 32, :]).then_inc(bias_rows, 16)
            sp.wait_ge(prep_mm, len(JOBS))
            sp.wait_ge(prep_dve, read_by("d", len(JOBS)))
            sp.dma_start(gu_sb[:, :, :], gateup).then_inc(ld_moe, 16)
            for c, (i0, m) in enumerate(CHUNKS):
                sp.dma_start(dn_sb[0:m, :, c, :], down[:, i0:i0 + m, :].rearrange("e i d -> i e d")).then_inc(ld_moe, 16)
            out_t = out.rearrange("(t p) d -> p t d", p=P)
            with sp.Fori(0, B) as i:
                sp.wait_ge(out_ready, i * 2 + 2)
                sp.dma_start(out_t[:, bass.ds(2 * i, 2), :], oall[:, bass.ds(2 * i, 2), :]).then_inc(stored, 16)
            sp.wait_ge(stored, 16 * B)

        @block.gpsimd
        def _(pool):
            pool.memset(KTbd, 0.0).then_inc(memsets, 1)
            pool.memset(VTbd, 0.0).then_inc(memsets, 1)
            for v in Vbd[1:]:
                pool.memset(v[:, :, :, :], 0.0).then_inc(memsets, 1)
            pool.memset(mhalf[:, :], -0.5).then_inc(memsets, 1)
            pool.memset(ones_bf[:, :], 1.0).then_inc(memsets, 1)
            pool.dma_start(m0w[:, :], mask0).then_inc(ld_masks, 16)
            pool.dma_start(m1i[:, :, :], mask1.rearrange("(t p) k -> p t k", p=P)).then_inc(ld_masks, 16)
            pool.dma_start(m2i[:, :, :], mask2).then_inc(ld_masks, 16)
            pool.wait_ge(wstat_ready, 1)
            pool.partition_all_reduce(wred[:, 0:2], wstat[:, 0:2], P, R_ADD).then_inc(wred_ready, 1)
            pool.wait_ge(wstat_ready, 2)
            pool.partition_all_reduce(wred[:, 2:4], wstat[:, 2:4], P, R_MAX).then_inc(wred_ready, 1)
            pool.wait_ge(ld_small, 48)
            pool.wait_ge(kt_ready, 2)
            pool.wait_ge(ld_e, 80)

            with pool.Fori(0, B) as i:
                def power(which):
                    pool.wait_ge(var_ready, i * N_POW + POW[which] + 1)
                    pool.tensor_tensor(rs[:, :], ve[:, :], mhalf[:, :], ALU.pow).then_inc(rstd_ready, 1)

                def add_bias(name, src):
                    pool.tensor_tensor(XB[:, :, :], src,
                                       part(rows_sb, ROWS, name).unsqueeze(1).to_broadcast([P, TILES, D]),
                                       ALU.add).then_inc(xb_ready, 1)

                def small_keys(a):
                    pool.tensor_tensor(Kbd[a][:, :, :], KT[a][:, i, :].unsqueeze(1).to_broadcast([P, 16, CTX]),
                                       blockm.unsqueeze(2).to_broadcast([P, 16, CTX]), ALU.mult).then_inc(kbd_ready, 1)

                power(0)
                add_bias("bo0", xall[:, bass.ds(2 * i, 2), :])
                small_keys(1)
                for s in range(TILES):
                    pool.wait_ge(recip_ready, i * 2 + s + 1)
                    for h in range(2):
                        e = E[:, s, 512 * h:512 * h + 512].rearrange("p (n k) -> p n k", k=CTX)
                        pool.tensor_tensor(e, e, rc[:, s, 8 * h:8 * h + 8].unsqueeze(2).to_broadcast([P, 8, CTX]),
                                           ALU.mult).then_inc(norm_ready, 1)
                power(1)
                add_bias("b2", X[:, :, :])
                power("rms1")
                power("rms2")
                power(2)
                add_bias("bo1", X[:, :, :])
                power(3)
                add_bias("bpj", X[:, :, :])
                pool.tensor_copy(ctxb[:, :], ctxn_sb[:, i, :]).then_inc(ctxb_ready, 1)
                power(4)
                power(5)
                small_keys(2)
                power(6)
                power(7)

        @block.scalar
        def _(act):
            def copy(out_ap, in_ap):
                return act.activation(out_ap, in_ap, ACT.Copy)

            act.wait_ge(ld_small, 48)
            act.wait_ge(memsets, 2)
            for n, (kind, c, readers) in enumerate(JOBS):
                if "a" not in readers:
                    continue
                act.wait_ge(prep_mm, n + 1)
                bank = ps[:, n % 8, :]
                if kind in ("K0", "V0"):
                    dst, bias = (KTbd, "bk0") if kind == "K0" else (VTbd, "bv0")
                    ins = act.activation(dst[0:64, c, :, 0:CTX], bank[0:64, 0:256].rearrange("p (b k) -> p b k", b=B),
                                         ACT.Identity, bias=part(cols_sb, COLS, bias)[0:64, c:c + 1])
                elif kind == "M0":
                    ins = copy(M0[:, :, c, :], bank.rearrange("p (b k) -> p b k", b=B))
                elif kind == "VO":
                    ins = copy(VO0[:, :, c, :], bank.rearrange("p (b k) -> p b k", b=B))
                else:
                    ins = copy(bpT[:, :], bank.bitcast(BF16)[0:96, 0:P])
                ins.then_inc(prep_act, 1)

            with act.Fori(0, B) as i:
                def x_transposed(l):
                    k = 2 * LN_OF_XT.index(l)
                    for s in range(TILES):
                        act.wait_ge(xT_psum, i * N_XT + k + s + 1)
                        copy(XT[:, s * P:(s + 1) * P], TR(s)[:, 0:P]).then_inc(xT_ready, 1)

                def softmax(a):
                    for s in range(TILES):
                        for h in range(2):
                            act.wait_ge(shifted, i * 12 + 4 * a + 2 * s + h + 1)
                            e = E[:, s, 512 * h:512 * h + 512]
                            act.activation(e, e, ACT.Exp, scale=SCALES[a]).then_inc(exp_ready, 1)
                    for s in range(TILES):
                        for h in range(2):
                            act.wait_ge(pT_psum, i * 12 + 4 * a + 2 * s + h + 1)
                            copy(PT[:, s, 512 * h:512 * h + 512], SC(s, h)).then_inc(pT_ready, 1)

                def heads_transposed(n):
                    for s in range(TILES):
                        act.wait_ge(headsT_psum, i * 4 + 2 * n + s + 1)
                        copy(AOT[:, s, :], TR(s)[:, 0:P]).then_inc(headsT_ready, 1)

                x_transposed(0)
                softmax(0)
                for s in range(TILES):
                    act.wait_ge(quantT_psum, i * 4 + s + 1)
                    copy(qTbf[:, s, 0:P], TR(s).bitcast(BF16)[:, 0:P]).then_inc(quantT_ready, 1)
                for s in range(TILES):
                    act.wait_ge(hid_ready, i * 2 + s + 1)
                    act.activation(E[:, s, 512:1024], E[:, s, 0:512], ACT.Gelu).then_inc(gelu_ready, 1)
                for s in range(TILES):
                    act.wait_ge(quantT_psum, i * 4 + 2 + s + 1)
                    copy(qTbf[:, s, :], TR(s).bitcast(BF16)[:, 0:FF]).then_inc(quantT_ready, 1)
                x_transposed(2)
                for s in range(TILES):
                    act.wait_ge(qT_psum, i * 4 + s + 1)
                    act.activation(QT[:, s, :], OU(s)[:, 0:P], ACT.Identity,
                                   bias=part(cols_sb, COLS, "bq1")).then_inc(qT_ready, 1)
                softmax(1)
                heads_transposed(0)
                x_transposed(3)
                for c in range(FF // P):
                    act.wait_ge(fc_psum, i * 4 + c + 1)
                    act.activation(GT[:, c, :], SC(c // 2, c % 2)[:, 0:256], ACT.Gelu,
                                   bias=part(cols_sb, COLS, "bfc")[:, c:c + 1]).then_inc(fc_gelu, 1)
                x_transposed(4)
                for s in range(TILES):
                    act.wait_ge(sx_neg, i * 2 + s + 1)
                    act.activation(E[:, s, 0:CTX], OU(s)[:, 0:CTX], ACT.Exp, bias=mxc[:, s, 0:1], scale=SCALE_L2X,
                                   accum_out=sm[:, s, 0:1]).then_inc(sx_exp, 1)
                for s in range(TILES):
                    act.wait_ge(sxT_psum, i * 2 + s + 1)
                    copy(PT[0:CTX, s, 0:P], TR(s)[0:CTX, 0:P]).then_inc(sxT_ready, 1)
                x_transposed(5)
                for s in range(TILES):
                    act.wait_ge(gate_psum, i * 2 + s + 1)
                    copy(XG[:, s, :], OU(s)[:, 0:400]).then_inc(gate_ready, 1)
                for c in range(2):
                    act.wait_ge(qf_psum, i * 4 + c + 1)
                    copy(QF[:, 2 * c:2 * c + 2, :].rearrange("p a b -> p (a b)"), SC(0, c)).then_inc(qf_ready, 1)
                for s in range(TILES):
                    act.wait_ge(gate_ready, i * 2 + s + 1)
                    act.activation(th[:, s, :], XG[:, s, XV:XV + 40], ACT.Tanh, scale=0.5).then_inc(tanh_ready, 1)
                for s in range(TILES):
                    for u in range(2):
                        act.wait_ge(nmf_ready, i * 4 + 2 * s + u + 1)
                        for g in range(4):
                            h = 4 * u + g
                            bank = ((SC(s, 0), SC(s, 1)), (TR(s), OU(s)))[u][g % 2]
                            act.activation(EF[:, s, h, :], bank[:, (g // 2) * 256:(g // 2) * 256 + 256], ACT.Exp,
                                           bias=nmf[:, s, h:h + 1], scale=SCALE_L2F,
                                           accum_out=smf[:, s, h:h + 1]).then_inc(ef_ready, 1)
                for s in range(TILES):
                    for u in range(2):
                        act.wait_ge(pf_psum, i * 4 + 2 * s + u + 1)
                        bank = (SC(s, 0), TR(s))[u]
                        copy(PF[:, s, 4 * u:4 * u + 3:2, :], bank.rearrange("p (h q) -> p h q", h=2)).then_inc(pfa_ready, 1)
                for s in range(TILES):
                    act.wait_ge(mixT_psum, i * 2 + s + 1)
                    copy(AT[:, s, 0:2, :].rearrange("p a b -> p (a b)"), TR(s)[:, 0:256])
                    copy(AT[0:64, s, 2, :], TR(s)[0:64, 256:384]).then_inc(mixT_ready, 1)
                x_transposed(6)
                softmax(2)
                heads_transposed(1)
                x_transposed(7)
                for s in range(TILES):
                    act.wait_ge(rneg_ready, i * 2 + s + 1)
                    act.activation(pr[:, s, :], OU(s)[:, 0:E3], ACT.Exp, bias=rmx[:, s, 1:2],
                                   accum_out=rmx[:, s, 2:3]).then_inc(rexp_ready, 1)
                for u in range(UNITS):
                    m = CHUNKS[u % 3][1]
                    act.wait_ge(up_psum, i * UNITS + u + 1)
                    act.activation(SG[0:m, u % RING, :], SC((u % RING) // 2, u % 2)[0:m, 0:256],
                                   ACT.Silu).then_inc(silu_ready, 1)

        @block.vector
        def _(dve):
            steps = [0]
            pads = iter(range(32))

            def pad():
                k = next(pads)
                return filler[:, k:k + 1]


            def count_prep(ins):
                steps[0] += 1
                ins.then_inc(bsplit, 1)

            def settle_prep():
                dve.wait_ge(bsplit, steps[0])

            dve.wait_ge(ld_masks, 48)
            count_prep(dve.tensor_scalar(m0row[:, :, :], m0w[:, :].bitcast(U8).rearrange("p (b k) -> p b k", b=B), MASKED, None, ALU.mult))
            dve.tensor_scalar(mneg1[:, :, :], m1i[:, :, :], 0.0, MASKED, ALU.is_equal, ALU.mult).then_inc(prep_done, 1)
            dve.tensor_scalar(mneg2[:, :, :], m2i[:, :, :], 0.0, MASKED, ALU.is_equal, ALU.mult).then_inc(prep_done, 1)
            settle_prep()
            dve.tensor_copy(pad()[0:1, :], m0row[0:1, 0, 0:1]).then_inc(mrows, 1)
            dve.wait_ge(ld_small, 48)
            dve.tensor_copy(ident_bf[:, :], ident).then_inc(prep_done, 1)
            dve.wait_ge(memsets, 6)
            for v in Vbd[1:]:
                count_prep(dve.memset(v[0:64, :, :, 16:17], 1.0))
                count_prep(dve.memset(v[64:128, :, :, 17:18], 1.0))

            def weight_stats():
                dve.wait_ge(ld_b, 16)
                for n in range(2):
                    ins = dve.tensor_reduce(wstat[:, n:n + 1], wb_sb[:, 512 * n:512 * n + 512], X_AXIS, ALU.add,
                                            apply_absolute_value=True)
                    count_prep(ins)
                settle_prep()
                dve.tensor_copy(pad(), wstat[:, 0:1]).then_inc(wstat_ready, 1)
                dve.wait_ge(ld_d, 48)
                for n in range(2):
                    ins = dve.tensor_reduce(wstat[:, 2 + n:3 + n], wd_sb[:, 512 * n:512 * n + 512], X_AXIS, ALU.max,
                                            apply_absolute_value=True)
                    count_prep(ins)
                settle_prep()
                dve.tensor_copy(pad(), wstat[:, 2:3]).then_inc(wstat_ready, 1)

            def ternary_weights():
                dve.wait_ge(wred_ready, 1)
                count_prep(dve.tensor_scalar(wmean[:, :], wred[:, 0:2], 1.0 / (D * FF), 1e-5, ALU.mult, ALU.max))
                settle_prep()
                count_prep(dve.reciprocal(wsc[:, 0:2], wmean[:, :]))
                settle_prep()
                for n in range(2):
                    count_prep(dve.tensor_scalar(wtmp[:, 512 * n:512 * n + 512], wb_sb[:, 512 * n:512 * n + 512],
                                                 wsc[:, n:n + 1], ROUND, ALU.mult, ALU.add))
                settle_prep()
                count_prep(dve.tensor_scalar(wtmp2, wtmp, ROUND, -1.0, ALU.subtract, ALU.max))
                settle_prep()
                dve.tensor_scalar(w1q[:, :], wtmp2[:, 0:512], 1.0, None, ALU.min).then_inc(prep_done, 1)
                count_prep(dve.tensor_scalar(w2q[:, :, :].rearrange("p c d -> p (c d)"), wtmp2[:, 512:1024], 1.0, None,
                                             ALU.min))

            def int8_weights():
                dve.wait_ge(wred_ready, 2)
                count_prep(dve.tensor_scalar(wsc[:, 0:2], wred[:, 2:4], 1.0 / QMAX, None, ALU.mult))
                settle_prep()
                count_prep(dve.reciprocal(wsc[:, 2:4], wsc[:, 0:2]))
                settle_prep()
                for n in range(2):
                    count_prep(dve.tensor_scalar(wtmp[:, 512 * n:512 * n + 512], wd_sb[:, 512 * n:512 * n + 512],
                                                 wsc[:, 2 + n:3 + n], ROUND, ALU.mult, ALU.add))
                settle_prep()
                for n in range(2):
                    count_prep(dve.tensor_scalar(wtmp2[:, 512 * n:512 * n + 512], wtmp[:, 512 * n:512 * n + 512], ROUND,
                                                 wsc[:, n:n + 1], ALU.subtract, ALU.mult))
                settle_prep()

            for n, (kind, c, readers) in enumerate(JOBS):
                if "d" not in readers:
                    continue
                if kind == "VO" and c == 0:
                    weight_stats()
                if kind == "K1":
                    ternary_weights()
                    dve.wait_ge(ld_c, 16)
                if kind == "Lfc":
                    int8_weights()
                dve.wait_ge(prep_mm, n + 1)
                bank = ps[:, n % 8, :]
                if kind in ("K0", "V0"):
                    dst, bias = (KTbd, "bk0") if kind == "K0" else (VTbd, "bv0")
                    ins = dve.tensor_scalar(dst[64:128, c, :, CTX:P], bank[64:128, 0:256].rearrange("p (b k) -> p b k", b=B),
                                            part(cols_sb, COLS, bias)[64:128, c:c + 1], None, ALU.add)
                elif kind == "VO":
                    ins = dve.tensor_copy(VO0[:, :, c, :], bank.rearrange("p (b k) -> p b k", b=B))
                elif kind == "b0":
                    v, r1, r2 = bank[:, 0:32], bres[:, 0, :], bres[:, 1, :]
                    hi, mid, lo = (bpart[:, r, :, :].rearrange("p b c -> p (b c)") for r in range(3))
                    count_prep(dve.tensor_copy(hi, v))
                    settle_prep()
                    count_prep(dve.tensor_tensor(r1, v, hi, ALU.subtract))
                    settle_prep()
                    count_prep(dve.tensor_copy(mid, r1))
                    settle_prep()
                    count_prep(dve.tensor_tensor(r2, r1, mid, ALU.subtract))
                    settle_prep()
                    ins = dve.tensor_copy(lo, r2)
                elif kind == "K1":
                    ins = dve.tensor_scalar(KT1, bank[:, 0:256], part(cols_sb, COLS, "bk1"), None, ALU.add)
                elif kind == "K3":
                    for src, dst, tab in ((bank[:, 0:256], KT3a, cosT), (bank[:, 256:512], KT3b, sinT)):
                        count_prep(dve.tensor_tensor(dst.rearrange("p (b k) -> p b k", b=B),
                                                     src.rearrange("p (b k) -> p b k", b=B),
                                                     tab[:, 0:CTX].unsqueeze(1).to_broadcast([P, B, CTX]), ALU.mult))
                    settle_prep()
                    ins = dve.tensor_tensor(KT3, KT3a, KT3b, ALU.add)
                elif kind in ("V1", "V3"):
                    dst = Vbd[1] if kind == "V1" else Vbd[2]
                    v = bank.rearrange("p (b c q d) -> p b c q d", b=B, c=NC8, q=2)
                    bv = part(rows_sb, ROWS, "bv1").rearrange("p (c q d) -> p c q d", q=2, d=8)
                    for q in range(2):
                        rows_q = slice(64 * q, 64 * q + 64)
                        for b in range(B):
                            o = dst[rows_q, b, :, 8 * q:8 * q + 8]
                            if kind == "V1":
                                ins = dve.tensor_tensor(o, v[rows_q, b, :, q, :], bv[rows_q, :, q, :], ALU.add)
                            else:
                                ins = dve.tensor_copy(o, v[rows_q, b, :, q, :])
                            if (q, b) != (1, B - 1):
                                count_prep(ins)
                elif kind == "Lfc":
                    ins = dve.scalar_tensor_tensor(wfc[:, :], bank, LORA_SCALE, wtmp2[:, 0:512], ALU.mult, ALU.add)
                elif kind == "Lpj":
                    ins = dve.scalar_tensor_tensor(wpj[:, :, :].rearrange("p c d -> p (c d)"), bank, LORA_SCALE,
                                                   wtmp2[:, 512:1024], ALU.mult, ALU.add)
                ins.then_inc(prep_dve, 1)
                if kind in ("K1", "K3"):
                    dve.wait_ge(prep_dve, read_by("d", n))
                    dve.tensor_copy(pad(), (KT1 if kind == "K1" else KT3)[:, 0:1]).then_inc(kt_ready, 1)
            settle_prep()
            dve.wait_ge(prep_dve, read_by("d", len(JOBS)))

            with dve.Fori(0, B) as i:
                count = [0]

                def step(ins):
                    count[0] += 1
                    ins.then_inc(dve_seq, 1)
                    return count[0]

                def settle(mark=None):
                    dve.wait_ge(dve_seq, i * DVE_STEPS + (count[0] if mark is None else mark))

                def stats(src, width=None):
                    marks = [step(dve.bn_stats(st[:, s, :], src(s))) for s in range(TILES)]
                    for s in range(TILES):
                        settle(marks[s])
                        step(dve.tensor_copy(pad(), st[:, s, 0:1]))
                        step(dve.bn_aggr(mv[:, s, :], st[:, s, :]))
                    settle()

                def layer_norm(l, src, sink=True):
                    stats(src)
                    dve.tensor_scalar(ve[:, :], mv[:, :, 1], EPS, None, ALU.add).then_inc(var_ready, 1)
                    dve.wait_ge(rstd_ready, i * N_POW + POW[l] + 1)
                    for s in range(TILES):
                        ins = dve.tensor_scalar(XH[:, s, :], src(s), mv[:, s, 0:1], rs[:, s:s + 1], ALU.subtract, ALU.mult)
                        if sink:
                            ins.then_inc(xhat_ready, 1)
                        else:
                            step(ins)

                def softmax(a):
                    marks = []
                    for s in range(TILES):
                        for h in range(2):
                            dve.wait_ge(scores_ready, i * 12 + 4 * a + 2 * s + h + 1)
                            step(dve.tensor_reduce(mx[:, s, 8 * h:8 * h + 8], SC(s, h).rearrange("p (n k) -> p n k", k=CTX),
                                                   X_AXIS, ALU.max))
                        marks.append(count[0])
                    top = mx
                    if CLAMPS[a] is not None:
                        top = mxc
                        for s in range(TILES):
                            settle(marks[s])
                            marks[s] = step(dve.tensor_scalar(mxc[:, s, :], mx[:, s, :], CLAMPS[a], None, ALU.max))
                    for s in range(TILES):
                        settle(marks[s])
                        for h in range(2):
                            sc = SC(s, h).rearrange("p (n k) -> p n k", k=CTX)
                            e = E[:, s, 512 * h:512 * h + 512].rearrange("p (n k) -> p n k", k=CTX)
                            m = top[:, s, 8 * h:8 * h + 8].unsqueeze(2).to_broadcast([P, 8, CTX])
                            if CLAMPS[a] is not None:
                                ins = dve.scalar_tensor_tensor(e, sc, CLAMPS[a], m, ALU.max, ALU.subtract)
                            else:
                                ins = dve.tensor_tensor(e, sc, m, ALU.subtract)
                            ins.then_inc(shifted, 1)

                def head_norms(n, a):
                    marks = []
                    for s in range(TILES):
                        dve.wait_ge(attn_out, i * 6 + 2 * a + s + 1)
                        o = OU(s)[:, 0:144].rearrange("p (c v) -> p c v", v=18)
                        marks.append(step(dve.reciprocal(rc[:, s, :].rearrange("p (c q) -> p c q", q=2), o[:, :, 16:18])))
                    for s in range(TILES):
                        settle(marks[s])
                        o = OU(s)[:, 0:144].rearrange("p (c v) -> p c v", v=18)
                        for q in range(2):
                            r = rc[:, s, :].rearrange("p (c q) -> p c q", q=2)[:, :, q].unsqueeze(2).to_broadcast([P, 8, 8])
                            ins = dve.tensor_tensor(AO[:, s, :].rearrange("p (c q d) -> p c q d", q=2, d=8)[:, :, q, :],
                                                    o[:, :, 8 * q:8 * q + 8], r, ALU.mult)
                            if q == 0:
                                step(ins)
                        ins.then_inc(heads_ready, 1)

                def beats(dst, g, n):
                    shape = list(g.shape)
                    for f in range(n):
                        pick = g[:, :, f:f + 1]
                        step(dve.tensor_tensor(dst[:, :, 0:f + 1, f], pick.to_broadcast([P, shape[1], f + 1]),
                                               g[:, :, 0:f + 1], ALU.is_gt))
                        if f < n - 1:
                            step(dve.tensor_tensor(dst[:, :, f + 1:n, f], pick.to_broadcast([P, shape[1], n - 1 - f]),
                                                   g[:, :, f + 1:n], ALU.is_ge))

                def rms_quant(which, ms_src, top_of, width, src, weight):
                    amax, am, ra, s1, deq = (q_small[:, k, :] for k in range(1, 6))
                    for s in range(TILES):
                        step(dve.tensor_reduce(amax[:, s:s + 1], top_of(s), X_AXIS, ALU.max, apply_absolute_value=True))
                    ms_src()
                    dve.wait_ge(rstd_ready, i * N_POW + POW[which] + 1)
                    settle()
                    step(dve.tensor_tensor(am, amax, rs[:, :], ALU.mult))
                    settle()
                    step(dve.tensor_scalar(am, am, 1e-5, None, ALU.max))
                    settle()
                    step(dve.reciprocal(ra, am))
                    step(dve.tensor_scalar(deq, am, 1.0 / QMAX, wmean[:, weight:weight + 1], ALU.mult, ALU.mult))
                    settle()
                    step(dve.scalar_tensor_tensor(s1, ra, QMAX, rs[:, :], ALU.mult, ALU.mult))
                    settle()
                    for s in range(TILES):
                        step(dve.tensor_scalar(PT[:, s, 0:width], src(s), s1[:, s:s + 1], ROUND, ALU.mult, ALU.add))
                    settle()
                    for s in range(TILES):
                        dve.tensor_scalar(qbf[:, s, 0:width], PT[:, s, 0:width], ROUND, None,
                                          ALU.subtract).then_inc(quant_ready, 1)
                    return deq

                layer_norm(0, lambda s: xall[:, 2 * i + s, :])
                softmax(0)
                for s in range(TILES):
                    for h in range(2):
                        dve.wait_ge(exp_ready, i * 12 + 2 * s + h + 1)
                        step(dve.tensor_reduce(sm[:, s, 8 * h:8 * h + 8],
                                               E[:, s, 512 * h:512 * h + 512].rearrange("p (n k) -> p n k", k=CTX),
                                               X_AXIS, ALU.add))
                    settle()
                    dve.reciprocal(rc[:, s, :], sm[:, s, :]).then_inc(recip_ready, 1)
                dve.wait_ge(xb_ready, i * 4 + 1)
                for s in range(TILES):
                    dve.wait_ge(attn_out, i * 6 + s + 1)
                    step(dve.tensor_tensor(X[:, s, :], OU(s)[:, 0:D], XB[:, s, :], ALU.add))
                settle()
                layer_norm(1, lambda s: X[:, s, :], sink=False)
                settle()

                def ms_of_xhat():
                    t = q_small[:, 6, :]
                    step(dve.tensor_tensor(t, rs[:, :], rs[:, :], ALU.mult))
                    settle()
                    step(dve.tensor_tensor(t, t, mv[:, :, 1], ALU.mult))
                    settle()
                    dve.tensor_scalar(ve[:, :], t, RMS_EPS, None, ALU.add).then_inc(var_ready, 1)

                deq = rms_quant("rms1", ms_of_xhat, lambda s: XH[:, s, :], D, lambda s: XH[:, s, :], 0)
                for s in range(TILES):
                    dve.wait_ge(bit_out, i * 4 + s + 1)
                    dve.scalar_tensor_tensor(E[:, s, 0:512], OU(s), deq[:, s:s + 1], part(rows_sb, ROWS, "b1"),
                                             ALU.mult, ALU.add).then_inc(hid_ready, 1)

                def ms_of_hidden():
                    stats(lambda s: E[:, s, 512:1024])
                    t = q_small[:, 6, :]
                    step(dve.tensor_tensor(t, mv[:, :, 0], mv[:, :, 0], ALU.mult))
                    settle()
                    step(dve.tensor_tensor(t, t, mv[:, :, 1], ALU.add))
                    settle()
                    dve.tensor_scalar(ve[:, :], t, RMS_EPS, None, ALU.add).then_inc(var_ready, 1)

                dve.wait_ge(gelu_ready, i * 2 + 2)
                deq = rms_quant("rms2", ms_of_hidden, lambda s: E[:, s, 512:1024], FF, lambda s: E[:, s, 512:1024], 1)
                dve.wait_ge(xb_ready, i * 4 + 2)
                for s in range(TILES):
                    dve.wait_ge(bit_out, i * 4 + 2 + s + 1)
                    step(dve.scalar_tensor_tensor(X[:, s, :], OU(s)[:, 0:D], deq[:, s:s + 1], XB[:, s, :],
                                                  ALU.mult, ALU.add))
                settle()
                layer_norm(2, lambda s: X[:, s, :])
                softmax(1)
                head_norms(0, 1)
                dve.wait_ge(xb_ready, i * 4 + 3)
                for s in range(TILES):
                    dve.wait_ge(proj_out, i * 4 + s + 1)
                    step(dve.tensor_tensor(X[:, s, :], OU(s)[:, 256:384], XB[:, s, :], ALU.add))
                settle()
                layer_norm(3, lambda s: X[:, s, :])
                dve.wait_ge(xb_ready, i * 4 + 4)
                for s in range(TILES):
                    dve.wait_ge(pj_out, i * 2 + s + 1)
                    step(dve.tensor_tensor(X[:, s, :], OU(s)[:, 0:D], XB[:, s, :], ALU.add))
                settle()
                layer_norm(4, lambda s: X[:, s, :])
                for s in range(TILES):
                    dve.wait_ge(sx_psum, i * 2 + s + 1)
                    step(dve.tensor_reduce(mx[:, s, 0:1], OU(s)[:, 0:CTX], X_AXIS, ALU.max))
                    settle()
                    dve.tensor_scalar(mxc[:, s, 0:1], mx[:, s, 0:1], -SCALE_L2X, None, ALU.mult).then_inc(sx_neg, 1)
                dve.wait_ge(sx_exp, i * 2 + 2)
                step(dve.reciprocal(rc[:, :, 0], sm[:, :, 0]))
                settle()
                for s in range(TILES):
                    dve.wait_ge(sx_out, i * 2 + s + 1)
                    step(dve.scalar_tensor_tensor(X[:, s, :], OU(s)[:, 128:256], rc[:, s, 0:1], X[:, s, :],
                                                  ALU.mult, ALU.add))
                settle()
                layer_norm(5, lambda s: X[:, s, :])
                for c in range(2):
                    dve.wait_ge(qf_psum, i * 4 + 2 + c + 1)
                    dve.tensor_copy(KF[:, 2 * c:2 * c + 2, :].rearrange("p a b -> p (a b)"), SC(1, c)).then_inc(kf_ready, 1)
                dve.wait_ge(gate_ready, i * 2 + 2)
                for s in range(TILES):
                    beats(cmp[:, s * G2:(s + 1) * G2, :, :], XG[:, s, XV:].rearrange("p (g e) -> p g e", e=E2), E2)
                settle()
                step(dve.tensor_reduce(cnt[:, :, :], cmp[:, :, :, :], X_AXIS, ALU.add))
                dve.wait_ge(tanh_ready, i * 2 + 2)
                step(dve.tensor_scalar(th[:, :, :], th[:, :, :], 0.5, 0.5, ALU.mult, ALU.add))
                settle()
                chosen = cnt[:, :, :].rearrange("p (t g) e -> p t g e", t=TILES)
                step(dve.scalar_tensor_tensor(wv[:, :, :, :].rearrange("p t h e -> p t (h e)"),
                                              chosen[:, :, 0:H2, :].rearrange("p t h e -> p t (h e)"), SEL - 0.5,
                                              th[:, :, :], ALU.is_lt, ALU.mult))
                settle()
                for s in range(TILES):
                    pr4 = prod[:, s, :].rearrange("p (e h k) -> p e h k", e=E2, k=DH2)
                    for e in range(E2):
                        step(dve.tensor_tensor(
                            pr4[:, e, :, :], XG[:, s, e * DH2:(e + 1) * DH2].unsqueeze(1).to_broadcast([P, H2, DH2]),
                            wv[:, s, :, e].unsqueeze(2).to_broadcast([P, H2, DH2]), ALU.mult))
                    settle()
                    step(dve.tensor_tensor(prod[:, s, 0:1024], prod[:, s, 0:1024], prod[:, s, 1024:2048], ALU.add))
                    settle()
                    step(dve.tensor_tensor(prod[:, s, 0:512], prod[:, s, 0:512], prod[:, s, 512:1024], ALU.add))
                    settle()
                    dve.tensor_tensor(V[:, s, :], prod[:, s, 0:512], prod[:, s, 2048:2560], ALU.add).then_inc(v_ready, 1)
                for s in range(TILES):
                    for u in range(2):
                        dve.wait_ge(sf_psum, i * 4 + 2 * s + u + 1)
                        banks = ((SC(s, 0), SC(s, 1)), (TR(s), OU(s)))[u]
                        for q in range(2):
                            step(dve.tensor_reduce(mxf[:, s, 4 * u + q:4 * u + q + 3:2],
                                                   banks[q].rearrange("p (h k) -> p h k", h=2), X_AXIS, ALU.max))
                        settle()
                        dve.tensor_scalar(nmf[:, s, 4 * u:4 * u + 4], mxf[:, s, 4 * u:4 * u + 4], -SCALE_L2F, None,
                                          ALU.mult).then_inc(nmf_ready, 1)
                for s in range(TILES):
                    for u in range(2):
                        dve.wait_ge(pf_psum, i * 4 + 2 * s + u + 1)
                        bank = (SC(s, 1), OU(s))[u]
                        dve.tensor_copy(PF[:, s, 4 * u + 1:4 * u + 4:2, :],
                                        bank.rearrange("p (h q) -> p h q", h=2)).then_inc(pfd_ready, 1)
                step(dve.reciprocal(rcf[:, :, :], smf[:, :, :]))
                settle()
                for s in range(TILES):
                    step(dve.scalar_tensor_tensor(mo[:, s, :, :], chosen[:, s, H2:G2, :], SEL - 0.5,
                                                  rcf[:, s, :].unsqueeze(2).to_broadcast([P, H2, E2]), ALU.is_lt, ALU.mult))
                settle()
                for s in range(TILES):
                    dve.wait_ge(pv_out, i * 2 + s + 1)
                    pr4 = prod[:, s, :].rearrange("p (h e k) -> p h e k", h=H2, k=DH2)
                    for h in range(H2):
                        step(dve.tensor_tensor(
                            pr4[:, h, :, :], SC(s, 0)[:, h * DH2:(h + 1) * DH2].unsqueeze(1).to_broadcast([P, E2, DH2]),
                            mo[:, s, h, :].unsqueeze(2).to_broadcast([P, E2, DH2]), ALU.mult))
                    settle()
                    step(dve.tensor_tensor(prod[:, s, 0:1280], prod[:, s, 0:1280], prod[:, s, 1280:2560], ALU.add))
                    settle()
                    step(dve.tensor_tensor(prod[:, s, 0:640], prod[:, s, 0:640], prod[:, s, 640:1280], ALU.add))
                    settle()
                    dve.tensor_tensor(Amix[:, s, :], prod[:, s, 0:320], prod[:, s, 320:640], ALU.add).then_inc(mix_ready, 1)
                for s in range(TILES):
                    dve.wait_ge(swo_out, i * 2 + s + 1)
                    step(dve.tensor_tensor(X[:, s, :], OU(s)[:, 0:D], X[:, s, :], ALU.add))
                settle()
                layer_norm(6, lambda s: X[:, s, :])
                marks = []
                for s in range(TILES):
                    dve.wait_ge(qT_psum, i * 4 + 2 + s + 1)
                    for k, tab in enumerate((cosT, sinT)):
                        step(dve.tensor_tensor(rope[:, s, k, :], OU(s)[:, P * k:P * k + P], tab[:, s * P:(s + 1) * P],
                                               ALU.mult))
                    marks.append(count[0])
                for s in range(TILES):
                    settle(marks[s])
                    dve.tensor_tensor(QT[:, s, :], rope[:, s, 0, :], rope[:, s, 1, :], ALU.add).then_inc(qT_ready, 1)
                softmax(2)
                head_norms(1, 2)
                for s in range(TILES):
                    dve.wait_ge(proj_out, i * 4 + 2 + s + 1)
                    step(dve.tensor_tensor(X[:, s, :], OU(s)[:, 256:384], X[:, s, :], ALU.add))
                settle()
                layer_norm(7, lambda s: X[:, s, :])
                for s in range(TILES):
                    dve.wait_ge(router_psum, i * 2 + s + 1)
                    step(dve.tensor_reduce(rmx[:, s, 0:1], OU(s)[:, 0:E3], X_AXIS, ALU.max))
                    settle()
                    dve.tensor_scalar(rmx[:, s, 1:2], rmx[:, s, 0:1], -1.0, None, ALU.mult).then_inc(rneg_ready, 1)
                dve.wait_ge(rexp_ready, i * 2 + 2)
                step(dve.reciprocal(rmx[:, :, 3], rmx[:, :, 2]))
                settle()
                step(dve.tensor_tensor(pr[:, :, :], pr[:, :, :], rmx[:, :, 3].unsqueeze(2).to_broadcast([P, TILES, E3]),
                                       ALU.mult))
                settle()
                beats(cmp3[:, :, :, :], pr[:, :, :], E3)
                settle()
                step(dve.tensor_reduce(cnt3[:, :, :], cmp3[:, :, :, :], X_AXIS, ALU.add))
                settle()
                step(dve.scalar_tensor_tensor(wte[:, :, :], cnt3[:, :, :], SEL - 0.5, pr[:, :, :], ALU.is_lt, ALU.mult))
                settle()

                def combine(e):
                    for s in range(TILES):
                        dve.wait_ge(down_psum, i * 2 * E3 + 2 * e + s + 1)
                        dst = X[:, s, :] if e < E3 - 1 else oall[:, 2 * i + s, :]
                        ins = dve.scalar_tensor_tensor(dst, (OU(s), TR(s))[e % 2][:, 0:D], wte[:, s, e:e + 1], X[:, s, :],
                                                       ALU.mult, ALU.add)
                        ins.then_inc(comb_done if e < E3 - 1 else out_ready, 1)

                for u in range(UNITS):
                    m = CHUNKS[u % 3][1]
                    dve.wait_ge(silu_ready, i * UNITS + u + 1)
                    dve.tensor_tensor(HT[0:m, u % RING, :], SG[0:m, u % RING, :],
                                      SC((u % RING) // 2, u % 2)[0:m, 256:512], ALU.mult).then_inc(h_ready, 1)
                    if u % 3 == 1 and u > 3:
                        e = u // 3 - 1
                        if e:
                            dve.wait_ge(comb_done, i * 2 * (E3 - 1) + 2 * e)
                        combine(e)
                dve.wait_ge(comb_done, i * 2 * (E3 - 1) + 2 * (E3 - 1))
                combine(E3 - 1)
                assert count[0] == DVE_STEPS, f"DVE_STEPS = {count[0]}"

        @block.tensor
        def _(pe):
            pe.wait_ge(ld_a, 32)
            W = {k: part(wa_sb, WA, k) for k in WA}
            ctxT = W["ctxT"]
            for n, (kind, c, _) in enumerate(JOBS):
                if n >= 8:
                    if read_by("a", n - 8):
                        pe.wait_ge(prep_act, read_by("a", n - 8))
                    if read_by("d", n - 8):
                        pe.wait_ge(prep_dve, read_by("d", n - 8))
                bank = ps[:, n % 8, :]
                if kind in ("K0", "V0"):
                    w = W["WkT" if kind == "K0" else "WvT"]
                    mm = pe.matmul(bank[:, 0:256], w[:, c * P:(c + 1) * P], ctxT, start=True, stop=True)
                elif kind == "M0":
                    pe.wait_ge(prep_act, read_by("a", JOB["K0", c]))
                    pe.wait_ge(prep_dve, read_by("d", JOB["K0", c]))
                    mm = pe.matmul(bank, W["Wq"][:, c * P:(c + 1) * P], KTbd[:, c, :, :].rearrange("p b k -> p (b k)"),
                                   start=True, stop=True)
                elif kind == "b0":
                    pe.wait_ge(ld_small, 48)
                    for b in range(B):
                        for cc in range(NC8):
                            mm = pe.matmul(bank[:, b * NC8 + cc:b * NC8 + cc + 1], KTbd[:, cc, b, :],
                                           part(cols_sb, COLS, "bq0")[:, cc:cc + 1], start=True, stop=True)
                elif kind == "VO":
                    pe.wait_ge(prep_act, read_by("a", JOB["V0", c]))
                    pe.wait_ge(prep_dve, read_by("d", JOB["V0", c]))
                    for b in range(B):
                        mm = pe.matmul(bank[:, b * P:(b + 1) * P], VTbd[:, c, b, :], W["WoT"][:, c * P:(c + 1) * P],
                                       start=True, stop=True)
                elif kind == "b0T":
                    pe.wait_ge(prep_dve, read_by("d", JOB["b0", 0]))
                    pe.wait_ge(prep_done, 3)
                    mm = pe.transpose(bank.bitcast(BF16)[0:96, 0:P],
                                      bpart[:, :, :, :].rearrange("p r b c -> p (r b c)"), ident_bf[:, :])
                elif kind == "K1":
                    pe.wait_ge(ld_c, 16)
                    mm = pe.matmul(bank[:, 0:256], wcol("Wk1"), ctxT, start=True, stop=True)
                elif kind == "K3":
                    pe.matmul(bank[:, 0:256], wcol("Wk3"), ctxT, start=True, stop=True)
                    mm = pe.matmul(bank[:, 256:512], wcol("Wk3s"), ctxT, start=True, stop=True)
                elif kind in ("V1", "V3"):
                    for b in range(B):
                        mm = pe.matmul(bank[:, b * P:(b + 1) * P], wcol("ctxT2")[:, b * P:(b + 1) * P],
                                       wcol("Wv1" if kind == "V1" else "Wv3"), start=True, stop=True)
                elif kind == "Lfc":
                    pe.wait_ge(ld_d, 48)
                    mm = pe.matmul(bank, lora_sb[:, 0:128], lora_sb[:, 128:640], start=True, stop=True)
                else:
                    for cc in range(FF // P):
                        mm = pe.matmul(bank[:, cc * P:(cc + 1) * P], loraB_sb[:, cc * P:(cc + 1) * P],
                                       loraB_sb[:, 512:640], start=True, stop=True)
                mm.then_inc(prep_mm, 1)
            pe.wait_ge(prep_act, read_by("a", len(JOBS)))
            pe.wait_ge(prep_dve, read_by("d", len(JOBS)))
            pe.wait_ge(prep_done, 4)
            pe.wait_ge(memsets, 6)
            pe.wait_ge(ld_e, 80)
            pe.wait_ge(bias_rows, 16 * (B + 3))

            with pe.Fori(0, B) as i:
                def x_transposed(l):
                    k = 2 * LN_OF_XT.index(l)
                    for s in range(TILES):
                        pe.wait_ge(xhat_ready, i * N_XT + k + s + 1)
                        pe.transpose(TR(s)[:, 0:P], XH[:, s, :], ident).then_inc(xT_psum, 1)

                def xt_wait(l, s):
                    pe.wait_ge(xT_ready, i * N_XT + 2 * LN_OF_XT.index(l) + s + 1)

                def xt(s):
                    return XT[:, s * P:(s + 1) * P]

                def probs_transposed(a):
                    for s in range(TILES):
                        for h in range(2):
                            if a == 0:
                                pe.wait_ge(norm_ready, i * 4 + 2 * s + h + 1)
                            else:
                                pe.wait_ge(exp_ready, i * 12 + 4 * a + 2 * s + h + 1)
                            for c in range(4):
                                mm = pe.transpose(SC(s, h)[:, c * P:(c + 1) * P],
                                                  E[:, s, 512 * h + c * P:512 * h + (c + 1) * P], ident)
                            mm.then_inc(pT_psum, 1)

                def small_heads(n, a):
                    for s in range(TILES):
                        pe.wait_ge(pT_ready, i * 12 + 4 * a + 2 * s + 2)
                        for c in range(NC8):
                            mm = pe.matmul(OU(s)[:, 18 * c:18 * c + 18], PT[:, s, c * P:(c + 1) * P], Vbd[a][:, i, c, :],
                                           start=True, stop=True)
                        mm.then_inc(attn_out, 1)
                    for s in range(TILES):
                        pe.wait_ge(heads_ready, i * 4 + 2 * n + s + 1)
                        pe.transpose(TR(s)[:, 0:P], AO[:, s, :], ident).then_inc(headsT_psum, 1)
                    for s in range(TILES):
                        pe.wait_ge(headsT_ready, i * 4 + 2 * n + s + 1)
                        pe.matmul(OU(s)[:, 256:384], AOT[:, s, :], wcol(("Wo1", "Wo3")[n]), start=True,
                                  stop=True).then_inc(proj_out, 1)

                x_transposed(0)
                for s in range(TILES):
                    xt_wait(0, s)
                    for h in range(2):
                        pe.matmul(SC(s, h), xt(s), M0[:, i, 4 * h:4 * h + 4, :].rearrange("p c k -> p (c k)"),
                                  start=True, stop=False)
                        pe.matmul(SC(s, h), ones_bf[:, :], bias0[:, i, 512 * h:512 * h + 512], start=False,
                                  stop=True).then_inc(scores_ready, 1)
                probs_transposed(0)
                for s in range(TILES):
                    pe.wait_ge(pT_ready, i * 12 + 2 * s + 2)
                    for c in range(NC8):
                        mm = pe.matmul(OU(s)[:, 0:D], PT[:, s, c * P:(c + 1) * P], VO0[:, i, c, :], start=(c == 0),
                                       stop=(c == NC8 - 1))
                    mm.then_inc(attn_out, 1)
                for s in range(TILES):
                    pe.wait_ge(quant_ready, i * 4 + s + 1)
                    pe.transpose(TR(s).bitcast(BF16)[:, 0:P], qbf[:, s, 0:P], ident_bf[:, :]).then_inc(quantT_psum, 1)
                for s in range(TILES):
                    pe.wait_ge(quantT_ready, i * 4 + s + 1)
                    pe.matmul(OU(s), qTbf[:, s, 0:P], w1q[:, :], start=True, stop=True).then_inc(bit_out, 1)
                for s in range(TILES):
                    pe.wait_ge(quant_ready, i * 4 + 2 + s + 1)
                    for c in range(FF // P):
                        mm = pe.transpose(TR(s).bitcast(BF16)[:, c * P:(c + 1) * P], qbf[:, s, c * P:(c + 1) * P],
                                          ident_bf[:, :])
                    mm.then_inc(quantT_psum, 1)
                for s in range(TILES):
                    pe.wait_ge(quantT_ready, i * 4 + 2 + s + 1)
                    for c in range(FF // P):
                        mm = pe.matmul(OU(s)[:, 0:D], qTbf[:, s, c * P:(c + 1) * P], w2q[:, c, :], start=(c == 0),
                                       stop=(c == FF // P - 1))
                    mm.then_inc(bit_out, 1)
                x_transposed(2)
                for s in range(TILES):
                    xt_wait(2, s)
                    pe.matmul(OU(s)[:, 0:P], wcol("Wq1"), xt(s), start=True, stop=True).then_inc(qT_psum, 1)
                for s in range(TILES):
                    pe.wait_ge(qT_ready, i * 4 + s + 1)
                    if s == 0:
                        pe.wait_ge(kbd_ready, i * 2 + 1)
                    for h in range(2):
                        pe.matmul(SC(s, h), QT[:, s, :], Kbd[1][:, 8 * h:8 * h + 8, :].rearrange("p n k -> p (n k)"),
                                  start=True, stop=False)
                        pe.matmul(SC(s, h), ident_bf[:, :], mneg1[:, s, :].unsqueeze(1).to_broadcast([P, 8, CTX]),
                                  start=False, stop=True).then_inc(scores_ready, 1)
                probs_transposed(1)
                small_heads(0, 1)
                x_transposed(3)
                xt_wait(3, 1)
                for c in range(FF // P):
                    pe.matmul(SC(c // 2, c % 2)[:, 0:256], wfc[:, c * P:(c + 1) * P], XT[:, :],
                              start=True, stop=True).then_inc(fc_psum, 1)
                for s in range(TILES):
                    pe.wait_ge(fc_gelu, i * 4 + 4)
                    for c in range(FF // P):
                        mm = pe.matmul(OU(s)[:, 0:D], GT[:, c, s * P:(s + 1) * P], wpj[:, c, :], start=(c == 0),
                                       stop=(c == FF // P - 1))
                    mm.then_inc(pj_out, 1)
                x_transposed(4)
                for s in range(TILES):
                    xt_wait(4, s)
                    pe.matmul(OU(s)[:, 0:CTX], xt(s), ctxT_sb[:, i, :],
                              start=True, stop=False)
                    pe.matmul(OU(s)[:, 0:CTX], ones_bf[0:1, :], mneg2[:, i, :], start=False, stop=True).then_inc(sx_psum, 1)
                for s in range(TILES):
                    pe.wait_ge(sx_exp, i * 2 + s + 1)
                    pe.matmul(TR(s)[0:CTX, 0:P], E[:, s, 0:CTX], ident, start=True, stop=True).then_inc(sxT_psum, 1)
                for s in range(TILES):
                    if s == 0:
                        pe.wait_ge(ctxb_ready, i + 1)
                    pe.wait_ge(sxT_ready, i * 2 + s + 1)
                    pe.matmul(OU(s)[:, 128:256], PT[0:CTX, s, 0:P], ctxb[:, :], start=True,
                              stop=True).then_inc(sx_out, 1)
                x_transposed(5)
                for s in range(TILES):
                    xt_wait(5, s)
                    pe.matmul(OU(s)[:, 0:400], xt(s), part(we_sb, WE, "VSD"), start=True, stop=True).then_inc(gate_psum, 1)
                for w, name in enumerate(("Wq", "Wk")):
                    for c in range(H2 // 2):
                        mm = pe.matmul(SC(w, c // 2)[:, (c % 2) * 256:(c % 2) * 256 + 256],
                                       part(we_sb, WE, name)[:, c * P:(c + 1) * P], XT[:, :], start=True, stop=True)
                        if c % 2:
                            mm.then_inc(qf_psum, 1)
                pe.wait_ge(qf_ready, i * 2 + 2)
                pe.wait_ge(kf_ready, i * 2 + 2)
                pe.wait_ge(gate_ready, i * 2 + 2)
                for s in range(TILES):
                    for u in range(2):
                        for g in range(4):
                            h = 4 * u + g
                            r = slice(64 * (h % 2), 64 * (h % 2) + 64)
                            bank = ((SC(s, 0), SC(s, 1)), (TR(s), OU(s)))[u][g % 2]
                            mm = pe.matmul(bank[:, (g // 2) * 256:(g // 2) * 256 + 256],
                                           QF[r, h // 2, s * P:(s + 1) * P], KF[r, h // 2, :], start=True, stop=True)
                        mm.then_inc(sf_psum, 1)
                for s in range(TILES):
                    for u in range(2):
                        pe.wait_ge(ef_ready, i * 16 + 8 * s + 4 * u + 4)
                        for g in range(4):
                            h = 4 * u + g
                            bank = ((SC(s, 0), SC(s, 1)), (TR(s), OU(s)))[u][g % 2]
                            for j in range(2):
                                mm = pe.transpose(bank[:, (g // 2) * 256 + j * P:(g // 2) * 256 + (j + 1) * P],
                                                  EF[:, s, h, j * P:(j + 1) * P], ident)
                        mm.then_inc(pf_psum, 1)
                pe.wait_ge(v_ready, i * 2 + 2)
                for s in range(TILES):
                    pe.wait_ge(pfa_ready, i * 4 + 2 * s + 2)
                    pe.wait_ge(pfd_ready, i * 4 + 2 * s + 2)
                    for h in range(H2):
                        for j in range(2):
                            mm = pe.matmul(SC(s, 0)[:, h * DH2:(h + 1) * DH2], PF[:, s, h, j * P:(j + 1) * P],
                                           V[:, j, h * DH2:(h + 1) * DH2], start=(j == 0), stop=(j == 1))
                    mm.then_inc(pv_out, 1)
                for s in range(TILES):
                    pe.wait_ge(mix_ready, i * 2 + s + 1)
                    pe.transpose(TR(s)[:, 0:128], Amix[:, s, 0:128], ident)
                    pe.transpose(TR(s)[:, 128:256], Amix[:, s, 128:256], ident)
                    pe.transpose(TR(s)[0:64, 256:384], Amix[:, s, 256:320], ident).then_inc(mixT_psum, 1)
                for s in range(TILES):
                    pe.wait_ge(mixT_ready, i * 2 + s + 1)
                    pe.matmul(OU(s)[:, 0:D], AT[:, s, 0, :], wo2_sb[:, 0, :], start=True, stop=False)
                    pe.matmul(OU(s)[:, 0:D], AT[:, s, 1, :], wo2_sb[:, 1, :], start=False, stop=False)
                    pe.matmul(OU(s)[:, 0:D], AT[0:64, s, 2, :], wo2b_sb[:, :], start=False, stop=True).then_inc(swo_out, 1)
                x_transposed(6)
                for s in range(TILES):
                    xt_wait(6, s)
                    pe.matmul(OU(s)[:, 0:P], wcol("Wq3"), xt(s), start=True, stop=True)
                    pe.matmul(OU(s)[:, P:2 * P], wcol("Wq3s"), xt(s), start=True, stop=True).then_inc(qT_psum, 1)
                for s in range(TILES):
                    pe.wait_ge(qT_ready, i * 4 + 2 + s + 1)
                    if s == 0:
                        pe.wait_ge(kbd_ready, i * 2 + 2)
                    for h in range(2):
                        pe.matmul(SC(s, h), QT[:, s, :], Kbd[2][:, 8 * h:8 * h + 8, :].rearrange("p n k -> p (n k)"),
                                  start=True, stop=True).then_inc(scores_ready, 1)
                probs_transposed(2)
                small_heads(1, 2)
                x_transposed(7)
                pe.wait_ge(ld_moe, 64)
                for s in range(TILES):
                    xt_wait(7, s)
                    pe.matmul(OU(s)[:, 0:E3], xt(s), part(we_sb, WE, "router"), start=True, stop=True).then_inc(router_psum, 1)

                def up(u):
                    e, c = divmod(u, 3)
                    i0, m = CHUNKS[c]
                    if u >= RING:
                        pe.wait_ge(h_ready, i * UNITS + u - RING + 1)
                    bank = SC((u % RING) // 2, u % 2)
                    for w in range(2):
                        mm = pe.matmul(bank[0:m, 256 * w:256 * w + 256], gu_sb[:, w, e * I3 + i0:e * I3 + i0 + m], XT[:, :],
                                       start=True, stop=True)
                    mm.then_inc(up_psum, 1)

                def down_product(u):
                    e, c = divmod(u, 3)
                    m = CHUNKS[c][1]
                    if u == 0:
                        pe.wait_ge(rexp_ready, i * 2 + 2)
                    if c == 0 and e >= 2:
                        pe.wait_ge(comb_done, i * 2 * (E3 - 1) + 2 * (e - 1))
                    pe.wait_ge(h_ready, i * UNITS + u + 1)
                    for s in range(TILES):
                        mm = pe.matmul((OU(s), TR(s))[e % 2][:, 0:D], HT[0:m, u % RING, s * P:(s + 1) * P],
                                       dn_sb[0:m, e, c, :], start=(c == 0), stop=(c == 2))
                        if c == 2:
                            mm.then_inc(down_psum, 1)

                for u in range(UNITS + LAG):
                    if u < UNITS:
                        up(u)
                    if u >= LAG:
                        down_product(u - LAG)



def rope_tables():
    inv = (1.0 / np.float32(10000.0) ** (np.arange(0, 8, 2, dtype=np.float32) / np.float32(8))).astype(np.float32)
    freqs = np.outer(np.arange(S, dtype=np.float32), inv).astype(np.float32)
    d = np.arange(P) % 8
    cos = np.cos(freqs).T[d // 2]
    sin = np.sin(freqs).T[d // 2] * np.where(d % 2 == 0, -1.0, 1.0)[:, None]
    return cos.astype(np.float32), sin.astype(np.float32)


def chunked(a):
    return a.reshape(-1, P, a.shape[1]).transpose(1, 0, 2).reshape(P, -1)


def kernel(**inputs):
    import concourse.bacc as bacc
    from concourse.bass_utils import run_bass_kernel_spmd

    a = {k: np.asarray(v) for k, v in inputs.items()}
    cat = lambda *parts: np.ascontiguousarray(np.concatenate(parts, axis=1))
    col = lambda v: v.reshape(-1, P).T
    ctx = a["ctx_1024"]
    ctxT = ctx.reshape(B * CTX, D).T
    ctxT2 = np.stack([ctx, ctx], axis=1).reshape(2 * B * CTX, D).T
    swap = np.arange(P) ^ 1
    cos, sin = rope_tables()
    block = (np.arange(P)[:, None] // 8 == np.arange(16)[None, :]).astype(np.float32)
    w3q, w3k = a["L3_xattn_Wq"], a["L3_xattn_Wk"]
    wv2 = a["L2_ffn_Wv"].transpose(1, 0, 2).reshape(D, XV)
    arrays = {
        "x": a["x"].reshape(B * S, D),
        "wa": cat(ctxT, a["L0_xattn_Wk"].T, a["L0_xattn_Wv"].T, chunked(a["L0_xattn_Wq"]), chunked(a["L0_xattn_Wo"].T)),
        "cols": cat(col(a["L0_xattn_bq"]), col(a["L0_xattn_bk"]), col(a["L0_xattn_bv"]), col(a["L1_xattn_bq"]),
                    col(a["L1_xattn_bk"]), col(a["L1_ffn_b_fc"])),
        "rows": cat(*(a[n][None, :] for n in ("L0_xattn_bo", "L0_ffn_b2", "L1_xattn_bo", "L1_ffn_b_proj", "L0_ffn_b1",
                                              "L1_xattn_bv"))),
        "wb": cat(a["L0_ffn_w1"].T, chunked(a["L0_ffn_w2"].T)),
        "wc": cat(a["L1_xattn_Wq"].T, a["L1_xattn_Wk"].T, a["L1_xattn_Wv"].T, a["L1_xattn_Wo"].T, w3q.T, w3q[swap].T,
                  w3k.T, w3k[swap].T, a["L3_xattn_Wv"].T, a["L3_xattn_Wo"].T, ctxT2),
        "wd": cat(a["L1_ffn_W_fc"].T, chunked(a["L1_ffn_W_proj"].T)),
        "lora": cat(a["L1_ffn_A_fc"], a["L1_ffn_B_fc"].T, a["L1_ffn_A_proj"], a["L1_ffn_B_proj"].T),
        "we": cat(a["L2_ffn_Wq"], a["L2_ffn_Wk"], wv2, a["L2_ffn_Ws"], a["L2_ffn_Wd"], a["L3_ffn_router_w"].T),
        "wo2": a["L2_ffn_Wo"].reshape(XV, D),
        "ctxn": ctx,
        "gateup": np.ascontiguousarray(np.stack([a["L3_ffn_gate_w"].transpose(2, 0, 1).reshape(D, -1),
                                                 a["L3_ffn_up_w"].transpose(2, 0, 1).reshape(D, -1)], axis=1)),
        "down": np.ascontiguousarray(a["L3_ffn_down_w"].transpose(0, 2, 1)),
        "const": cat(np.eye(P, dtype=np.float32), cos, sin, block),
        "mask0": a["mask_BxS2_bk0"].reshape(1, B * CTX).view(np.int32),
        "mask1": a["mask_1x1xSxS2_ik0"].reshape(S, CTX),
        "mask2": a["mask_BxS2_ik1"].reshape(1, B, CTX),
    }
    arrays = {f"in_{k}": np.ascontiguousarray(v) for k, v in arrays.items()}
    nc = bacc.Bacc("TRN2", target_bir_lowering=False, num_devices=1)
    args = [nc.dram_tensor(k, v.shape, mybir.dt.from_np(v.dtype), kind="ExternalInput").ap() for k, v in arrays.items()]
    args.append(nc.dram_tensor("out_0_dram", (B * S, D), F32, kind="ExternalOutput").ap())
    build(nc, *args)
    r = run_bass_kernel_spmd(nc, [arrays], core_ids=[0])
    return r.results[0]["out_0_dram"].reshape(B, S, D)
```

```python
from contextlib import ExitStack

import numpy as np

import concourse.bass as bass
from concourse import mybir

F32 = mybir.dt.float32
BF16 = mybir.dt.bfloat16
I32 = mybir.dt.int32
U8 = mybir.dt.uint8
ALU = mybir.AluOpType
ACT = mybir.ActivationFunctionType
X_AXIS = mybir.AxisListType.X
R_ADD = bass.bass_isa.ReduceOp.add
R_MAX = bass.bass_isa.ReduceOp.max

P = 128
D = 128
B, S, CTX = 4, 256, 64
TILES = S // P
NC8 = 8
SIDE = 16
FF = 512
H2, DH2, E2X, SEL = 8, 64, 5, 2
G2 = 2 * H2
XV = E2X * DH2
E3, I3 = 8, 352
CHUNKS = [(0, 128), (128, 128), (256, 96)]
UNITS = E3 * len(CHUNKS)
UP_BANKS = 3
RING = 4
LAG = 2
HEAD_UNITS = 8
HEAD_BANKS = 3
EPS = 1e-5
RMS_EPS = 1e-5
QMAX = 127.0
ROUND = 12582912.0
MASKED = -1e30
SCALE_L0 = 0.125
SCALE_L1 = float(1.0 / np.sqrt(np.float32(8)))
SCALE_L2X = float(1.0 / np.sqrt(128.0))
SCALE_L2F = 0.125
SCALES = [SCALE_L0, SCALE_L1, SCALE_L1]
CLAMPS = [-1e9 / SCALE_L0, -1e9 / SCALE_L1, None]
LORA_SCALE = 2.0

WA = {"ctxT": (0, 256), "WkT": (256, 1024), "WvT": (1280, 1024), "Wq": (2304, 1024), "WoT": (3328, 1024)}
COLS = {"bq0": (0, 8), "bk0": (8, 8), "bv0": (16, 8), "bq1": (24, 1), "bk1": (25, 1), "bfc": (26, 4)}
ROWS = {"bo0": (0, 128), "b2": (128, 128), "bo1": (256, 128), "bpj": (384, 128), "b1": (512, 512), "bv1": (1024, 128)}
WC = {n: (128 * k, 128) for k, n in enumerate(
    ["Wq1", "Wk1", "Wv1", "Wo1", "Wq3", "Wq3s", "Wk3", "Wk3s", "Wv3", "Wo3"])}
LORA = {"Afc": (0, 128), "BfcT": (128, 512), "Apj": (640, 512), "BpjT": (1152, 128)}
WE = {"Wq": (0, 512), "Wk": (512, 512), "VSD": (1024, 400), "router": (1424, 8)}
CONST = {"ident": (0, 128), "cos": (128, 256), "sin": (384, 256), "block": (640, 16)}

OPENING = {e: "P" * 10 for e in ("pool", "act", "dve", "pe")}
WEAVE = {
    "pool": "BBBFFBBBBBBBBBBFFFBFFBFFBBBBBBBBBBBBBBBBBBBBFBBBBBB",
    "act": "BBBBBBBFBBBBBBBBBBFBFBBBBFFBBBBBFFBBBBFBFBBFFBBBFFFFBBBBBBBBFBBFBBFFBBFBFBFBBFBBFBFBFBBBFF"
            "BBBBBFBFBBBBBBFBFBBFFFFBBB",
    "dve": "BBBFBBFBBBBBBBBBBBBFFFFFFBBFFBBFBBBBBFBFBBFBFBFFBBBBFFBFBFBBFBFBBBFFFFBBBBBBBBFBBFBBFBBFBF"
            "BBBBFBFBBBFBFBB",
    "pe": "FBBBBBBBBFBBBBBFBFBBFBBBBBBBBBBBFFBFBBFFBFBFBBBBBFFFFBBBBBBBFFBBFBBFBBBFFBFFBFBBFBFBBFBBBF"
            "BBBFBBBBBBFBBBFBFBBBBFBBFBBBBBBBBBBBFBFFBBFBBFBBBBBFB",
}

F_POW = {0: 0, 1: 1, "rms1": 2, "rms2": 3, 2: 4, 3: 5}
B_POW = {4: 0, 5: 1, 6: 2, 7: 3}
F_LN = [0, 2, 3]
B_LN = [4, 5, 6, 7]
F_STEPS = 75
B_STEPS = 110


def build(nc, x, wa, cols, rows, wb, wc, wd, lora, we, wo2, ctxn, gateup, down, const, mask0, mask1, mask2, out):
    ctx = ExitStack()
    with ctx:
        def sb(name, shape, dt=F32):
            return ctx.enter_context(nc.sbuf_tensor(name, shape, dt))

        def sem(name):
            return ctx.enter_context(nc.semaphore(name))

        wc_sb = sb("wc_sb", [P, 1280])
        we_sb = sb("we_sb", [P, 1432])
        cols_sb = sb("cols_sb", [P, 30])
        rows_sb = sb("rows_sb", [P, 1152])
        const_sb = sb("const_sb", [P, 656])
        wo2_sb = sb("wo2_sb", [P, 2, D])
        wo2b_sb = sb("wo2b_sb", [XV - 2 * P, D])
        ctxn_sb = sb("ctxn_sb", [CTX, B, D])
        ctxb = sb("ctxb", [CTX, D])
        ctxT_sb = sb("ctxT_sb", [P, B, CTX])
        gu_sb = sb("gu_sb", [P, 2, E3 * I3])
        dn_sb = sb("dn_sb", [P, E3, len(CHUNKS), D])
        ident_bf = sb("ident_bf", [P, P], BF16)
        ones_bf = sb("ones_bf", [4, P], BF16)
        w1q = sb("w1q", [P, FF], BF16)
        w2q = sb("w2q", [P, FF // P, D], BF16)
        wfc = sb("wfc", [P, FF])
        wpj = sb("wpj", [P, FF // P, D])
        wmean = sb("wmean", [P, 2])
        mhalf = sb("mhalf", [P, TILES])
        M0 = sb("M0", [P, B, NC8, P])
        VO0 = sb("VO0", [P, B, NC8, D])
        bias0 = sb("bias0", [4, B, NC8 * P], BF16)
        KT = [None, sb("KT1", [P, B, CTX]), sb("KT3", [P, B, CTX])]
        Kbd = [None, sb("Kbd1", [P, 16, CTX]), sb("Kbd3", [P, 16, CTX])]
        Vbd = [None, sb("Vbd1", [P, B, NC8, 18]), sb("Vbd3", [P, B, NC8, 18])]
        mneg1 = sb("mneg1", [P, TILES, CTX], BF16)
        mneg2 = sb("mneg2", [1, B, CTX], BF16)
        xall = sb("xall", [P, B * TILES, D])
        hand = sb("hand", [P, TILES, D])
        XB = sb("XB", [P, TILES, D])
        work = sb("work", [P, 2048 + 2560])
        E1 = work[:, 0:2048].rearrange("p (t c) -> p t c", t=TILES)
        prod = work[:, 2048:]
        EF = sb("EF", [P, TILES, H2, S])
        EF_flat = EF[:, :, :, :].rearrange("p t h q -> p (t h q)")
        E2 = EF_flat[:, 0:2048].rearrange("p (t c) -> p t c", t=TILES)
        q_small = sb("q_small", [P, 8, TILES])
        qbf = sb("qbf", [P, TILES, FF], BF16)
        qTbf = sb("qTbf", [P, TILES, FF], BF16)
        GT = sb("GT", [P, FF // P, TILES * P])
        QF = sb("QF", [P, H2 // 2, S])
        KFbd = sb("KFbd", [P, H2 // 2, 2, S])
        XG = sb("XG", [P, TILES, XV + E2X * G2])
        cmp = prod[:, 0:TILES * G2 * E2X * E2X].rearrange("p (g e f) -> p g e f", e=E2X, f=E2X)
        cnt = sb("cnt", [P, TILES * G2, E2X])
        th = sb("th", [P, TILES, E2X * H2])
        wv = sb("wv", [P, TILES, H2, E2X])
        mo = sb("mo", [P, TILES, H2, E2X])
        V = sb("V", [P, TILES, FF])
        mxf = sb("mxf", [P, TILES, H2])
        nmf = sb("nmf", [P, TILES, H2])
        smf = sb("smf", [P, TILES, H2])
        rcf = sb("rcf", [P, TILES, H2])
        Amix = XG[:, :, 0:XV]
        AT = QF[:, :, :].rearrange("p a b -> p (a b)")[:, 0:TILES * 3 * P].rearrange("p (t c q) -> p t c q", t=TILES, c=3)
        TH = prod[:, 0:1024].rearrange("p (r q) -> p r q", q=S)
        UC = prod[:, 1024:2048].rearrange("p (r q) -> p r q", q=S)
        T1 = V[:, :, :].rearrange("p t (r q) -> p (t r) q", q=S)
        HT = sb("HT", [P, RING, S])
        DW = EF_flat[:, 0:2048].rearrange("p (t e q) -> p t e q", t=TILES, e=E3)
        XTw = EF_flat[:, 2048:4096].rearrange("p (e q) -> p e q", e=E3)
        rmx = sb("rmx", [P, TILES, 4])
        pr = sb("pr", [P, TILES, E3])
        cmp3 = prod[:, 2048:2048 + TILES * E3 * E3].rearrange("p (t e f) -> p t e f", t=TILES, e=E3)
        cnt3 = sb("cnt3", [P, TILES, E3])
        wte = sb("wte", [P, TILES, E3])
        filler = sb("filler", [P, 32])
        KTbd = EF_flat.rearrange("p (c b k) -> p c b k", c=NC8, b=B)
        VTbd = work[:, 0:4096].rearrange("p (c b k) -> p c b k", c=NC8, b=B)
        wa_sb = gu_sb[:, :, :].rearrange("p a b -> p (a b)")[:, 0:4352]
        dn_flat = dn_sb[:, :, :, :].rearrange("p a b c -> p (a b c)")
        wb_sb = dn_flat[:, 0:1024]
        wd_sb = dn_flat[:, 1024:2048]
        wtmp = dn_flat[:, 2048:3072]
        wtmp2 = GT[:, :, :].rearrange("p a b -> p (a b)")
        lora_sb = HT[0:16, :, :].rearrange("p a b -> p (a b)")
        loraB_sb = V[0:16, :, :].rearrange("p a b -> p (a b)")
        KT1 = KT[1][:, :, :].rearrange("p b k -> p (b k)")
        KT3 = KT[2][:, :, :].rearrange("p b k -> p (b k)")
        KT3a = EF_flat[:, 0:256]
        KT3b = EF_flat[:, 256:512]
        wstat = sb("wstat", [P, 4])
        wred = sb("wred", [P, 4])
        wsc = sb("wsc", [P, 4])
        ps = ctx.enter_context(nc.psum_tensor("ps", [P, 8, 512], F32))

        class Half:

            def __init__(self, name, bank0, power, norms):
                self.power, self.norms = power, norms
                self.n_pow, self.n_xt = len(power), TILES * len(norms)
                self.banks = [ps[:, bank0 + k, :] for k in range(4)]
                self.XH = sb(f"{name}_XH", [P, TILES, D])
                self.XT = sb(f"{name}_XT", [P, TILES * P])
                self.X = sb(f"{name}_X", [P, TILES, D])
                self.st = sb(f"{name}_st", [P, TILES, 6])
                self.mv = sb(f"{name}_mv", [P, TILES, 2])
                self.pad = sb(f"{name}_pad", [P, 1])
                self.ve = sb(f"{name}_ve", [P, TILES])
                self.rs = sb(f"{name}_rs", [P, TILES])
                self.mx = sb(f"{name}_mx", [P, TILES, 16])
                self.mxc = sb(f"{name}_mxc", [P, TILES, 16])
                self.sm = sb(f"{name}_sm", [P, TILES, 16])
                self.rc = sb(f"{name}_rc", [P, TILES, 16])
                self.QT = sb(f"{name}_QT", [P, TILES * P])
                self.AO = sb(f"{name}_AO", [P, TILES, D])
                self.AOT = sb(f"{name}_AOT", [P, TILES, P])
                self.dve_seq = sem(f"{name}_dve_seq")
                self.var_ready = sem(f"{name}_var_ready")
                self.rstd_ready = sem(f"{name}_rstd_ready")
                self.xhat_ready = sem(f"{name}_xhat_ready")
                self.xT_psum = sem(f"{name}_xT_psum")
                self.xT_ready = sem(f"{name}_xT_ready")
                self.scores_ready = sem(f"{name}_scores_ready")
                self.shifted = sem(f"{name}_shifted")
                self.exp_ready = sem(f"{name}_exp_ready")
                self.pT_psum = sem(f"{name}_pT_psum")
                self.pT_ready = sem(f"{name}_pT_ready")
                self.attn_out = sem(f"{name}_attn_out")
                self.qT_psum = sem(f"{name}_qT_psum")
                self.qT_ready = sem(f"{name}_qT_ready")
                self.heads_ready = sem(f"{name}_heads_ready")
                self.headsT_psum = sem(f"{name}_headsT_psum")
                self.headsT_ready = sem(f"{name}_headsT_ready")
                self.proj_out = sem(f"{name}_proj_out")

            def A(self, s):
                return self.banks[2 * s]

            def Bk(self, s):
                return self.banks[2 * s + 1]

            def bank(self, s, h):
                return self.banks[2 * s + h]

        FR = Half("front", 0, F_POW, F_LN)
        BA = Half("back", 4, B_POW, B_LN)
        spare = BA.AO[:, :, :].rearrange("p t d -> p (t d)")
        bpart = spare[:, 0:48].bitcast(BF16).rearrange("p (r b c) -> p r b c", r=3, b=B)
        bres = spare[:, 64:128].rearrange("p (r k) -> p r k", r=2)
        bpT = spare[0:96, 128:192].bitcast(BF16)
        m0w = spare[0:1, 192:256].bitcast(I32)
        m0row = BA.QT[0:1, 0:128].bitcast(BF16).rearrange("p (b k) -> p b k", b=B)
        m1i = BA.XH[:, 0, :].bitcast(I32).rearrange("p (t k) -> p t k", t=TILES)
        m2i = BA.XT[0:1, 0:B * CTX].bitcast(I32).rearrange("p (b k) -> p b k", b=B)
        ctxT2 = QF[:, :, :].rearrange("p a b -> p (a b)")[:, 0:512]

        def part(t, table, name):
            a, n = table[name]
            return t[:, a:a + n]

        def wcol(name):
            return part(wc_sb, WC, name)

        ident = part(const_sb, CONST, "ident")
        cosT = part(const_sb, CONST, "cos")
        sinT = part(const_sb, CONST, "sin")
        blockm = part(const_sb, CONST, "block")

        def head_bank(k):
            return BA.banks[k % HEAD_BANKS]

        def heads_out(s):
            return BA.banks[3] if s == 0 else BA.banks[0]

        def mix_bank(s):
            return BA.banks[1 + s]

        def up_bank(u):
            return BA.banks[1 + u % UP_BANKS]

        ld_a = sem("ld_a")
        ld_small = sem("ld_small")
        ld_masks = sem("ld_masks")
        ld_x = sem("ld_x")
        ld_b = sem("ld_b")
        ld_c = sem("ld_c")
        ld_d = sem("ld_d")
        ld_e = sem("ld_e")
        ld_moe = sem("ld_moe")
        bias_rows = sem("bias_rows")
        stored = sem("stored")
        memsets = sem("memsets")
        vt_zero = sem("vt_zero")
        mrows = sem("mrows")
        prep_mm = sem("prep_mm")
        prep_act = sem("prep_act")
        prep_dve = sem("prep_dve")
        wstat_ready = sem("wstat_ready")
        wred_ready = sem("wred_ready")
        kt_ready = sem("kt_ready")
        prep_steps = sem("prep_steps")
        consts_ready = sem("consts_ready")
        ternary_ready = sem("ternary_ready")
        xb_ready = sem("xb_ready")
        kbd1_ready = sem("kbd1_ready")
        recip_ready = sem("recip_ready")
        norm_ready = sem("norm_ready")
        quant_ready = sem("quant_ready")
        quantT_psum = sem("quantT_psum")
        quantT_ready = sem("quantT_ready")
        bit_out = sem("bit_out")
        hid_ready = sem("hid_ready")
        gelu_ready = sem("gelu_ready")
        fc_psum = sem("fc_psum")
        fc_gelu = sem("fc_gelu")
        pj_out = sem("pj_out")
        ctxb_ready = sem("ctxb_ready")
        kbd3_ready = sem("kbd3_ready")
        sx_psum = sem("sx_psum")
        sx_neg = sem("sx_neg")
        sx_exp = sem("sx_exp")
        sxT_psum = sem("sxT_psum")
        sxT_ready = sem("sxT_ready")
        sx_out = sem("sx_out")
        gate_psum = sem("gate_psum")
        gate_ready = sem("gate_ready")
        tanh_ready = sem("tanh_ready")
        qf_psum = sem("qf_psum")
        qf_ready = sem("qf_ready")
        kfa_ready = sem("kfa_ready")
        kfd_ready = sem("kfd_ready")
        wv_ready = sem("wv_ready")
        vmix_steps = sem("vmix_steps")
        v_ready = sem("v_ready")
        sf_psum = sem("sf_psum")
        nmf_ready = sem("nmf_ready")
        ef_ready = sem("ef_ready")
        pf_psum = sem("pf_psum")
        pf_ready = sem("pf_ready")
        pv_out = sem("pv_out")
        mix_ready = sem("mix_ready")
        mixT_psum = sem("mixT_psum")
        mixT_ready = sem("mixT_ready")
        swo_out = sem("swo_out")
        router_psum = sem("router_psum")
        rneg_ready = sem("rneg_ready")
        rexp_ready = sem("rexp_ready")
        wte_ready = sem("wte_ready")
        dw_ready = sem("dw_ready")
        xw_psum = sem("xw_psum")
        xw_ready = sem("xw_ready")
        up_psum = sem("up_psum")
        silu_in = sem("silu_in")
        t1_ready = sem("t1_ready")
        h_ready = sem("h_ready")
        y_psum = sem("y_psum")
        yT_ready = sem("yT_ready")
        y_out = sem("y_out")
        out_ready = sem("out_ready")

        JOBS = ([("K0", c, "ad") for c in range(NC8)] + [("M0", c, "a") for c in range(NC8)] + [("b0", 0, "d")]
                + [("V0", c, "ad") for c in range(NC8)] + [("VO", c, "da"[c % 2]) for c in range(NC8)]
                + [("b0T", 0, "a")]
                + [("K1", 0, "d"), ("V1", 0, "d"), ("K3", 0, "d"), ("V3", 0, "d"), ("Lfc", 0, "d"), ("Lpj", 0, "d")])
        JOB = {(k, c): n for n, (k, c, _) in enumerate(JOBS)}
        FIRST_JOBS = JOB["K1", 0]

        def job_bank(n):
            return ps[:, n % 8 if n < FIRST_JOBS else 4 + n % 4, :]

        def read_by(engine, n):
            return sum(engine in r for _, _, r in JOBS[:n + 1])

        def weave(order, front, other):
            for c in order:
                next(front if c == "F" else other, None)
            alone(front)
            alone(other)

        def alone(half):
            for _ in half:
                pass

        block = ctx.enter_context(nc.Block())

        @block.sync
        def _(sp):
            sp.dma_start(wa_sb[:, 0:1280], wa[:, 0:1280]).then_inc(ld_a, 16)
            sp.dma_start(cols_sb[:, :], cols).then_inc(ld_small, 16)
            sp.dma_start(wa_sb[:, 1280:4352], wa[:, 1280:4352]).then_inc(ld_a, 16)
            sp.dma_start(const_sb[:, :], const).then_inc(ld_small, 16)
            sp.dma_start(xall[:, :, :], x.rearrange("(t p) d -> p t d", p=P)).then_inc(ld_x, 16)
            sp.dma_start(wb_sb, wb).then_inc(ld_b, 16)
            sp.dma_start(rows_sb[:, :], rows.to_broadcast([P, 1152])).then_inc(ld_small, 16)
            sp.dma_start(wc_sb[:, :], wc[:, 0:1280]).then_inc(ld_c, 16)
            sp.dma_start(ctxT2, wc[:, 1280:1792]).then_inc(ld_c, 16)
            sp.dma_start(wd_sb, wd).then_inc(ld_d, 16)
            sp.dma_start(lora_sb[:, 0:640], lora[:, 0:640]).then_inc(ld_d, 16)
            sp.dma_start(loraB_sb[:, 0:640], lora[:, 640:1280]).then_inc(ld_d, 16)
            sp.wait_ge(mrows, 1)
            for b in range(B):
                sp.dma_start(bias0[0:1, b, :].rearrange("p (n k) -> p n k", k=CTX),
                             m0row[:, b, :].unsqueeze(1).to_broadcast([1, 16, CTX])).then_inc(bias_rows, 16)
            sp.wait_ge(prep_act, read_by("a", JOB["b0T", 0]))
            for r in range(3):
                sp.dma_start(bias0[r + 1:r + 2, :, :].rearrange("p b (c k) -> p (b c) k", k=P),
                             bpT[32 * r:32 * r + 32, :]).then_inc(bias_rows, 16)
            sp.dma_start(we_sb[:, :], we).then_inc(ld_e, 16)
            sp.dma_start(wo2_sb[:, :, :], wo2[0:256, :].rearrange("(c p) d -> p c d", p=P)).then_inc(ld_e, 16)
            sp.dma_start(wo2b_sb[:, :], wo2[256:320, :]).then_inc(ld_e, 16)
            sp.dma_start(ctxT_sb[:, :, :], wa[:, 0:256].rearrange("p (b k) -> p b k", b=B)).then_inc(ld_e, 16)
            sp.dma_start(ctxn_sb[:, :, :], ctxn.rearrange("b k d -> k b d")).then_inc(ld_e, 16)
            sp.wait_ge(prep_mm, len(JOBS))
            sp.wait_ge(prep_dve, read_by("d", len(JOBS)))
            sp.dma_start(gu_sb[:, :, :], gateup).then_inc(ld_moe, 16)
            for c, (i0, m) in enumerate(CHUNKS):
                sp.dma_start(dn_sb[0:m, :, c, :], down[:, i0:i0 + m, :].rearrange("e i d -> i e d")).then_inc(ld_moe, 16)
            out_t = out.rearrange("(t p) d -> p t d", p=P)
            with sp.Fori(0, B) as i:
                sp.wait_ge(out_ready, i * 2 + 2)
                sp.dma_start(out_t[:, bass.ds(2 * i, 2), :], xall[:, bass.ds(2 * i, 2), :]).then_inc(stored, 16)
            sp.wait_ge(stored, 16 * B)

        @block.gpsimd
        def _(pool):
            pool.memset(KTbd, 0.0).then_inc(memsets, 1)
            pool.memset(KFbd[:, :, :, :], 0.0).then_inc(memsets, 1)
            for v in Vbd[1:]:
                pool.memset(v[:, :, :, :], 0.0).then_inc(memsets, 1)
            pool.memset(mhalf[:, :], -0.5).then_inc(memsets, 1)
            pool.memset(ones_bf[:, :], 1.0).then_inc(memsets, 1)
            pool.dma_start(m0w, mask0).then_inc(ld_masks, 16)
            pool.dma_start(m1i[:, :, :], mask1.rearrange("(t p) k -> p t k", p=P)).then_inc(ld_masks, 16)
            pool.dma_start(m2i[:, :, :], mask2).then_inc(ld_masks, 16)
            pool.wait_ge(ld_small, 48)
            pool.wait_ge(memsets, 6)

            def power(h, n, which):
                yield
                pool.wait_ge(h.var_ready, n * h.n_pow + h.power[which] + 1)
                pool.tensor_tensor(h.rs[:, :], h.ve[:, :], mhalf[:, :], ALU.pow).then_inc(h.rstd_ready, 1)

            def add_bias(name, src):
                pool.tensor_tensor(XB[:, :, :], src,
                                   part(rows_sb, ROWS, name).unsqueeze(1).to_broadcast([P, TILES, D]),
                                   ALU.add).then_inc(xb_ready, 1)

            def small_keys(a, n, signal):
                pool.tensor_tensor(Kbd[a][:, :, :], KT[a][:, n, :].unsqueeze(1).to_broadcast([P, 16, CTX]),
                                   blockm.unsqueeze(2).to_broadcast([P, 16, CTX]), ALU.mult).then_inc(signal, 1)

            def prep():
                pool.wait_ge(wstat_ready, 1)
                pool.partition_all_reduce(wred[:, 0:2], wstat[:, 0:2], P, R_ADD).then_inc(wred_ready, 1)
                pool.wait_ge(wstat_ready, 2)
                pool.partition_all_reduce(wred[:, 2:4], wstat[:, 2:4], P, R_MAX).then_inc(wred_ready, 1)
                yield

            def front(n):
                yield from power(FR, n, 0)
                add_bias("bo0", xall[:, bass.ds(2 * n, 2), :])
                for s in range(TILES):
                    yield
                    pool.wait_ge(recip_ready, n * 2 + s + 1)
                    for h in range(2):
                        e = E1[:, s, 512 * h:512 * h + 512].rearrange("p (n k) -> p n k", k=CTX)
                        pool.tensor_tensor(e, e, FR.rc[:, s, 8 * h:8 * h + 8].unsqueeze(2).to_broadcast([P, 8, CTX]),
                                           ALU.mult).then_inc(norm_ready, 1)
                yield from power(FR, n, 1)
                add_bias("b2", FR.X[:, :, :])
                yield from power(FR, n, "rms1")
                yield from power(FR, n, "rms2")
                yield from power(FR, n, 2)
                add_bias("bo1", FR.X[:, :, :])
                yield
                pool.wait_ge(kt_ready, 1)
                small_keys(1, n, kbd1_ready)
                yield from power(FR, n, 3)
                add_bias("bpj", FR.X[:, :, :])

            def back(n):
                yield
                pool.wait_ge(ld_e, 80)
                pool.tensor_copy(ctxb[:, :], ctxn_sb[:, n, :]).then_inc(ctxb_ready, 1)
                yield from power(BA, n, 4)
                yield from power(BA, n, 5)
                for s in range(TILES):
                    yield
                    pool.wait_ge(wv_ready, n * 2 + s + 1)
                    pr4 = prod.rearrange("p (e h k) -> p e h k", e=E2X, k=DH2)
                    k = n * 6 + 3 * s
                    if s:
                        yield
                        pool.wait_ge(v_ready, n * 2 + s)
                    for e in range(E2X):
                        ins = pool.tensor_tensor(
                            pr4[:, e, :, :], XG[:, s, e * DH2:(e + 1) * DH2].unsqueeze(1).to_broadcast([P, H2, DH2]),
                            wv[:, s, :, e].unsqueeze(2).to_broadcast([P, H2, DH2]), ALU.mult)
                    ins.then_inc(vmix_steps, 1)
                    yield
                    pool.wait_ge(vmix_steps, k + 1)
                    pool.tensor_tensor(prod[:, 0:1024], prod[:, 0:1024], prod[:, 1024:2048], ALU.add).then_inc(vmix_steps, 1)
                    yield
                    pool.wait_ge(vmix_steps, k + 2)
                    pool.tensor_tensor(prod[:, 0:512], prod[:, 0:512], prod[:, 512:1024], ALU.add).then_inc(vmix_steps, 1)
                    yield
                    pool.wait_ge(vmix_steps, k + 3)
                    pool.tensor_tensor(V[:, s, :], prod[:, 0:512], prod[:, 2048:2560], ALU.add).then_inc(v_ready, 1)
                small_keys(2, n, kbd3_ready)
                yield from power(BA, n, 6)
                yield from power(BA, n, 7)
                for s in range(TILES):
                    yield
                    pool.wait_ge(wte_ready, n + 1)
                    pool.tensor_tensor(DW[:, s, :, :], ident.unsqueeze(1).to_broadcast([P, E3, P]),
                                       wte[:, s, :].unsqueeze(2).to_broadcast([P, E3, P]), ALU.mult).then_inc(dw_ready, 1)
                for e in range(E3):
                    for u in range(3 * e, 3 * e + 3):
                        m = CHUNKS[u % 3][1]
                        yield
                        pool.wait_ge(t1_ready, n * UNITS + u + 1)
                        pool.tensor_tensor(HT[0:m, u % RING, :], T1[0:m, u % RING, :], UC[0:m, u % RING, :],
                                           ALU.mult).then_inc(h_ready, 1)

            weave(OPENING["pool"], front(0), prep())
            pool.wait_ge(kt_ready, 2)
            with pool.Fori(1, B) as i:
                weave(WEAVE["pool"], front(i), back(i - 1))
            alone(back(B - 1))

        @block.scalar
        def _(act):
            def copy(out_ap, in_ap):
                return act.activation(out_ap, in_ap, ACT.Copy)

            act.wait_ge(ld_small, 48)
            act.wait_ge(memsets, 1)
            act.wait_ge(vt_zero, 1)
            for n, (kind, c, readers) in enumerate(JOBS):
                if "a" not in readers:
                    continue
                act.wait_ge(prep_mm, n + 1)
                bank = job_bank(n)
                if kind in ("K0", "V0"):
                    dst, bias = (KTbd, "bk0") if kind == "K0" else (VTbd, "bv0")
                    ins = act.activation(dst[0:64, c, :, 0:CTX], bank[0:64, 0:256].rearrange("p (b k) -> p b k", b=B),
                                         ACT.Identity, bias=part(cols_sb, COLS, bias)[0:64, c:c + 1])
                elif kind == "M0":
                    ins = copy(M0[:, :, c, :], bank.rearrange("p (b k) -> p b k", b=B))
                elif kind == "VO":
                    ins = copy(VO0[:, :, c, :], bank.rearrange("p (b k) -> p b k", b=B))
                else:
                    ins = copy(bpT[:, :], bank.bitcast(BF16)[0:96, 0:P])
                ins.then_inc(prep_act, 1)

            def x_transposed(h, n, l):
                k = TILES * h.norms.index(l)
                for s in range(TILES):
                    yield
                    act.wait_ge(h.xT_psum, n * h.n_xt + k + s + 1)
                    copy(h.XT[:, s * P:(s + 1) * P], h.Bk(s)[:, 0:P]).then_inc(h.xT_ready, 1)

            def exps(hf, n, E, a, k0, per):
                for s in range(TILES):
                    for h in range(2):
                        yield
                        act.wait_ge(hf.shifted, n * per + k0 + 2 * s + h + 1)
                        e = E[:, s, 512 * h:512 * h + 512]
                        act.activation(e, e, ACT.Exp, scale=SCALES[a]).then_inc(hf.exp_ready, 1)

            def probs_transposed(hf, n, E, k0, per):
                for s in range(TILES):
                    for h in range(2):
                        yield
                        act.wait_ge(hf.pT_psum, n * per + k0 + 2 * s + h + 1)
                        copy(E[:, s, 512 * h:512 * h + 512], hf.bank(s, h)).then_inc(hf.pT_ready, 1)

            def heads_transposed(h, n):
                for s in range(TILES):
                    yield
                    act.wait_ge(h.headsT_psum, n * 2 + s + 1)
                    copy(h.AOT[:, s, :], h.Bk(s)[:, 0:P]).then_inc(h.headsT_ready, 1)

            def prep():
                yield

            def front(n):
                yield from x_transposed(FR, n, 0)
                yield from exps(FR, n, E1, 0, 0, 8)
                yield from probs_transposed(FR, n, E1, 0, 8)
                for s in range(TILES):
                    yield
                    act.wait_ge(quantT_psum, n * 4 + s + 1)
                    copy(qTbf[:, s, 0:P], FR.Bk(s).bitcast(BF16)[:, 0:P]).then_inc(quantT_ready, 1)
                for s in range(TILES):
                    yield
                    act.wait_ge(hid_ready, n * 2 + s + 1)
                    act.activation(E1[:, s, 512:1024], E1[:, s, 0:512], ACT.Gelu).then_inc(gelu_ready, 1)
                for s in range(TILES):
                    yield
                    act.wait_ge(quantT_psum, n * 4 + 2 + s + 1)
                    copy(qTbf[:, s, :], FR.Bk(s).bitcast(BF16)[:, 0:FF]).then_inc(quantT_ready, 1)
                yield from x_transposed(FR, n, 2)
                yield
                act.wait_ge(FR.qT_psum, n + 1)
                act.activation(FR.QT[:, :], FR.A(0)[:, 0:256], ACT.Identity,
                               bias=part(cols_sb, COLS, "bq1")).then_inc(FR.qT_ready, 1)
                yield from exps(FR, n, E1, 1, 4, 8)
                yield from probs_transposed(FR, n, E1, 4, 8)
                yield from heads_transposed(FR, n)
                yield from x_transposed(FR, n, 3)
                for c in range(FF // P):
                    yield
                    act.wait_ge(fc_psum, n * 4 + c + 1)
                    act.activation(GT[:, c, :], FR.banks[c][:, 0:256], ACT.Gelu,
                                   bias=part(cols_sb, COLS, "bfc")[:, c:c + 1]).then_inc(fc_gelu, 1)

            def back(n):
                yield from x_transposed(BA, n, 4)
                for s in range(TILES):
                    yield
                    act.wait_ge(sx_neg, n * 2 + s + 1)
                    act.activation(E2[:, s, 0:CTX], BA.A(s)[:, 0:CTX], ACT.Exp, bias=BA.mxc[:, s, 0:1], scale=SCALE_L2X,
                                   accum_out=BA.sm[:, s, 0:1]).then_inc(sx_exp, 1)
                for s in range(TILES):
                    yield
                    act.wait_ge(sxT_psum, n * 2 + s + 1)
                    copy(E2[0:CTX, s, P:2 * P], BA.Bk(s)[0:CTX, 0:P]).then_inc(sxT_ready, 1)
                yield from x_transposed(BA, n, 5)
                for s in range(TILES):
                    yield
                    act.wait_ge(gate_psum, n * 2 + s + 1)
                    copy(XG[:, s, :], BA.A(s)[:, 0:400]).then_inc(gate_ready, 1)
                for s in range(TILES):
                    yield
                    act.wait_ge(gate_ready, n * 2 + s + 1)
                    act.activation(th[:, s, :], XG[:, s, XV:XV + 40], ACT.Tanh, scale=0.5).then_inc(tanh_ready, 1)
                for c in range(2):
                    yield
                    act.wait_ge(qf_psum, n * 4 + c + 1)
                    copy(QF[:, 2 * c:2 * c + 2, :].rearrange("p a b -> p (a b)"), BA.Bk(c)).then_inc(qf_ready, 1)
                for c in range(2):
                    yield
                    act.wait_ge(qf_psum, n * 4 + 2 + c + 1)
                    copy(KFbd[0:64, 2 * c:2 * c + 2, 0, :], BA.A(c)[0:64, :].rearrange("p (c k) -> p c k", c=2)).then_inc(
                        kfa_ready, 1)
                for k in range(HEAD_UNITS + 3):
                    if k >= 3:
                        j = k - 3
                        yield
                        act.wait_ge(pf_psum, n * HEAD_UNITS + j + 1)
                        copy(EF[:, j // 4, 2 * (j % 4):2 * (j % 4) + 2, :].rearrange("p h q -> p (h q)"),
                             head_bank(j)).then_inc(pf_ready, 1)
                    if 1 <= k <= HEAD_UNITS:
                        j = k - 1
                        s, c = divmod(j, 4)
                        yield
                        act.wait_ge(nmf_ready, n * HEAD_UNITS + j + 1)
                        for g in range(2):
                            h = 2 * c + g
                            act.activation(EF[:, s, h, :], head_bank(j)[:, g * S:(g + 1) * S], ACT.Exp,
                                           bias=nmf[:, s, h:h + 1], scale=SCALE_L2F,
                                           accum_out=smf[:, s, h:h + 1]).then_inc(ef_ready, 1)
                for s in range(TILES):
                    yield
                    act.wait_ge(mixT_psum, n * 2 + s + 1)
                    copy(AT[:, s, 0:2, :].rearrange("p a b -> p (a b)"), mix_bank(s)[:, 0:256])
                    copy(AT[0:64, s, 2, :], mix_bank(s)[0:64, 256:384]).then_inc(mixT_ready, 1)
                yield from x_transposed(BA, n, 6)
                yield from exps(BA, n, E2, 2, 0, 4)
                yield from probs_transposed(BA, n, E2, 0, 4)
                yield from heads_transposed(BA, n)
                yield from x_transposed(BA, n, 7)
                for s in range(TILES):
                    yield
                    act.wait_ge(rneg_ready, n * 2 + s + 1)
                    act.activation(pr[:, s, :], BA.A(s)[:, 0:E3], ACT.Exp, bias=rmx[:, s, 1:2],
                                   accum_out=rmx[:, s, 2:3]).then_inc(rexp_ready, 1)
                for s in range(TILES):
                    for h in range(2):
                        yield
                        act.wait_ge(xw_psum, n * 4 + 2 * s + h + 1)
                        copy(XTw[:, 4 * h:4 * h + 4, s * P:(s + 1) * P],
                             BA.bank(s, h).rearrange("p (e q) -> p e q", e=4)).then_inc(xw_ready, 1)
                for e in range(E3):
                    for u in range(3 * e, 3 * e + 3):
                        m = CHUNKS[u % 3][1]
                        yield
                        act.wait_ge(up_psum, n * UNITS + u + 1)
                        act.activation(TH[0:m, u % RING, :], up_bank(u)[0:m, 0:256], ACT.Tanh, scale=0.5)
                        copy(UC[0:m, u % RING, :], up_bank(u)[0:m, 256:512]).then_inc(silu_in, 1)
                yield
                act.wait_ge(y_psum, n + 1)
                copy(BA.AOT[:, :, :].rearrange("p t q -> p (t q)"), BA.A(0)[:, 0:256]).then_inc(yT_ready, 1)

            weave(OPENING["act"], front(0), prep())
            with act.Fori(1, B) as i:
                weave(WEAVE["act"], front(i), back(i - 1))
            alone(back(B - 1))

        @block.vector
        def _(dve):
            steps = [0]
            pads = iter(range(32))

            def pad():
                k = next(pads)
                return filler[:, k:k + 1]

            def count_prep(ins):
                steps[0] += 1
                ins.then_inc(prep_steps, 1)

            def settle_prep():
                dve.wait_ge(prep_steps, steps[0])

            dve.memset(VTbd, 0.0).then_inc(vt_zero, 1)
            dve.wait_ge(ld_masks, 48)
            count_prep(dve.tensor_scalar(m0row[:, :, :], m0w.bitcast(U8).rearrange("p (b k) -> p b k", b=B),
                                         MASKED, None, ALU.mult))
            dve.tensor_scalar(mneg1[:, :, :], m1i[:, :, :], 0.0, MASKED, ALU.is_equal, ALU.mult).then_inc(consts_ready, 1)
            dve.tensor_scalar(mneg2[:, :, :], m2i[:, :, :], 0.0, MASKED, ALU.is_equal, ALU.mult).then_inc(consts_ready, 1)
            settle_prep()
            dve.tensor_copy(pad()[0:1, :], m0row[0:1, 0, 0:1]).then_inc(mrows, 1)
            dve.wait_ge(ld_small, 48)
            dve.tensor_copy(ident_bf[:, :], ident).then_inc(consts_ready, 1)
            dve.wait_ge(memsets, 1)
            dve.wait_ge(vt_zero, 1)

            def weight_stats():
                dve.wait_ge(ld_b, 16)
                for n in range(2):
                    count_prep(dve.tensor_reduce(wstat[:, n:n + 1], wb_sb[:, 512 * n:512 * n + 512], X_AXIS, ALU.add,
                                                 apply_absolute_value=True))
                settle_prep()
                dve.tensor_copy(pad(), wstat[:, 0:1]).then_inc(wstat_ready, 1)
                dve.wait_ge(ld_d, 48)
                for n in range(2):
                    count_prep(dve.tensor_reduce(wstat[:, 2 + n:3 + n], wd_sb[:, 512 * n:512 * n + 512], X_AXIS, ALU.max,
                                                 apply_absolute_value=True))
                settle_prep()
                dve.tensor_copy(pad(), wstat[:, 2:3]).then_inc(wstat_ready, 1)

            def ternary_weights():
                dve.wait_ge(wred_ready, 1)
                count_prep(dve.tensor_scalar(wmean[:, :], wred[:, 0:2], 1.0 / (D * FF), 1e-5, ALU.mult, ALU.max))
                settle_prep()
                count_prep(dve.reciprocal(wsc[:, 0:2], wmean[:, :]))
                settle_prep()
                for n in range(2):
                    count_prep(dve.tensor_scalar(wtmp[:, 512 * n:512 * n + 512], wb_sb[:, 512 * n:512 * n + 512],
                                                 wsc[:, n:n + 1], ROUND, ALU.mult, ALU.add))
                settle_prep()
                count_prep(dve.tensor_scalar(wtmp2, wtmp, ROUND, -1.0, ALU.subtract, ALU.max))
                settle_prep()
                dve.tensor_scalar(w1q[:, :], wtmp2[:, 0:512], 1.0, None, ALU.min).then_inc(ternary_ready, 1)
                dve.tensor_scalar(w2q[:, :, :].rearrange("p c d -> p (c d)"), wtmp2[:, 512:1024], 1.0, None,
                                  ALU.min).then_inc(ternary_ready, 1)

            def int8_weights():
                dve.wait_ge(wred_ready, 2)
                count_prep(dve.tensor_scalar(wsc[:, 0:2], wred[:, 2:4], 1.0 / QMAX, None, ALU.mult))
                settle_prep()
                count_prep(dve.reciprocal(wsc[:, 2:4], wsc[:, 0:2]))
                settle_prep()
                dve.wait_ge(ternary_ready, 2)
                for n in range(2):
                    count_prep(dve.tensor_scalar(wtmp[:, 512 * n:512 * n + 512], wd_sb[:, 512 * n:512 * n + 512],
                                                 wsc[:, 2 + n:3 + n], ROUND, ALU.mult, ALU.add))
                settle_prep()
                for n in range(2):
                    count_prep(dve.tensor_scalar(wtmp2[:, 512 * n:512 * n + 512], wtmp[:, 512 * n:512 * n + 512], ROUND,
                                                 wsc[:, n:n + 1], ALU.subtract, ALU.mult))
                settle_prep()

            def read_job(n):
                kind, c, readers = JOBS[n]
                dve.wait_ge(prep_mm, n + 1)
                bank = job_bank(n)
                if kind in ("K0", "V0"):
                    dst, bias = (KTbd, "bk0") if kind == "K0" else (VTbd, "bv0")
                    ins = dve.tensor_scalar(dst[64:128, c, :, CTX:P], bank[64:128, 0:256].rearrange("p (b k) -> p b k", b=B),
                                            part(cols_sb, COLS, bias)[64:128, c:c + 1], None, ALU.add)
                elif kind == "VO":
                    ins = dve.tensor_copy(VO0[:, :, c, :], bank.rearrange("p (b k) -> p b k", b=B))
                elif kind == "b0":
                    v, r1, r2 = bank[:, 0:32], bres[:, 0, :], bres[:, 1, :]
                    hi, mid, lo = (bpart[:, r, :, :].rearrange("p b c -> p (b c)") for r in range(3))
                    count_prep(dve.tensor_copy(hi, v))
                    settle_prep()
                    count_prep(dve.tensor_tensor(r1, v, hi, ALU.subtract))
                    settle_prep()
                    count_prep(dve.tensor_copy(mid, r1))
                    settle_prep()
                    count_prep(dve.tensor_tensor(r2, r1, mid, ALU.subtract))
                    settle_prep()
                    ins = dve.tensor_copy(lo, r2)
                elif kind == "K1":
                    ins = dve.tensor_scalar(KT1, bank[:, 0:256], part(cols_sb, COLS, "bk1"), None, ALU.add)
                elif kind == "K3":
                    for src, dst, tab in ((bank[:, 0:256], KT3a, cosT), (bank[:, 256:512], KT3b, sinT)):
                        count_prep(dve.tensor_tensor(dst.rearrange("p (b k) -> p b k", b=B),
                                                     src.rearrange("p (b k) -> p b k", b=B),
                                                     tab[:, 0:CTX].unsqueeze(1).to_broadcast([P, B, CTX]), ALU.mult))
                    settle_prep()
                    ins = dve.tensor_tensor(KT3, KT3a, KT3b, ALU.add)
                elif kind in ("V1", "V3"):
                    dst = Vbd[1] if kind == "V1" else Vbd[2]
                    v = bank.rearrange("p (b c q d) -> p b c q d", b=B, c=NC8, q=2)
                    bv = part(rows_sb, ROWS, "bv1").rearrange("p (c q d) -> p c q d", q=2, d=8)
                    for q in range(2):
                        rows_q = slice(64 * q, 64 * q + 64)
                        for b in range(B):
                            o = dst[rows_q, b, :, 8 * q:8 * q + 8]
                            if kind == "V1":
                                ins = dve.tensor_tensor(o, v[rows_q, b, :, q, :], bv[rows_q, :, q, :], ALU.add)
                            else:
                                ins = dve.tensor_copy(o, v[rows_q, b, :, q, :])
                            if (q, b) != (1, B - 1):
                                count_prep(ins)
                elif kind == "Lfc":
                    ins = dve.scalar_tensor_tensor(wfc[:, :], bank, LORA_SCALE, wtmp2[:, 0:512], ALU.mult, ALU.add)
                elif kind == "Lpj":
                    ins = dve.scalar_tensor_tensor(wpj[:, :, :].rearrange("p c d -> p (c d)"), bank, LORA_SCALE,
                                                   wtmp2[:, 512:1024], ALU.mult, ALU.add)
                ins.then_inc(prep_dve, 1)
                if kind in ("K1", "K3"):
                    dve.wait_ge(prep_dve, read_by("d", n))
                    dve.tensor_copy(pad(), (KT1 if kind == "K1" else KT3)[:, 0:1]).then_inc(kt_ready, 1)

            for n in range(FIRST_JOBS):
                if n == JOB["VO", 0]:
                    weight_stats()
                if "d" in JOBS[n][2]:
                    read_job(n)

            def prep():
                ternary_weights()
                dve.wait_ge(memsets, 6)
                for v in Vbd[1:]:
                    count_prep(dve.memset(v[0:64, :, :, 16:17], 1.0))
                    count_prep(dve.memset(v[64:128, :, :, 17:18], 1.0))
                yield
                read_job(JOB["K1", 0])
                yield
                read_job(JOB["V1", 0])
                yield
                read_job(JOB["K3", 0])
                yield
                read_job(JOB["V3", 0])
                yield
                int8_weights()
                read_job(JOB["Lfc", 0])
                read_job(JOB["Lpj", 0])
                yield

            class Steps:

                def __init__(self, h, n, per):
                    self.h, self.n, self.per, self.count = h, n, per, 0

                def step(self, ins):
                    self.count += 1
                    ins.then_inc(self.h.dve_seq, 1)
                    return self.count

                def settle(self, mark=None):
                    dve.wait_ge(self.h.dve_seq, self.n * self.per + (self.count if mark is None else mark))

            def stats(c, src):
                h = c.h
                for s in range(TILES):
                    c.step(dve.bn_stats(h.st[:, s, :], src(s)))
                c.settle()
                c.step(dve.tensor_copy(h.pad[:, :], ident[:, 0:1]))
                for s in range(TILES):
                    c.step(dve.bn_aggr(h.mv[:, s, :], h.st[:, s, :]))
                c.settle()

            def layer_norm(c, l, src, sink=True):
                h, n = c.h, c.n
                stats(c, src)
                dve.tensor_scalar(h.ve[:, :], h.mv[:, :, 1], EPS, None, ALU.add).then_inc(h.var_ready, 1)
                yield
                dve.wait_ge(h.rstd_ready, n * h.n_pow + h.power[l] + 1)
                for s in range(TILES):
                    ins = dve.tensor_scalar(h.XH[:, s, :], src(s), h.mv[:, s, 0:1], h.rs[:, s:s + 1],
                                            ALU.subtract, ALU.mult)
                    if sink:
                        ins.then_inc(h.xhat_ready, 1)
                    else:
                        c.step(ins)

            def softmax(c, E, a, k0, per):
                hf, n = c.h, c.n
                marks = []
                for s in range(TILES):
                    for h in range(2):
                        yield
                        dve.wait_ge(hf.scores_ready, n * per + k0 + 2 * s + h + 1)
                        c.step(dve.tensor_reduce(hf.mx[:, s, 8 * h:8 * h + 8],
                                                 hf.bank(s, h).rearrange("p (n k) -> p n k", k=CTX), X_AXIS, ALU.max))
                    marks.append(c.count)
                top = hf.mx
                if CLAMPS[a] is not None:
                    top = hf.mxc
                    for s in range(TILES):
                        c.settle(marks[s])
                        marks[s] = c.step(dve.tensor_scalar(hf.mxc[:, s, :], hf.mx[:, s, :], CLAMPS[a], None, ALU.max))
                for s in range(TILES):
                    c.settle(marks[s])
                    for h in range(2):
                        sc = hf.bank(s, h).rearrange("p (n k) -> p n k", k=CTX)
                        e = E[:, s, 512 * h:512 * h + 512].rearrange("p (n k) -> p n k", k=CTX)
                        m = top[:, s, 8 * h:8 * h + 8].unsqueeze(2).to_broadcast([P, 8, CTX])
                        if CLAMPS[a] is not None:
                            ins = dve.scalar_tensor_tensor(e, sc, CLAMPS[a], m, ALU.max, ALU.subtract)
                        else:
                            ins = dve.tensor_tensor(e, sc, m, ALU.subtract)
                        ins.then_inc(hf.shifted, 1)

            def head_norms(c, a, k0, per):
                h, n = c.h, c.n
                marks = []
                for s in range(TILES):
                    yield
                    dve.wait_ge(h.attn_out, n * per + k0 + s + 1)
                    o = h.A(s)[:, 0:144].rearrange("p (c v) -> p c v", v=18)
                    marks.append(c.step(dve.reciprocal(h.rc[:, s, :].rearrange("p (c q) -> p c q", q=2), o[:, :, 16:18])))
                for s in range(TILES):
                    c.settle(marks[s])
                    o = h.A(s)[:, 0:144].rearrange("p (c v) -> p c v", v=18)[:, :, 0:16].rearrange(
                        "p c (q d) -> p c q d", q=2)
                    r = h.rc[:, s, :].rearrange("p (c q) -> p c q", q=2).unsqueeze(3).to_broadcast([P, 8, 2, 8])
                    dve.tensor_tensor(h.AO[:, s, :].rearrange("p (c q d) -> p c q d", q=2, d=8), o, r,
                                      ALU.mult).then_inc(h.heads_ready, 1)

            def beats(c, dst, g, n):
                groups = g.shape[1]
                for f in range(n):
                    pick = g[:, :, f:f + 1]
                    c.step(dve.tensor_tensor(dst[:, :, 0:f + 1, f], pick.to_broadcast([P, groups, f + 1]),
                                             g[:, :, 0:f + 1], ALU.is_gt))
                    if f < n - 1:
                        c.step(dve.tensor_tensor(dst[:, :, f + 1:n, f], pick.to_broadcast([P, groups, n - 1 - f]),
                                                 g[:, :, f + 1:n], ALU.is_ge))

            def rms_quant(c, which, ms_src, src, width, weight):
                h, n = c.h, c.n
                amax, am, ra, s1, deq = (q_small[:, k, :] for k in range(1, 6))
                ms_src()
                for s in range(TILES):
                    c.step(dve.tensor_reduce(amax[:, s:s + 1], src(s), X_AXIS, ALU.max, apply_absolute_value=True))
                c.settle()
                yield
                dve.wait_ge(h.rstd_ready, n * h.n_pow + h.power[which] + 1)
                c.step(dve.tensor_tensor(am, amax, h.rs[:, :], ALU.mult))
                c.settle()
                c.step(dve.tensor_scalar(am, am, 1e-5, None, ALU.max))
                c.settle()
                c.step(dve.reciprocal(ra, am))
                c.step(dve.tensor_scalar(deq, am, 1.0 / QMAX, wmean[:, weight:weight + 1], ALU.mult, ALU.mult))
                c.settle()
                c.step(dve.scalar_tensor_tensor(s1, ra, QMAX, h.rs[:, :], ALU.mult, ALU.mult))
                c.settle()
                for s in range(TILES):
                    c.step(dve.tensor_scalar(E1[:, s, 0:width], src(s), s1[:, s:s + 1], ROUND, ALU.mult, ALU.add))
                c.settle()
                for s in range(TILES):
                    dve.tensor_scalar(qbf[:, s, 0:width], E1[:, s, 0:width], ROUND, None,
                                      ALU.subtract).then_inc(quant_ready, 1)
                return deq

            def front(n):
                c = Steps(FR, n, F_STEPS)
                X = FR.X
                yield from layer_norm(c, 0, lambda s: xall[:, 2 * n + s, :])
                yield from softmax(c, E1, 0, 0, 8)
                for s in range(TILES):
                    for h in range(2):
                        yield
                        dve.wait_ge(FR.exp_ready, n * 8 + 2 * s + h + 1)
                        c.step(dve.tensor_reduce(FR.sm[:, s, 8 * h:8 * h + 8],
                                                 E1[:, s, 512 * h:512 * h + 512].rearrange("p (n k) -> p n k", k=CTX),
                                                 X_AXIS, ALU.add))
                    c.settle()
                    dve.reciprocal(FR.rc[:, s, :], FR.sm[:, s, :]).then_inc(recip_ready, 1)
                yield
                dve.wait_ge(xb_ready, n * 4 + 1)
                for s in range(TILES):
                    yield
                    dve.wait_ge(FR.attn_out, n * 4 + s + 1)
                    c.step(dve.tensor_tensor(X[:, s, :], FR.A(s)[:, 0:D], XB[:, s, :], ALU.add))
                c.settle()
                yield from layer_norm(c, 1, lambda s: X[:, s, :], sink=False)
                c.settle()

                def ms_of_xhat():
                    t = q_small[:, 6, :]
                    c.step(dve.tensor_tensor(t, FR.rs[:, :], FR.rs[:, :], ALU.mult))
                    c.settle()
                    c.step(dve.tensor_tensor(t, t, FR.mv[:, :, 1], ALU.mult))
                    c.settle()
                    dve.tensor_scalar(FR.ve[:, :], t, RMS_EPS, None, ALU.add).then_inc(FR.var_ready, 1)

                deq = yield from rms_quant(c, "rms1", ms_of_xhat, lambda s: FR.XH[:, s, :], D, 0)
                for s in range(TILES):
                    yield
                    dve.wait_ge(bit_out, n * 4 + s + 1)
                    dve.scalar_tensor_tensor(E1[:, s, 0:512], FR.A(s), deq[:, s:s + 1], part(rows_sb, ROWS, "b1"),
                                             ALU.mult, ALU.add).then_inc(hid_ready, 1)

                def ms_of_hidden():
                    stats(c, lambda s: E1[:, s, 512:1024])
                    t = q_small[:, 6, :]
                    c.step(dve.tensor_tensor(t, FR.mv[:, :, 0], FR.mv[:, :, 0], ALU.mult))
                    c.settle()
                    c.step(dve.tensor_tensor(t, t, FR.mv[:, :, 1], ALU.add))
                    c.settle()
                    dve.tensor_scalar(FR.ve[:, :], t, RMS_EPS, None, ALU.add).then_inc(FR.var_ready, 1)

                yield
                dve.wait_ge(gelu_ready, n * 2 + 2)
                deq = yield from rms_quant(c, "rms2", ms_of_hidden, lambda s: E1[:, s, 512:1024], FF, 1)
                yield
                dve.wait_ge(xb_ready, n * 4 + 2)
                for s in range(TILES):
                    yield
                    dve.wait_ge(bit_out, n * 4 + 2 + s + 1)
                    c.step(dve.scalar_tensor_tensor(X[:, s, :], FR.A(s)[:, 0:D], deq[:, s:s + 1], XB[:, s, :],
                                                    ALU.mult, ALU.add))
                c.settle()
                yield from layer_norm(c, 2, lambda s: X[:, s, :])
                yield from softmax(c, E1, 1, 4, 8)
                yield from head_norms(c, 1, 2, 4)
                yield
                dve.wait_ge(xb_ready, n * 4 + 3)
                for s in range(TILES):
                    yield
                    dve.wait_ge(FR.proj_out, n * 2 + s + 1)
                    c.step(dve.tensor_tensor(X[:, s, :], FR.A(s)[:, 256:384], XB[:, s, :], ALU.add))
                c.settle()
                yield from layer_norm(c, 3, lambda s: X[:, s, :])
                yield
                dve.wait_ge(xb_ready, n * 4 + 4)
                for s in range(TILES):
                    yield
                    dve.wait_ge(pj_out, n * 2 + s + 1)
                    c.step(dve.tensor_tensor(hand[:, s, :], FR.A(s)[:, 0:D], XB[:, s, :], ALU.add))
                c.settle()
                assert c.count == F_STEPS, f"F_STEPS = {c.count}"

            def back(n):
                c = Steps(BA, n, B_STEPS)
                X = BA.X
                yield
                dve.wait_ge(FR.dve_seq, n * F_STEPS + F_STEPS)
                yield from layer_norm(c, 4, lambda s: hand[:, s, :])
                for s in range(TILES):
                    yield
                    dve.wait_ge(sx_psum, n * 2 + s + 1)
                    c.step(dve.tensor_reduce(BA.mx[:, s, 0:1], BA.A(s)[:, 0:CTX], X_AXIS, ALU.max))
                    c.settle()
                    dve.tensor_scalar(BA.mxc[:, s, 0:1], BA.mx[:, s, 0:1], -SCALE_L2X, None, ALU.mult).then_inc(sx_neg, 1)
                yield
                dve.wait_ge(sx_exp, n * 2 + 2)
                c.step(dve.reciprocal(BA.rc[:, :, 0], BA.sm[:, :, 0]))
                c.settle()
                for s in range(TILES):
                    yield
                    dve.wait_ge(sx_out, n * 2 + s + 1)
                    c.step(dve.scalar_tensor_tensor(X[:, s, :], BA.A(s)[:, 128:256], BA.rc[:, s, 0:1], hand[:, s, :],
                                                    ALU.mult, ALU.add))
                c.settle()
                yield from layer_norm(c, 5, lambda s: X[:, s, :])
                for cc in range(2):
                    yield
                    dve.wait_ge(qf_psum, n * 4 + 2 + cc + 1)
                    dve.tensor_copy(KFbd[64:128, 2 * cc:2 * cc + 2, 1, :],
                                    BA.A(cc)[64:128, :].rearrange("p (c k) -> p c k", c=2)).then_inc(kfd_ready, 1)
                yield
                dve.wait_ge(gate_ready, n * 2 + 2)
                for s in range(TILES):
                    beats(c, cmp[:, s * G2:(s + 1) * G2, :, :], XG[:, s, XV:].rearrange("p (g e) -> p g e", e=E2X), E2X)
                c.settle()
                c.step(dve.tensor_reduce(cnt[:, :, :], cmp[:, :, :, :], X_AXIS, ALU.add))
                yield
                dve.wait_ge(tanh_ready, n * 2 + 2)
                c.step(dve.tensor_scalar(th[:, :, :], th[:, :, :], 0.5, 0.5, ALU.mult, ALU.add))
                c.settle()
                chosen = cnt[:, :, :].rearrange("p (t g) e -> p t g e", t=TILES)
                for s in range(TILES):
                    dve.scalar_tensor_tensor(wv[:, s, :, :], chosen[:, s, 0:H2, :], SEL - 0.5,
                                             th[:, s, :].rearrange("p (h e) -> p h e", e=E2X),
                                             ALU.is_lt, ALU.mult).then_inc(wv_ready, 1)
                for k in range(HEAD_UNITS + 3):
                    if k < HEAD_UNITS:
                        s, cc = divmod(k, 4)
                        yield
                        dve.wait_ge(sf_psum, n * HEAD_UNITS + k + 1)
                        c.step(dve.tensor_reduce(mxf[:, s, 2 * cc:2 * cc + 2], head_bank(k).rearrange("p (h k) -> p h k", h=2),
                                                 X_AXIS, ALU.max))
                        c.settle()
                        dve.tensor_scalar(nmf[:, s, 2 * cc:2 * cc + 2], mxf[:, s, 2 * cc:2 * cc + 2], -SCALE_L2F, None,
                                          ALU.mult).then_inc(nmf_ready, 1)
                for s in range(TILES):
                    yield
                    dve.wait_ge(ef_ready, n * 16 + 8 * s + 8)
                    c.step(dve.reciprocal(rcf[:, s, :], smf[:, s, :]))
                    c.settle()
                    c.step(dve.scalar_tensor_tensor(mo[:, s, :, :], chosen[:, s, H2:G2, :], SEL - 0.5,
                                                    rcf[:, s, :].unsqueeze(2).to_broadcast([P, H2, E2X]),
                                                    ALU.is_lt, ALU.mult))
                    c.settle()
                    yield
                    dve.wait_ge(pv_out, n * 2 + s + 1)
                    pr4 = prod.rearrange("p (h e k) -> p h e k", h=H2, k=DH2)
                    for h in range(H2):
                        c.step(dve.tensor_tensor(
                            pr4[:, h, :, :], heads_out(s)[:, h * DH2:(h + 1) * DH2].unsqueeze(1).to_broadcast([P, E2X, DH2]),
                            mo[:, s, h, :].unsqueeze(2).to_broadcast([P, E2X, DH2]), ALU.mult))
                    c.settle()
                    c.step(dve.tensor_tensor(prod[:, 0:1280], prod[:, 0:1280], prod[:, 1280:2560], ALU.add))
                    c.settle()
                    c.step(dve.tensor_tensor(prod[:, 0:640], prod[:, 0:640], prod[:, 640:1280], ALU.add))
                    c.settle()
                    dve.tensor_tensor(Amix[:, s, :], prod[:, 0:320], prod[:, 320:640], ALU.add).then_inc(mix_ready, 1)
                    yield
                    dve.wait_ge(mix_ready, n * 2 + s + 1)
                for s in range(TILES):
                    yield
                    dve.wait_ge(swo_out, n * 2 + s + 1)
                    c.step(dve.tensor_tensor(X[:, s, :], mix_bank(s)[:, 0:D], X[:, s, :], ALU.add))
                c.settle()
                yield from layer_norm(c, 6, lambda s: X[:, s, :])
                yield
                dve.wait_ge(BA.qT_psum, n + 1)
                rope = BA.AO[:, :, :].rearrange("p t q -> p (t q)"), BA.AOT[:, :, :].rearrange("p t q -> p (t q)")
                for k, tab in enumerate((cosT, sinT)):
                    c.step(dve.tensor_tensor(rope[k], BA.A(0)[:, 256 * k:256 * k + 256], tab, ALU.mult))
                c.settle()
                dve.tensor_tensor(BA.QT[:, :], rope[0], rope[1], ALU.add).then_inc(BA.qT_ready, 1)
                yield from softmax(c, E2, 2, 0, 4)
                yield from head_norms(c, 2, 0, 2)
                for s in range(TILES):
                    yield
                    dve.wait_ge(BA.proj_out, n * 2 + s + 1)
                    c.step(dve.tensor_tensor(X[:, s, :], BA.A(s)[:, 256:384], X[:, s, :], ALU.add))
                c.settle()
                yield from layer_norm(c, 7, lambda s: X[:, s, :])
                for s in range(TILES):
                    yield
                    dve.wait_ge(router_psum, n * 2 + s + 1)
                    c.step(dve.tensor_reduce(rmx[:, s, 0:1], BA.A(s)[:, 0:E3], X_AXIS, ALU.max))
                    c.settle()
                    dve.tensor_scalar(rmx[:, s, 1:2], rmx[:, s, 0:1], -1.0, None, ALU.mult).then_inc(rneg_ready, 1)
                yield
                dve.wait_ge(rexp_ready, n * 2 + 2)
                c.step(dve.reciprocal(rmx[:, :, 3], rmx[:, :, 2]))
                c.settle()
                c.step(dve.tensor_tensor(pr[:, :, :], pr[:, :, :], rmx[:, :, 3].unsqueeze(2).to_broadcast([P, TILES, E3]),
                                         ALU.mult))
                c.settle()
                beats(c, cmp3[:, :, :, :], pr[:, :, :], E3)
                c.settle()
                c.step(dve.tensor_scalar(pr[:, :, :], pr[:, :, :], 0.5, None, ALU.mult))
                c.step(dve.tensor_reduce(cnt3[:, :, :], cmp3[:, :, :, :], X_AXIS, ALU.add))
                c.settle()
                dve.scalar_tensor_tensor(wte[:, :, :], cnt3[:, :, :], SEL - 0.5, pr[:, :, :], ALU.is_lt,
                                         ALU.mult).then_inc(wte_ready, 1)
                for e in range(E3):
                    for u in range(3 * e, 3 * e + 3):
                        m = CHUNKS[u % 3][1]
                        yield
                        dve.wait_ge(silu_in, n * UNITS + u + 1)
                        dve.scalar_tensor_tensor(T1[0:m, u % RING, :], TH[0:m, u % RING, :], 1.0, up_bank(u)[0:m, 0:256],
                                                 ALU.add, ALU.mult).then_inc(t1_ready, 1)
                for s in range(TILES):
                    yield
                    dve.wait_ge(y_out, n * 2 + s + 1)
                    dve.tensor_tensor(xall[:, 2 * n + s, :], mix_bank(s)[:, 0:D], X[:, s, :], ALU.add).then_inc(out_ready, 1)
                assert c.count == B_STEPS, f"B_STEPS = {c.count}"

            weave(OPENING["dve"], front(0), prep())
            settle_prep()
            with dve.Fori(1, B) as i:
                weave(WEAVE["dve"], front(i), back(i - 1))
            alone(back(B - 1))

        @block.tensor
        def _(pe):
            pe.wait_ge(ld_a, 32)
            W = {k: part(wa_sb, WA, k) for k in WA}
            ctxT = W["ctxT"]

            def product(n):
                kind, c, _ = JOBS[n]
                last = n - 8 if n < FIRST_JOBS else max(n - 4, FIRST_JOBS - 1)
                if last >= 0:
                    if read_by("a", last):
                        pe.wait_ge(prep_act, read_by("a", last))
                    if read_by("d", last):
                        pe.wait_ge(prep_dve, read_by("d", last))
                bank = job_bank(n)
                if kind in ("K0", "V0"):
                    w = W["WkT" if kind == "K0" else "WvT"]
                    mm = pe.matmul(bank[:, 0:256], w[:, c * P:(c + 1) * P], ctxT, start=True, stop=True)
                elif kind == "M0":
                    pe.wait_ge(prep_act, read_by("a", JOB["K0", c]))
                    pe.wait_ge(prep_dve, read_by("d", JOB["K0", c]))
                    mm = pe.matmul(bank, W["Wq"][:, c * P:(c + 1) * P], KTbd[:, c, :, :].rearrange("p b k -> p (b k)"),
                                   start=True, stop=True)
                elif kind == "b0":
                    pe.wait_ge(ld_small, 48)
                    for b in range(B):
                        for cc in range(NC8):
                            mm = pe.matmul(bank[:, b * NC8 + cc:b * NC8 + cc + 1], KTbd[:, cc, b, :],
                                           part(cols_sb, COLS, "bq0")[:, cc:cc + 1], start=True, stop=True)
                elif kind == "VO":
                    pe.wait_ge(prep_act, read_by("a", JOB["V0", c]))
                    pe.wait_ge(prep_dve, read_by("d", JOB["V0", c]))
                    for b in range(B):
                        mm = pe.matmul(bank[:, b * P:(b + 1) * P], VTbd[:, c, b, :], W["WoT"][:, c * P:(c + 1) * P],
                                       start=True, stop=True)
                elif kind == "b0T":
                    pe.wait_ge(prep_dve, read_by("d", JOB["b0", 0]))
                    pe.wait_ge(consts_ready, 3)
                    mm = pe.transpose(bank.bitcast(BF16)[0:96, 0:P],
                                      bpart[:, :, :, :].rearrange("p r b c -> p (r b c)"), ident_bf[:, :])
                elif kind == "K1":
                    pe.wait_ge(ld_c, 32)
                    mm = pe.matmul(bank[:, 0:256], wcol("Wk1"), ctxT, start=True, stop=True)
                elif kind == "K3":
                    pe.matmul(bank[:, 0:256], wcol("Wk3"), ctxT, start=True, stop=True)
                    mm = pe.matmul(bank[:, 256:512], wcol("Wk3s"), ctxT, start=True, stop=True)
                elif kind in ("V1", "V3"):
                    for b in range(B):
                        mm = pe.matmul(bank[:, b * P:(b + 1) * P], ctxT2[:, b * P:(b + 1) * P],
                                       wcol("Wv1" if kind == "V1" else "Wv3"), start=True, stop=True)
                elif kind == "Lfc":
                    pe.wait_ge(ld_d, 48)
                    mm = pe.matmul(bank, lora_sb[:, 0:128], lora_sb[:, 128:640], start=True, stop=True)
                else:
                    for cc in range(FF // P):
                        mm = pe.matmul(bank[:, cc * P:(cc + 1) * P], loraB_sb[:, cc * P:(cc + 1) * P],
                                       loraB_sb[:, 512:640], start=True, stop=True)
                mm.then_inc(prep_mm, 1)

            for n in range(FIRST_JOBS):
                product(n)

            def prep():
                yield
                for kind in ("K1", "V1", "K3", "V3"):
                    product(JOB[kind, 0])
                    yield
                product(JOB["Lfc", 0])
                product(JOB["Lpj", 0])
                yield

            pe.wait_ge(prep_act, read_by("a", FIRST_JOBS - 1))
            pe.wait_ge(prep_dve, read_by("d", FIRST_JOBS - 1))
            pe.wait_ge(memsets, 6)
            pe.wait_ge(bias_rows, 16 * (B + 3))

            def x_transposed(h, n, l):
                k = TILES * h.norms.index(l)
                for s in range(TILES):
                    yield
                    pe.wait_ge(h.xhat_ready, n * h.n_xt + k + s + 1)
                    pe.transpose(h.Bk(s)[:, 0:P], h.XH[:, s, :], ident).then_inc(h.xT_psum, 1)

            def xt_wait(h, n, l, s):
                pe.wait_ge(h.xT_ready, n * h.n_xt + TILES * h.norms.index(l) + s + 1)

            def xt(h, s):
                return h.XT[:, s * P:(s + 1) * P]

            def probs_transposed(hf, n, E, k0, per):
                for s in range(TILES):
                    for h in range(2):
                        if hf is FR and k0 == 0:
                            yield
                            pe.wait_ge(norm_ready, n * 4 + 2 * s + h + 1)
                        else:
                            yield
                            pe.wait_ge(hf.exp_ready, n * per + k0 + 2 * s + h + 1)
                        for c in range(4):
                            mm = pe.transpose(hf.bank(s, h)[:, c * P:(c + 1) * P],
                                              E[:, s, 512 * h + c * P:512 * h + (c + 1) * P], ident)
                        mm.then_inc(hf.pT_psum, 1)

            def small_values(hf, n, E, a, k0, per):
                for s in range(TILES):
                    yield
                    pe.wait_ge(hf.pT_ready, n * per + k0 + 2 * s + 2)
                    for c in range(NC8):
                        mm = pe.matmul(hf.A(s)[:, 18 * c:18 * c + 18], E[:, s, c * P:(c + 1) * P], Vbd[a][:, n, c, :],
                                       start=True, stop=True)
                    mm.then_inc(hf.attn_out, 1)

            def project(hf, n, w):
                for s in range(TILES):
                    yield
                    pe.wait_ge(hf.heads_ready, n * 2 + s + 1)
                    pe.transpose(hf.Bk(s)[:, 0:P], hf.AO[:, s, :], ident).then_inc(hf.headsT_psum, 1)
                for s in range(TILES):
                    yield
                    pe.wait_ge(hf.headsT_ready, n * 2 + s + 1)
                    pe.matmul(hf.A(s)[:, 256:384], hf.AOT[:, s, :], wcol(w), start=True, stop=True).then_inc(hf.proj_out, 1)

            def front(n):
                yield from x_transposed(FR, n, 0)
                for s in range(TILES):
                    yield
                    xt_wait(FR, n, 0, s)
                    for h in range(2):
                        pe.matmul(FR.bank(s, h), xt(FR, s), M0[:, n, 4 * h:4 * h + 4, :].rearrange("p c k -> p (c k)"),
                                  start=True, stop=False)
                        pe.matmul(FR.bank(s, h), ones_bf[:, :], bias0[:, n, 512 * h:512 * h + 512], start=False,
                                  stop=True).then_inc(FR.scores_ready, 1)
                yield from probs_transposed(FR, n, E1, 0, 8)
                for s in range(TILES):
                    yield
                    pe.wait_ge(FR.pT_ready, n * 8 + 2 * s + 2)
                    for c in range(NC8):
                        mm = pe.matmul(FR.A(s)[:, 0:D], E1[:, s, c * P:(c + 1) * P], VO0[:, n, c, :], start=(c == 0),
                                       stop=(c == NC8 - 1))
                    mm.then_inc(FR.attn_out, 1)
                yield
                pe.wait_ge(ternary_ready, 2)
                for s in range(TILES):
                    yield
                    pe.wait_ge(quant_ready, n * 4 + s + 1)
                    pe.transpose(FR.Bk(s).bitcast(BF16)[:, 0:P], qbf[:, s, 0:P], ident_bf[:, :]).then_inc(quantT_psum, 1)
                for s in range(TILES):
                    yield
                    pe.wait_ge(quantT_ready, n * 4 + s + 1)
                    pe.matmul(FR.A(s), qTbf[:, s, 0:P], w1q[:, :], start=True, stop=True).then_inc(bit_out, 1)
                for s in range(TILES):
                    yield
                    pe.wait_ge(quant_ready, n * 4 + 2 + s + 1)
                    for c in range(FF // P):
                        mm = pe.transpose(FR.Bk(s).bitcast(BF16)[:, c * P:(c + 1) * P], qbf[:, s, c * P:(c + 1) * P],
                                          ident_bf[:, :])
                    mm.then_inc(quantT_psum, 1)
                for s in range(TILES):
                    yield
                    pe.wait_ge(quantT_ready, n * 4 + 2 + s + 1)
                    for c in range(FF // P):
                        mm = pe.matmul(FR.A(s)[:, 0:D], qTbf[:, s, c * P:(c + 1) * P], w2q[:, c, :], start=(c == 0),
                                       stop=(c == FF // P - 1))
                    mm.then_inc(bit_out, 1)
                yield from x_transposed(FR, n, 2)
                yield
                pe.wait_ge(ld_c, 32)
                yield
                xt_wait(FR, n, 2, 1)
                pe.matmul(FR.A(0)[:, 0:256], wcol("Wq1"), FR.XT[:, :], start=True, stop=True).then_inc(FR.qT_psum, 1)
                yield
                pe.wait_ge(kbd1_ready, n + 1)
                pe.wait_ge(FR.qT_ready, n + 1)
                for s in range(TILES):
                    for h in range(2):
                        pe.matmul(FR.bank(s, h), FR.QT[:, s * P:(s + 1) * P],
                                  Kbd[1][:, 8 * h:8 * h + 8, :].rearrange("p n k -> p (n k)"), start=True, stop=False)
                        pe.matmul(FR.bank(s, h), ident_bf[:, :], mneg1[:, s, :].unsqueeze(1).to_broadcast([P, 8, CTX]),
                                  start=False, stop=True).then_inc(FR.scores_ready, 1)
                yield from probs_transposed(FR, n, E1, 4, 8)
                yield from small_values(FR, n, E1, 1, 4, 8)
                yield from project(FR, n, "Wo1")
                yield from x_transposed(FR, n, 3)
                yield
                pe.wait_ge(prep_dve, read_by("d", len(JOBS)))
                yield
                xt_wait(FR, n, 3, 1)
                for c in range(FF // P):
                    pe.matmul(FR.banks[c][:, 0:256], wfc[:, c * P:(c + 1) * P], FR.XT[:, :],
                              start=True, stop=True).then_inc(fc_psum, 1)
                for s in range(TILES):
                    yield
                    pe.wait_ge(fc_gelu, n * 4 + 4)
                    for c in range(FF // P):
                        mm = pe.matmul(FR.A(s)[:, 0:D], GT[:, c, s * P:(s + 1) * P], wpj[:, c, :], start=(c == 0),
                                       stop=(c == FF // P - 1))
                    mm.then_inc(pj_out, 1)

            def up(n, u):
                e, c = divmod(u, 3)
                i0, m = CHUNKS[c]
                if u >= UP_BANKS:
                    yield
                    pe.wait_ge(t1_ready, n * UNITS + u - UP_BANKS + 1)
                for w, rhs in enumerate((BA.XT[:, :], XTw[:, e, :])):
                    mm = pe.matmul(up_bank(u)[0:m, 256 * w:256 * w + 256], gu_sb[:, w, e * I3 + i0:e * I3 + i0 + m], rhs,
                                   start=True, stop=True)
                mm.then_inc(up_psum, 1)

            def down_product(n, u):
                e, c = divmod(u, 3)
                m = CHUNKS[c][1]
                yield
                pe.wait_ge(h_ready, n * UNITS + u + 1)
                mm = pe.matmul(BA.A(0)[:, 0:256], dn_sb[0:m, e, c, :], HT[0:m, u % RING, :], start=(u == 0),
                               stop=(u == UNITS - 1))
                if u == UNITS - 1:
                    mm.then_inc(y_psum, 1)

            def back(n):
                yield from x_transposed(BA, n, 4)
                for s in range(TILES):
                    yield
                    xt_wait(BA, n, 4, s)
                    pe.matmul(BA.A(s)[:, 0:CTX], xt(BA, s), ctxT_sb[:, n, :], start=True, stop=False)
                    pe.matmul(BA.A(s)[:, 0:CTX], ones_bf[0:1, :], mneg2[:, n, :], start=False, stop=True).then_inc(sx_psum, 1)
                for s in range(TILES):
                    yield
                    pe.wait_ge(sx_exp, n * 2 + s + 1)
                    pe.matmul(BA.Bk(s)[0:CTX, 0:P], E2[:, s, 0:CTX], ident, start=True, stop=True).then_inc(sxT_psum, 1)
                for s in range(TILES):
                    if s == 0:
                        yield
                        pe.wait_ge(ctxb_ready, n + 1)
                    pe.wait_ge(sxT_ready, n * 2 + s + 1)
                    pe.matmul(BA.A(s)[:, 128:256], E2[0:CTX, s, P:2 * P], ctxb[:, :], start=True, stop=True).then_inc(sx_out, 1)
                yield from x_transposed(BA, n, 5)
                for s in range(TILES):
                    yield
                    xt_wait(BA, n, 5, s)
                    pe.matmul(BA.A(s)[:, 0:400], xt(BA, s), part(we_sb, WE, "VSD"), start=True, stop=True).then_inc(gate_psum, 1)
                for w, name in enumerate(("Wq", "Wk")):
                    if w == 1:
                        yield
                        pe.wait_ge(gate_ready, n * 2 + 2)
                    for c in range(H2 // 2):
                        bank = (BA.Bk, BA.A)[w](c // 2)
                        mm = pe.matmul(bank[:, (c % 2) * 256:(c % 2) * 256 + 256], part(we_sb, WE, name)[:, c * P:(c + 1) * P],
                                       BA.XT[:, :], start=True, stop=True)
                        if c % 2:
                            mm.then_inc(qf_psum, 1)
                for k in range(HEAD_UNITS + 3):
                    if k == 0:
                        yield
                        pe.wait_ge(qf_ready, n * 2 + 2)
                        pe.wait_ge(kfa_ready, n * 2 + 2)
                        pe.wait_ge(kfd_ready, n * 2 + 2)
                    if k < HEAD_UNITS:
                        s, c = divmod(k, 4)
                        if k >= HEAD_BANKS:
                            yield
                            pe.wait_ge(pf_ready, n * HEAD_UNITS + k - HEAD_BANKS + 1)
                        pe.matmul(head_bank(k), QF[:, c, s * P:(s + 1) * P], KFbd[:, c, :, :].rearrange("p h k -> p (h k)"),
                                  start=True, stop=True).then_inc(sf_psum, 1)
                    if 2 <= k < HEAD_UNITS + 2:
                        j = k - 2
                        s, c = divmod(j, 4)
                        yield
                        pe.wait_ge(ef_ready, n * 16 + 2 * j + 2)
                        for g in range(2):
                            for q in range(2):
                                mm = pe.transpose(head_bank(j)[:, g * S + q * P:g * S + (q + 1) * P],
                                                  EF[:, s, 2 * c + g, q * P:(q + 1) * P], ident)
                        mm.then_inc(pf_psum, 1)
                    if k in (7, 10):
                        s = (7, 10).index(k)
                        if s == 0:
                            yield
                            pe.wait_ge(v_ready, n * 2 + 2)
                        yield
                        pe.wait_ge(pf_ready, n * HEAD_UNITS + 4 * s + 4)
                        for h in range(H2):
                            for j in range(2):
                                mm = pe.matmul(heads_out(s)[:, h * DH2:(h + 1) * DH2], EF[:, s, h, j * P:(j + 1) * P],
                                               V[:, j, h * DH2:(h + 1) * DH2], start=(j == 0), stop=(j == 1))
                        mm.then_inc(pv_out, 1)
                for s in range(TILES):
                    yield
                    pe.wait_ge(mix_ready, n * 2 + s + 1)
                    pe.transpose(mix_bank(s)[:, 0:128], Amix[:, s, 0:128], ident)
                    pe.transpose(mix_bank(s)[:, 128:256], Amix[:, s, 128:256], ident)
                    pe.transpose(mix_bank(s)[0:64, 256:384], Amix[:, s, 256:320], ident).then_inc(mixT_psum, 1)
                for s in range(TILES):
                    yield
                    pe.wait_ge(mixT_ready, n * 2 + s + 1)
                    bank = mix_bank(s)[:, 0:D]
                    pe.matmul(bank, AT[:, s, 0, :], wo2_sb[:, 0, :], start=True, stop=False)
                    pe.matmul(bank, AT[:, s, 1, :], wo2_sb[:, 1, :], start=False, stop=False)
                    pe.matmul(bank, AT[0:64, s, 2, :], wo2b_sb[:, :], start=False, stop=True).then_inc(swo_out, 1)
                yield from x_transposed(BA, n, 6)
                yield
                xt_wait(BA, n, 6, 1)
                pe.matmul(BA.A(0)[:, 0:256], wcol("Wq3"), BA.XT[:, :], start=True, stop=True)
                pe.matmul(BA.A(0)[:, 256:512], wcol("Wq3s"), BA.XT[:, :], start=True, stop=True).then_inc(BA.qT_psum, 1)
                yield
                pe.wait_ge(kbd3_ready, n + 1)
                pe.wait_ge(BA.qT_ready, n + 1)
                for s in range(TILES):
                    for h in range(2):
                        pe.matmul(BA.bank(s, h), BA.QT[:, s * P:(s + 1) * P],
                                  Kbd[2][:, 8 * h:8 * h + 8, :].rearrange("p n k -> p (n k)"), start=True,
                                  stop=True).then_inc(BA.scores_ready, 1)
                yield from probs_transposed(BA, n, E2, 0, 4)
                yield from small_values(BA, n, E2, 2, 0, 4)
                yield from project(BA, n, "Wo3")
                yield from x_transposed(BA, n, 7)
                for s in range(TILES):
                    yield
                    xt_wait(BA, n, 7, s)
                    pe.matmul(BA.A(s)[:, 0:E3], xt(BA, s), part(we_sb, WE, "router"), start=True, stop=True).then_inc(router_psum, 1)
                yield
                pe.wait_ge(rexp_ready, n * 2 + 2)
                for s in range(TILES):
                    yield
                    pe.wait_ge(dw_ready, n * 2 + s + 1)
                    for h in range(2):
                        pe.matmul(BA.bank(s, h), BA.XH[:, s, :], DW[:, s, 4 * h:4 * h + 4, :].rearrange("p e q -> p (e q)"),
                                  start=True, stop=True).then_inc(xw_psum, 1)
                for e in range(E3):
                    if e == 0:
                        yield
                        pe.wait_ge(ld_moe, 64)
                        pe.wait_ge(xw_ready, n * 4 + 4)
                    for u in range(3 * e, 3 * e + 3):
                        yield from up(n, u)
                        if u >= LAG:
                            yield from down_product(n, u - LAG)
                for u in range(UNITS - LAG, UNITS):
                    yield from down_product(n, u)
                yield
                pe.wait_ge(yT_ready, n + 1)
                for s in range(TILES):
                    pe.transpose(mix_bank(s)[:, 0:P], BA.AOT[:, s, :], ident).then_inc(y_out, 1)

            weave(OPENING["pe"], front(0), prep())
            pe.wait_ge(ld_e, 80)
            with pe.Fori(1, B) as i:
                weave(WEAVE["pe"], front(i), back(i - 1))
            alone(back(B - 1))


def rope_tables():
    inv = (1.0 / np.float32(10000.0) ** (np.arange(0, 8, 2, dtype=np.float32) / np.float32(8))).astype(np.float32)
    freqs = np.outer(np.arange(S, dtype=np.float32), inv).astype(np.float32)
    d = np.arange(P) % 8
    cos = np.cos(freqs).T[d // 2]
    sin = np.sin(freqs).T[d // 2] * np.where(d % 2 == 0, -1.0, 1.0)[:, None]
    return cos.astype(np.float32), sin.astype(np.float32)


def chunked(a):
    return a.reshape(-1, P, a.shape[1]).transpose(1, 0, 2).reshape(P, -1)


def kernel(**inputs):
    import concourse.bacc as bacc
    from concourse.bass_utils import run_bass_kernel_spmd

    a = {k: np.asarray(v) for k, v in inputs.items()}
    cat = lambda *parts: np.ascontiguousarray(np.concatenate(parts, axis=1))
    col = lambda v: v.reshape(-1, P).T
    ctx = a["ctx_1024"]
    ctxT = ctx.reshape(B * CTX, D).T
    ctxT2 = np.stack([ctx, ctx], axis=1).reshape(2 * B * CTX, D).T
    swap = np.arange(P) ^ 1
    cos, sin = rope_tables()
    block = (np.arange(P)[:, None] // 8 == np.arange(16)[None, :]).astype(np.float32)
    w3q, w3k = a["L3_xattn_Wq"], a["L3_xattn_Wk"]
    wv2 = a["L2_ffn_Wv"].transpose(1, 0, 2).reshape(D, XV)
    arrays = {
        "x": a["x"].reshape(B * S, D),
        "wa": cat(ctxT, a["L0_xattn_Wk"].T, a["L0_xattn_Wv"].T, chunked(a["L0_xattn_Wq"]), chunked(a["L0_xattn_Wo"].T)),
        "cols": cat(col(a["L0_xattn_bq"]), col(a["L0_xattn_bk"]), col(a["L0_xattn_bv"]), col(a["L1_xattn_bq"]),
                    col(a["L1_xattn_bk"]), col(a["L1_ffn_b_fc"])),
        "rows": cat(*(a[n][None, :] for n in ("L0_xattn_bo", "L0_ffn_b2", "L1_xattn_bo", "L1_ffn_b_proj", "L0_ffn_b1",
                                              "L1_xattn_bv"))),
        "wb": cat(a["L0_ffn_w1"].T, chunked(a["L0_ffn_w2"].T)),
        "wc": cat(a["L1_xattn_Wq"].T, a["L1_xattn_Wk"].T, a["L1_xattn_Wv"].T, a["L1_xattn_Wo"].T, w3q.T, w3q[swap].T,
                  w3k.T, w3k[swap].T, a["L3_xattn_Wv"].T, a["L3_xattn_Wo"].T, ctxT2),
        "wd": cat(a["L1_ffn_W_fc"].T, chunked(a["L1_ffn_W_proj"].T)),
        "lora": cat(a["L1_ffn_A_fc"], a["L1_ffn_B_fc"].T, a["L1_ffn_A_proj"], a["L1_ffn_B_proj"].T),
        "we": cat(a["L2_ffn_Wq"], a["L2_ffn_Wk"], wv2, a["L2_ffn_Ws"], a["L2_ffn_Wd"], a["L3_ffn_router_w"].T),
        "wo2": a["L2_ffn_Wo"].reshape(XV, D),
        "ctxn": ctx,
        "gateup": np.ascontiguousarray(np.stack([a["L3_ffn_gate_w"].transpose(2, 0, 1).reshape(D, -1),
                                                 a["L3_ffn_up_w"].transpose(2, 0, 1).reshape(D, -1)], axis=1)),
        "down": np.ascontiguousarray(a["L3_ffn_down_w"].transpose(0, 2, 1)),
        "const": cat(np.eye(P, dtype=np.float32), cos, sin, block),
        "mask0": a["mask_BxS2_bk0"].reshape(1, B * CTX).view(np.int32),
        "mask1": a["mask_1x1xSxS2_ik0"].reshape(S, CTX),
        "mask2": a["mask_BxS2_ik1"].reshape(1, B, CTX),
    }
    arrays = {f"in_{k}": np.ascontiguousarray(v) for k, v in arrays.items()}
    nc = bacc.Bacc("TRN2", target_bir_lowering=False, num_devices=1)
    args = [nc.dram_tensor(k, v.shape, mybir.dt.from_np(v.dtype), kind="ExternalInput").ap() for k, v in arrays.items()]
    args.append(nc.dram_tensor("out_0_dram", (B * S, D), F32, kind="ExternalOutput").ap())
    build(nc, *args)
    r = run_bass_kernel_spmd(nc, [arrays], core_ids=[0])
    return r.results[0]["out_0_dram"].reshape(B, S, D)
```

```python
from contextlib import ExitStack

import numpy as np

import concourse.bass as bass
from concourse import mybir

F32 = mybir.dt.float32
BF16 = mybir.dt.bfloat16
I32 = mybir.dt.int32
U8 = mybir.dt.uint8
ALU = mybir.AluOpType
ACT = mybir.ActivationFunctionType
X_AXIS = mybir.AxisListType.X
R_ADD = bass.bass_isa.ReduceOp.add
R_MAX = bass.bass_isa.ReduceOp.max

P = 128
D = 128
B, S, CTX = 4, 256, 64
TILES = S // P
NC8 = 8
FF = 512
H2, DH2, E2X, SEL = 8, 64, 5, 2
G2 = 2 * H2
XV = E2X * DH2
E3, I3 = 8, 352
CHUNKS = [(0, 128), (128, 128), (256, 96)]
UNITS = E3 * len(CHUNKS)
UP_BANKS = 3
RING = 4
LAG = 2
HEAD_UNITS = 8
HEAD_BANKS = 3
PV_LAG = 5
POOL_HEADS = 3
EPS = 1e-5
RMS_EPS = 1e-5
QMAX = 127.0
ROUND = 12582912.0
MASKED = -1e30
SCALE_L0 = 0.125
SCALE_L1 = float(1.0 / np.sqrt(np.float32(8)))
SCALE_L2X = float(1.0 / np.sqrt(128.0))
SCALE_L2F = 0.125
SCALES = [SCALE_L0, SCALE_L1, SCALE_L1]
CLAMPS = [-1e9 / SCALE_L0, -1e9 / SCALE_L1, None]
LORA_SCALE = 2.0

WA = {"ctxT": (0, 256), "WkT": (256, 1024), "WvT": (1280, 1024), "Wq": (2304, 1024), "WoT": (3328, 1024)}
COLS = {"bq0": (0, 8), "bk0": (8, 8), "bv0": (16, 8), "bq1": (24, 1), "bk1": (25, 1), "bfc": (26, 4)}
ROWS = {"bo0": (0, 128), "b2": (128, 128), "bo1": (256, 128), "bpj": (384, 128), "b1": (512, 512), "bv1": (1024, 128)}
WC = {n: (128 * k, 128) for k, n in enumerate(
    ["Wq1", "Wk1", "Wv1", "Wo1", "Wq3", "Wq3s", "Wk3", "Wk3s", "Wv3", "Wo3"])}
WE = {"Wq": (0, 512), "Wk": (512, 512), "VSD": (1024, 400), "router": (1424, 8)}
CONST = {"ident": (0, 128), "cos": (128, 256), "sin": (384, 256), "block": (640, 16)}

OPENING = {
    "pool": "FFPPFFPFFFFFFFFF",
    "act": "FPFFPFPPFPPFFPPPPFPPPFFFFFFFFFFFFFFFFFFFFFFFFFFFFFFFFFFFFFFFFFFFF",
    "dve": "PFPFPPPPFFPFFPFPPFPPPFFPPFFFFFFPFFFFFPPFFFFPPFFFFPFPFFFFFFFFFFFFFFF",
    "pe": "PPPPFPFFFPFPPPPPPPPFFPPPFFFFFFFFPFFFFPFFPFFFPFFFFFFFFFPPFFFFFFFFFFFFFFFFF",
}
WEAVE = {
    "pool": "FFBBBBBBFFBBBBBBFFBFFFBBBBBBBFBBBBBBFFBBBBBBFBBBBBB",
    "act": "BBBBBFBFFBBFBBFFBBFBBBBBFBBFFFBBFFBBFFBBFFBBBBBBFFBBFBBFBBFBFFBFFBFFBFBFBBBFFBBFFFFBBBBBFF"
            "BFFFBFBBBFFBFBFFFBFBFFF",
    "dve": "FBBBBFBBBFBFFBFFFBBFBFBBBBFFBFBBFBFFBFBBFBBFFBFBBBFBFFBFBBBFBBFBBFBFFBBBBBBBBFBFFBBBFBFBBF"
            "BFFBFBBBFFBBFBBFFFB",
    "pe": "FBBBFBBFBBFBBFBBBBBBFBBBFFBBBFBBFFBBBBFFBFBFBBBFBFFFBBBBFFBBFBBFBBBBBFFFBBFFBFBFBFBFFBBBBB"
            "BFFBFBBBBBBFFBBBBBFBFFBBFBFBFBBFBBBBBFBFFBBBFBBFBBB",
}

F_POW = {0: 0, 1: 1, "rms1": 2, "rms2": 3, 2: 4, 3: 5, 4: 6, 5: 7}
B_POW = {6: 0, 7: 1}
F_LN = [0, 2, 3, 4, 5]
B_LN = [6, 7]
F_STEPS = 112
B_STEPS = 115


def build(nc, x, wa, cols, rows, wb, wc, wd, lora, we, wo2, ctxn, gateup, down, const, mask0, mask1, mask2, out):
    ctx = ExitStack()
    with ctx:
        def sb(name, shape, dt=F32):
            return ctx.enter_context(nc.sbuf_tensor(name, shape, dt))

        def sem(name):
            return ctx.enter_context(nc.semaphore(name))

        wc_sb = sb("wc_sb", [P, 1280])
        we_sb = sb("we_sb", [P, 1432])
        cols_sb = sb("cols_sb", [P, 30])
        rows_sb = sb("rows_sb", [P, 1152])
        const_sb = sb("const_sb", [P, 656])
        wo2_sb = sb("wo2_sb", [P, 2, D])
        wo2b_sb = sb("wo2b_sb", [XV - 2 * P, D])
        ctxn_sb = sb("ctxn_sb", [CTX, B, D])
        ctxb = sb("ctxb", [CTX, D])
        ctxT_sb = sb("ctxT_sb", [P, B, CTX])
        gu_sb = sb("gu_sb", [P, 2, E3 * I3])
        dn_sb = sb("dn_sb", [P, E3, len(CHUNKS), D])
        ident_bf = sb("ident_bf", [P, P], BF16)
        ones_bf = sb("ones_bf", [4, P], BF16)
        w1q = sb("w1q", [P, FF], BF16)
        w2q = sb("w2q", [P, FF // P, D], BF16)
        wfc = sb("wfc", [P, FF])
        wpj = sb("wpj", [P, FF // P, D])
        wmean = sb("wmean", [P, 2])
        mhalf = sb("mhalf", [P, TILES])
        M0 = sb("M0", [P, B, NC8, P])
        VO0 = sb("VO0", [P, B, NC8, D])
        bias0 = sb("bias0", [4, B, NC8 * P], BF16)
        KT = [None, sb("KT1", [P, B, CTX]), sb("KT3", [P, B, CTX])]
        Kbd = [None, sb("Kbd1", [P, 16, CTX]), sb("Kbd3", [P, 16, CTX])]
        Vbd = [None, sb("Vbd1", [P, B, NC8, 18]), sb("Vbd3", [P, B, NC8, 18])]
        mneg1 = sb("mneg1", [P, TILES, CTX], BF16)
        mneg2 = sb("mneg2", [1, B, CTX], BF16)
        xall = sb("xall", [P, B * TILES, D])
        hand = sb("hand", [P, TILES, D])
        XB = sb("XB", [P, TILES, D])
        work = sb("work", [P, 2048 + 2560])
        E1 = work[:, 0:2048].rearrange("p (t c) -> p t c", t=TILES)
        prod = work[:, 2048:]
        EF = sb("EF", [P, TILES, H2, S])
        EF_flat = EF[:, :, :, :].rearrange("p t h q -> p (t h q)")
        E2 = EF_flat[:, 0:2048].rearrange("p (t c) -> p t c", t=TILES)
        q_small = sb("q_small", [P, 8, TILES])
        qbf = sb("qbf", [P, TILES, FF], BF16)
        qTbf = sb("qTbf", [P, TILES, FF], BF16)
        GT = sb("GT", [P, FF // P, TILES * P])
        QF = sb("QF", [P, H2 // 2, S])
        KFbd = sb("KFbd", [P, H2 // 2, 2, S])
        XG = sb("XG", [P, TILES, XV + E2X * G2])
        HO = QF[:, :, :].rearrange("p (t a) b -> p t (a b)", t=TILES)
        cmp = EF_flat[:, 0:TILES * G2 * E2X * E2X].rearrange("p (g e f) -> p g e f", e=E2X, f=E2X)
        cnt = sb("cnt", [P, TILES * G2, E2X])
        th = sb("th", [P, TILES, E2X * H2])
        wv = sb("wv", [P, TILES, H2, E2X])
        mo = sb("mo", [P, TILES, H2, E2X])
        V = sb("V", [P, TILES, FF])
        mxf = sb("mxf", [P, TILES, H2])
        nmf = sb("nmf", [P, TILES, H2])
        smf = sb("smf", [P, TILES, H2])
        rcf = sb("rcf", [P, TILES, H2])
        Amix = XG[:, :, 0:XV]
        AT = QF[:, :, :].rearrange("p a b -> p (a b)")[:, 0:TILES * 3 * P].rearrange("p (t c q) -> p t c q", t=TILES, c=3)
        TH = prod[:, 0:1024].rearrange("p (r q) -> p r q", q=S)
        UC = prod[:, 1024:2048].rearrange("p (r q) -> p r q", q=S)
        T1 = V[:, :, :].rearrange("p t (r q) -> p (t r) q", q=S)
        HT = sb("HT", [P, RING, S])
        rmx = sb("rmx", [P, TILES, 4])
        pr = sb("pr", [P, TILES, E3])
        cmp3 = prod[:, 2048:2048 + TILES * E3 * E3].rearrange("p (t e f) -> p t e f", t=TILES, e=E3)
        cnt3 = sb("cnt3", [P, TILES, E3])
        wte = sb("wte", [P, TILES, E3])
        filler = sb("filler", [P, 32])
        KVbd = EF_flat.rearrange("p (c b k) -> p c b k", c=NC8, b=B)
        wa_sb = gu_sb[:, :, :].rearrange("p a b -> p (a b)")[:, 0:4352]
        dn_flat = dn_sb[:, :, :, :].rearrange("p a b c -> p (a b c)")
        wb_sb = dn_flat[:, 0:1024]
        wd_sb = dn_flat[:, 1024:2048]
        wtmp = dn_flat[:, 2048:3072]
        wtmp2 = GT[:, :, :].rearrange("p a b -> p (a b)")
        lora_sb = HT[0:16, :, :].rearrange("p a b -> p (a b)")
        loraB_sb = V[0:16, :, :].rearrange("p a b -> p (a b)")
        KT1 = KT[1][:, :, :].rearrange("p b k -> p (b k)")
        KT3 = KT[2][:, :, :].rearrange("p b k -> p (b k)")
        KT3a = EF_flat[:, 0:256]
        KT3b = EF_flat[:, 256:512]
        wstat = sb("wstat", [P, 4])
        wred = sb("wred", [P, 4])
        wsc = sb("wsc", [P, 4])
        ps = ctx.enter_context(nc.psum_tensor("ps", [P, 8, 512], F32))

        class Half:

            def __init__(self, name, bank0, power, norms):
                self.power, self.norms = power, norms
                self.n_pow, self.n_xt = len(power), TILES * len(norms)
                self.banks = [ps[:, bank0 + k, :] for k in range(4)]
                self.XH = sb(f"{name}_XH", [P, TILES, D])
                self.XT = sb(f"{name}_XT", [P, TILES * P])
                self.X = sb(f"{name}_X", [P, TILES, D])
                self.st = sb(f"{name}_st", [P, TILES, 6])
                self.mv = sb(f"{name}_mv", [P, TILES, 2])
                self.pad = sb(f"{name}_pad", [P, 1])
                self.ve = sb(f"{name}_ve", [P, TILES])
                self.rs = sb(f"{name}_rs", [P, TILES])
                self.mx = sb(f"{name}_mx", [P, TILES, 16])
                self.mxc = sb(f"{name}_mxc", [P, TILES, 16])
                self.sm = sb(f"{name}_sm", [P, TILES, 16])
                self.rc = sb(f"{name}_rc", [P, TILES, 16])
                self.QT = sb(f"{name}_QT", [P, TILES * P])
                self.AO = sb(f"{name}_AO", [P, TILES, D])
                self.AOT = sb(f"{name}_AOT", [P, TILES, P])
                self.dve_seq = sem(f"{name}_dve_seq")
                self.var_ready = sem(f"{name}_var_ready")
                self.rstd_ready = sem(f"{name}_rstd_ready")
                self.xhat_ready = sem(f"{name}_xhat_ready")
                self.xT_psum = sem(f"{name}_xT_psum")
                self.xT_ready = sem(f"{name}_xT_ready")
                self.scores_ready = sem(f"{name}_scores_ready")
                self.shifted = sem(f"{name}_shifted")
                self.exp_ready = sem(f"{name}_exp_ready")
                self.pT_psum = sem(f"{name}_pT_psum")
                self.pT_ready = sem(f"{name}_pT_ready")
                self.attn_out = sem(f"{name}_attn_out")
                self.qT_psum = sem(f"{name}_qT_psum")
                self.qT_ready = sem(f"{name}_qT_ready")
                self.heads_ready = sem(f"{name}_heads_ready")
                self.headsT_psum = sem(f"{name}_headsT_psum")
                self.headsT_ready = sem(f"{name}_headsT_ready")
                self.proj_out = sem(f"{name}_proj_out")

            def A(self, s):
                return self.banks[2 * s]

            def Bk(self, s):
                return self.banks[2 * s + 1]

            def bank(self, s, h):
                return self.banks[2 * s + h]

        FR = Half("front", 0, F_POW, F_LN)
        BA = Half("back", 4, B_POW, B_LN)
        spare = BA.AO[:, :, :].rearrange("p t d -> p (t d)")
        bpart = spare[:, 0:48].bitcast(BF16).rearrange("p (r b c) -> p r b c", r=3, b=B)
        bres = spare[:, 64:128].rearrange("p (r k) -> p r k", r=2)
        bpT = spare[0:96, 128:192].bitcast(BF16)
        m0w = spare[0:1, 192:256].bitcast(I32)
        m0row = BA.QT[0:1, 0:128].bitcast(BF16).rearrange("p (b k) -> p b k", b=B)
        m1i = BA.XH[:, 0, :].bitcast(I32).rearrange("p (t k) -> p t k", t=TILES)
        m2i = BA.XT[0:1, 0:B * CTX].bitcast(I32).rearrange("p (b k) -> p b k", b=B)
        ctxT2 = QF[:, :, :].rearrange("p a b -> p (a b)")[:, 0:512]

        def part(t, table, name):
            a, n = table[name]
            return t[:, a:a + n]

        def wcol(name):
            return part(wc_sb, WC, name)

        ident = part(const_sb, CONST, "ident")
        cosT = part(const_sb, CONST, "cos")
        sinT = part(const_sb, CONST, "sin")
        blockm = part(const_sb, CONST, "block")

        def head_bank(k):
            return BA.banks[1 + k % HEAD_BANKS]

        def heads_out(s):
            return BA.banks[s]

        def mix_bank(s):
            return BA.banks[2 + s]

        def normalise(engine, s, h):
            e = E1[:, s, 512 * h:512 * h + 512].rearrange("p (n k) -> p n k", k=CTX)
            return engine.tensor_tensor(e, e, FR.rc[:, s, 8 * h:8 * h + 8].unsqueeze(2).to_broadcast([P, 8, CTX]), ALU.mult)

        def mo_product(engine, s, h):
            pr4 = prod.rearrange("p (h e k) -> p h e k", h=H2, k=DH2)
            return engine.tensor_tensor(
                pr4[:, h, :, :], HO[:, s, h * DH2:(h + 1) * DH2].unsqueeze(1).to_broadcast([P, E2X, DH2]),
                mo[:, s, h, :].unsqueeze(2).to_broadcast([P, E2X, DH2]), ALU.mult)

        def router_out(s):
            return BA.banks[0][:, E3 * s:E3 * s + E3]

        def up_bank(u):
            return BA.banks[1 + u % UP_BANKS]

        ld_a = sem("ld_a")
        ld_wq = sem("ld_wq")
        ld_wv = sem("ld_wv")
        ld_cols = sem("ld_cols")
        ld_const = sem("ld_const")
        ld_rows = sem("ld_rows")
        zeros_first = sem("zeros_first")
        ld_masks = sem("ld_masks")
        ld_x = sem("ld_x")
        ld_b = sem("ld_b")
        ld_c = sem("ld_c")
        ld_d = sem("ld_d")
        ld_e = sem("ld_e")
        ld_moe = sem("ld_moe")
        bias_rows = sem("bias_rows")
        stored = sem("stored")
        memsets = sem("memsets")
        mrows = sem("mrows")
        prep_mm = sem("prep_mm")
        prep_act = sem("prep_act")
        prep_dve = sem("prep_dve")
        wstat_ready = sem("wstat_ready")
        wred_ready = sem("wred_ready")
        kt_ready = sem("kt_ready")
        prep_steps = sem("prep_steps")
        consts_ready = sem("consts_ready")
        ternary_ready = sem("ternary_ready")
        xb_ready = sem("xb_ready")
        kbd1_ready = sem("kbd1_ready")
        recip_ready = sem("recip_ready")
        norm_first = sem("norm_first")
        norm_second = sem("norm_second")
        quant_ready = sem("quant_ready")
        quantT_psum = sem("quantT_psum")
        quantT_ready = sem("quantT_ready")
        bit_out = sem("bit_out")
        hid_ready = sem("hid_ready")
        gelu_ready = sem("gelu_ready")
        fc_psum = sem("fc_psum")
        fc_gelu = sem("fc_gelu")
        pj_out = sem("pj_out")
        ctxb_ready = sem("ctxb_ready")
        kbd3_ready = sem("kbd3_ready")
        sx_psum = sem("sx_psum")
        sx_neg = sem("sx_neg")
        sx_exp = sem("sx_exp")
        sxT_psum = sem("sxT_psum")
        sxT_ready = sem("sxT_ready")
        sx_out = sem("sx_out")
        gate_psum = sem("gate_psum")
        gate_ready = sem("gate_ready")
        tanh_ready = sem("tanh_ready")
        qf_psum = sem("qf_psum")
        qf_ready = sem("qf_ready")
        kfa_ready = sem("kfa_ready")
        kfd_ready = sem("kfd_ready")
        wv_ready = sem("wv_ready")
        vmix_steps = sem("vmix_steps")
        v_first = sem("v_first")
        v_second = sem("v_second")
        ho_ready = sem("ho_ready")
        mo_ready = sem("mo_ready")
        mo_products = sem("mo_products")
        sf_psum = sem("sf_psum")
        nmf_ready = sem("nmf_ready")
        ef_ready = sem("ef_ready")
        pf_psum = sem("pf_psum")
        pf_ready = sem("pf_ready")
        pv_out = sem("pv_out")
        mix_ready = sem("mix_ready")
        mixT_psum = sem("mixT_psum")
        mixT_ready = sem("mixT_ready")
        swo_out = sem("swo_out")
        router_psum = sem("router_psum")
        rneg_ready = sem("rneg_ready")
        rexp_ready = sem("rexp_ready")
        up_psum = sem("up_psum")
        silu_in = sem("silu_in")
        t1_ready = sem("t1_ready")
        h_ready = sem("h_ready")
        y_psum = sem("y_psum")
        y_used = sem("y_used")
        out_ready = sem("out_ready")

        JOBS = ([("K0", c, "ad") for c in range(NC8)] + [("b0", 0, "d")]
                + [("M0", c, "da"[c % 2]) for c in range(2)] + [("b0T", 0, "a")]
                + [("M0", c, "da"[c % 2]) for c in range(2, NC8)]
                + [("V0", c, "ad") for c in range(NC8)] + [("VO", c, "da"[c % 2]) for c in range(NC8)]
                + [("K1", 0, "d"), ("V1", 0, "d"), ("K3", 0, "d"), ("V3", 0, "d"), ("Lfc", 0, "d"), ("Lpj", 0, "d")])
        JOB = {(k, c): n for n, (k, c, _) in enumerate(JOBS)}
        FIRST_JOBS = JOB["V0", 0]

        def job_bank(n):
            return ps[:, n % 8 if n < FIRST_JOBS else 4 + n % 4, :]

        def read_by(engine, n):
            return sum(engine in r for _, _, r in JOBS[:n + 1])

        def weave(order, front, other):
            for c in order:
                next(front if c == "F" else other, None)
            alone(front)
            alone(other)

        def alone(half):
            for _ in half:
                pass

        block = ctx.enter_context(nc.Block())

        @block.sync
        def _(sp):
            sp.dma_start(wa_sb[:, 0:1280], wa[:, 0:1280]).then_inc(ld_a, 16)
            sp.dma_start(cols_sb[:, :], cols).then_inc(ld_cols, 16)
            sp.dma_start(part(wa_sb, WA, "Wq"), part(wa, WA, "Wq")).then_inc(ld_wq, 16)
            sp.dma_start(const_sb[:, :], const).then_inc(ld_const, 16)
            sp.dma_start(xall[:, :, :], x.rearrange("(t p) d -> p t d", p=P)).then_inc(ld_x, 16)
            for name in ("WvT", "WoT"):
                sp.dma_start(part(wa_sb, WA, name), part(wa, WA, name)).then_inc(ld_wv, 16)
            sp.dma_start(wb_sb, wb).then_inc(ld_b, 16)
            sp.dma_start(rows_sb[:, :], rows.to_broadcast([P, 1152])).then_inc(ld_rows, 16)
            sp.dma_start(wc_sb[:, :], wc[:, 0:1280]).then_inc(ld_c, 16)
            sp.dma_start(ctxT2, wc[:, 1280:1792]).then_inc(ld_c, 16)
            sp.dma_start(wd_sb, wd).then_inc(ld_d, 16)
            sp.dma_start(lora_sb[:, 0:640], lora[:, 0:640]).then_inc(ld_d, 16)
            sp.dma_start(loraB_sb[:, 0:640], lora[:, 640:1280]).then_inc(ld_d, 16)
            sp.wait_ge(mrows, 1)
            for b in range(B):
                sp.dma_start(bias0[0:1, b, :].rearrange("p (n k) -> p n k", k=CTX),
                             m0row[:, b, :].unsqueeze(1).to_broadcast([1, 16, CTX])).then_inc(bias_rows, 16)
            sp.wait_ge(prep_act, read_by("a", JOB["b0T", 0]))
            for r in range(3):
                sp.dma_start(bias0[r + 1:r + 2, :, :].rearrange("p b (c k) -> p (b c) k", k=P),
                             bpT[32 * r:32 * r + 32, :]).then_inc(bias_rows, 16)
            sp.dma_start(we_sb[:, :], we).then_inc(ld_e, 16)
            sp.dma_start(wo2_sb[:, :, :], wo2[0:256, :].rearrange("(c p) d -> p c d", p=P)).then_inc(ld_e, 16)
            sp.dma_start(wo2b_sb[:, :], wo2[256:320, :]).then_inc(ld_e, 16)
            sp.dma_start(ctxT_sb[:, :, :], wa[:, 0:256].rearrange("p (b k) -> p b k", b=B)).then_inc(ld_e, 16)
            sp.dma_start(ctxn_sb[:, :, :], ctxn.rearrange("b k d -> k b d")).then_inc(ld_e, 16)
            sp.wait_ge(prep_mm, len(JOBS))
            sp.wait_ge(prep_dve, read_by("d", len(JOBS)))
            sp.dma_start(gu_sb[:, :, :], gateup).then_inc(ld_moe, 16)
            for c, (i0, m) in enumerate(CHUNKS):
                sp.dma_start(dn_sb[0:m, :, c, :], down[:, i0:i0 + m, :].rearrange("e i d -> i e d")).then_inc(ld_moe, 16)
            out_t = out.rearrange("(t p) d -> p t d", p=P)
            with sp.Fori(0, B) as i:
                sp.wait_ge(out_ready, i * 2 + 2)
                sp.dma_start(out_t[:, bass.ds(2 * i, 2), :], xall[:, bass.ds(2 * i, 2), :]).then_inc(stored, 16)
            sp.wait_ge(stored, 16 * B)

        @block.gpsimd
        def _(pool):
            pool.memset(KVbd[:, NC8 // 2:NC8, :, :], 0.0).then_inc(memsets, 1)
            pool.dma_start(m0w, mask0).then_inc(ld_masks, 16)
            pool.dma_start(m1i[:, :, :], mask1.rearrange("(t p) k -> p t k", p=P)).then_inc(ld_masks, 16)
            pool.dma_start(m2i[:, :, :], mask2).then_inc(ld_masks, 16)
            pool.memset(KFbd[:, :, :, :], 0.0).then_inc(memsets, 1)
            for v in Vbd[1:]:
                pool.memset(v[:, :, :, :], 0.0).then_inc(memsets, 1)
            pool.memset(mhalf[:, :], -0.5).then_inc(memsets, 1)
            pool.memset(ones_bf[:, :], 1.0).then_inc(memsets, 1)
            pool.wait_ge(ld_const, 16)
            pool.wait_ge(ld_rows, 16)
            pool.wait_ge(ld_x, 16)
            pool.wait_ge(memsets, 6)

            def power(h, n, which):
                yield
                pool.wait_ge(h.var_ready, n * h.n_pow + h.power[which] + 1)
                pool.tensor_tensor(h.rs[:, :], h.ve[:, :], mhalf[:, :], ALU.pow).then_inc(h.rstd_ready, 1)

            def add_bias(name, src):
                pool.tensor_tensor(XB[:, :, :], src,
                                   part(rows_sb, ROWS, name).unsqueeze(1).to_broadcast([P, TILES, D]),
                                   ALU.add).then_inc(xb_ready, 1)

            def small_keys(a, n, signal):
                pool.tensor_tensor(Kbd[a][:, :, :], KT[a][:, n, :].unsqueeze(1).to_broadcast([P, 16, CTX]),
                                   blockm.unsqueeze(2).to_broadcast([P, 16, CTX]), ALU.mult).then_inc(signal, 1)

            def prep():
                yield
                pool.wait_ge(wstat_ready, 1)
                pool.partition_all_reduce(wred[:, 0:2], wstat[:, 0:2], P, R_ADD).then_inc(wred_ready, 1)
                yield
                pool.wait_ge(wstat_ready, 2)
                pool.partition_all_reduce(wred[:, 2:4], wstat[:, 2:4], P, R_MAX).then_inc(wred_ready, 1)
                yield

            def front(n):
                yield from power(FR, n, 0)
                add_bias("bo0", xall[:, bass.ds(2 * n, 2), :])
                for s in range(TILES):
                    yield
                    pool.wait_ge(recip_ready, n * 2 + s + 1)
                    normalise(pool, s, 1).then_inc(norm_second, 1)
                yield from power(FR, n, 1)
                add_bias("b2", FR.X[:, :, :])
                yield from power(FR, n, "rms1")
                yield from power(FR, n, "rms2")
                yield from power(FR, n, 2)
                add_bias("bo1", FR.X[:, :, :])
                yield
                pool.wait_ge(kt_ready, 1)
                small_keys(1, n, kbd1_ready)
                yield from power(FR, n, 3)
                add_bias("bpj", FR.X[:, :, :])
                yield
                pool.wait_ge(ld_e, 80)
                pool.tensor_copy(ctxb[:, :], ctxn_sb[:, n, :]).then_inc(ctxb_ready, 1)
                yield from power(FR, n, 4)
                yield from power(FR, n, 5)

            def back(n):
                yield
                pool.wait_ge(wv_ready, n * 2 + 1)
                pr4 = prod.rearrange("p (e h k) -> p e h k", e=E2X, k=DH2)
                for e in range(E2X):
                    ins = pool.tensor_tensor(
                        pr4[:, e, :, :], XG[:, 0, e * DH2:(e + 1) * DH2].unsqueeze(1).to_broadcast([P, H2, DH2]),
                        wv[:, 0, :, e].unsqueeze(2).to_broadcast([P, H2, DH2]), ALU.mult)
                ins.then_inc(vmix_steps, 1)
                yield
                pool.wait_ge(vmix_steps, n * 3 + 1)
                pool.tensor_tensor(prod[:, 0:1024], prod[:, 0:1024], prod[:, 1024:2048], ALU.add).then_inc(vmix_steps, 1)
                yield
                pool.wait_ge(vmix_steps, n * 3 + 2)
                pool.tensor_tensor(prod[:, 0:512], prod[:, 0:512], prod[:, 512:1024], ALU.add).then_inc(vmix_steps, 1)
                yield
                pool.wait_ge(vmix_steps, n * 3 + 3)
                pool.tensor_tensor(V[:, 0, :], prod[:, 0:512], prod[:, 2048:2560], ALU.add).then_inc(v_first, 1)
                yield
                small_keys(2, n, kbd3_ready)
                for s in range(TILES):
                    yield
                    if s:
                        pool.wait_ge(mix_ready, n * 2 + s)
                    pool.wait_ge(mo_ready, n * 2 + s + 1)
                    pool.wait_ge(ho_ready, n * 2 + s + 1)
                    for h in range(H2 - POOL_HEADS, H2):
                        ins = mo_product(pool, s, h)
                    ins.then_inc(mo_products, 1)
                    for k, h in enumerate(range(H2 - POOL_HEADS + 1, H2)):
                        yield
                        pool.wait_ge(mo_products, (n * 2 + s) * POOL_HEADS + k + 1)
                        a = prod[:, XV * (H2 - POOL_HEADS):XV * (H2 - POOL_HEADS + 1)]
                        pool.tensor_tensor(a, a, prod[:, XV * h:XV * h + XV], ALU.add).then_inc(mo_products, 1)
                yield from power(BA, n, 6)
                yield from power(BA, n, 7)
                for e in range(E3):
                    for u in range(3 * e, 3 * e + 3):
                        m = CHUNKS[u % 3][1]
                        yield
                        pool.wait_ge(t1_ready, n * UNITS + u + 1)
                        pool.tensor_tensor(HT[0:m, u % RING, :], T1[0:m, u % RING, :], UC[0:m, u % RING, :],
                                           ALU.mult).then_inc(h_ready, 1)
                pool.wait_ge(h_ready, n * UNITS + UNITS)

            weave(OPENING["pool"], front(0), prep())
            pool.wait_ge(kt_ready, 2)
            with pool.Fori(1, B) as i:
                weave(WEAVE["pool"], front(i), back(i - 1))
            alone(back(B - 1))

        @block.scalar
        def _(act):
            def copy(out_ap, in_ap):
                return act.activation(out_ap, in_ap, ACT.Copy)

            act.wait_ge(ld_cols, 16)
            act.wait_ge(memsets, 1)
            act.wait_ge(zeros_first, 1)

            def read_job(n):
                kind, c, readers = JOBS[n]
                act.wait_ge(prep_mm, n + 1)
                bank = job_bank(n)
                if kind in ("K0", "V0"):
                    bias = "bk0" if kind == "K0" else "bv0"
                    ins = act.activation(KVbd[0:64, c, :, 0:CTX], bank[0:64, 0:256].rearrange("p (b k) -> p b k", b=B),
                                         ACT.Identity, bias=part(cols_sb, COLS, bias)[0:64, c:c + 1])
                elif kind in ("M0", "VO"):
                    ins = copy((M0 if kind == "M0" else VO0)[:, :, c, :], bank.rearrange("p (b k) -> p b k", b=B))
                else:
                    ins = copy(bpT[:, :], bank.bitcast(BF16)[0:96, 0:P])
                ins.then_inc(prep_act, 1)

            for n in range(FIRST_JOBS):
                if "a" in JOBS[n][2]:
                    read_job(n)

            def x_transposed(h, n, l):
                k = TILES * h.norms.index(l)
                for s in range(TILES):
                    yield
                    act.wait_ge(h.xT_psum, n * h.n_xt + k + s + 1)
                    copy(h.XT[:, s * P:(s + 1) * P], h.Bk(s)[:, 0:P]).then_inc(h.xT_ready, 1)

            def exps(hf, n, E, a, k0, per):
                for s in range(TILES):
                    for h in range(2):
                        yield
                        act.wait_ge(hf.shifted, n * per + k0 + 2 * s + h + 1)
                        e = E[:, s, 512 * h:512 * h + 512]
                        act.activation(e, e, ACT.Exp, scale=SCALES[a]).then_inc(hf.exp_ready, 1)

            def probs_transposed(hf, n, E, k0, per):
                for s in range(TILES):
                    for h in range(2):
                        yield
                        act.wait_ge(hf.pT_psum, n * per + k0 + 2 * s + h + 1)
                        copy(E[:, s, 512 * h:512 * h + 512], hf.bank(s, h)).then_inc(hf.pT_ready, 1)

            def heads_transposed(h, n):
                for s in range(TILES):
                    yield
                    act.wait_ge(h.headsT_psum, n * 2 + s + 1)
                    copy(h.AOT[:, s, :], h.Bk(s)[:, 0:P]).then_inc(h.headsT_ready, 1)

            def prep():
                for n in range(FIRST_JOBS, len(JOBS)):
                    if "a" in JOBS[n][2]:
                        yield
                        read_job(n)

            def front(n):
                yield from x_transposed(FR, n, 0)
                yield from exps(FR, n, E1, 0, 0, 8)
                yield from probs_transposed(FR, n, E1, 0, 8)
                for s in range(TILES):
                    yield
                    act.wait_ge(quantT_psum, n * 4 + s + 1)
                    copy(qTbf[:, s, 0:P], FR.Bk(s).bitcast(BF16)[:, 0:P]).then_inc(quantT_ready, 1)
                for s in range(TILES):
                    yield
                    act.wait_ge(hid_ready, n * 2 + s + 1)
                    act.activation(E1[:, s, 512:1024], E1[:, s, 0:512], ACT.Gelu).then_inc(gelu_ready, 1)
                for s in range(TILES):
                    yield
                    act.wait_ge(quantT_psum, n * 4 + 2 + s + 1)
                    copy(qTbf[:, s, :], FR.Bk(s).bitcast(BF16)[:, 0:FF]).then_inc(quantT_ready, 1)
                yield from x_transposed(FR, n, 2)
                yield
                act.wait_ge(FR.qT_psum, n + 1)
                act.activation(FR.QT[:, :], FR.A(0)[:, 0:256], ACT.Identity,
                               bias=part(cols_sb, COLS, "bq1")).then_inc(FR.qT_ready, 1)
                yield from exps(FR, n, E1, 1, 4, 8)
                yield from probs_transposed(FR, n, E1, 4, 8)
                yield from heads_transposed(FR, n)
                yield from x_transposed(FR, n, 3)
                for c in range(FF // P):
                    yield
                    act.wait_ge(fc_psum, n * 4 + c + 1)
                    act.activation(GT[:, c, :], FR.banks[c][:, 0:256], ACT.Gelu,
                                   bias=part(cols_sb, COLS, "bfc")[:, c:c + 1]).then_inc(fc_gelu, 1)
                yield from x_transposed(FR, n, 4)
                for s in range(TILES):
                    yield
                    act.wait_ge(sx_neg, n * 2 + s + 1)
                    act.activation(E1[:, s, 0:CTX], FR.A(s)[:, 0:CTX], ACT.Exp, bias=FR.mxc[:, s, 0:1], scale=SCALE_L2X,
                                   accum_out=FR.sm[:, s, 0:1]).then_inc(sx_exp, 1)
                for s in range(TILES):
                    yield
                    act.wait_ge(sxT_psum, n * 2 + s + 1)
                    copy(E1[0:CTX, s, P:2 * P], FR.Bk(s)[0:CTX, 0:P]).then_inc(sxT_ready, 1)
                yield from x_transposed(FR, n, 5)
                for s in range(TILES):
                    yield
                    act.wait_ge(gate_psum, n * 2 + s + 1)
                    copy(XG[:, s, :], FR.A(s)[:, 0:400]).then_inc(gate_ready, 1)
                for s in range(TILES):
                    yield
                    act.wait_ge(gate_ready, n * 2 + s + 1)
                    act.activation(th[:, s, :], XG[:, s, XV:XV + 40], ACT.Tanh, scale=0.5).then_inc(tanh_ready, 1)
                for c in range(2):
                    yield
                    act.wait_ge(qf_psum, n * 4 + c + 1)
                    copy(QF[:, 2 * c:2 * c + 2, :].rearrange("p a b -> p (a b)"), FR.Bk(c)).then_inc(qf_ready, 1)
                for c in range(2):
                    yield
                    act.wait_ge(qf_psum, n * 4 + 2 + c + 1)
                    copy(KFbd[0:64, 2 * c:2 * c + 2, 0, :], FR.A(c)[0:64, :].rearrange("p (c k) -> p c k", c=2)).then_inc(
                        kfa_ready, 1)

            def back(n):
                def heads_copied(s):
                    yield
                    act.wait_ge(pv_out, n * 2 + s + 1)
                    copy(HO[:, s, :], heads_out(s)).then_inc(ho_ready, 1)

                for k in range(HEAD_UNITS + 3):
                    if k == HEAD_UNITS + 2:
                        yield from heads_copied(0)
                    if k >= 3:
                        j = k - 3
                        yield
                        act.wait_ge(pf_psum, n * HEAD_UNITS + j + 1)
                        copy(EF[:, j // 4, 2 * (j % 4):2 * (j % 4) + 2, :].rearrange("p h q -> p (h q)"),
                             head_bank(j)).then_inc(pf_ready, 1)
                    if 1 <= k <= HEAD_UNITS:
                        j = k - 1
                        s, c = divmod(j, 4)
                        yield
                        act.wait_ge(nmf_ready, n * HEAD_UNITS + j + 1)
                        for g in range(2):
                            h = 2 * c + g
                            act.activation(EF[:, s, h, :], head_bank(j)[:, g * S:(g + 1) * S], ACT.Exp,
                                           bias=nmf[:, s, h:h + 1], scale=SCALE_L2F,
                                           accum_out=smf[:, s, h:h + 1]).then_inc(ef_ready, 1)
                yield from heads_copied(1)
                for s in range(TILES):
                    yield
                    act.wait_ge(mixT_psum, n * 2 + s + 1)
                    copy(AT[:, s, 0:2, :].rearrange("p a b -> p (a b)"), mix_bank(s)[:, 0:256])
                    copy(AT[0:64, s, 2, :], mix_bank(s)[0:64, 256:384]).then_inc(mixT_ready, 1)
                yield from x_transposed(BA, n, 6)
                yield from exps(BA, n, E2, 2, 0, 4)
                yield from probs_transposed(BA, n, E2, 0, 4)
                yield from heads_transposed(BA, n)
                yield from x_transposed(BA, n, 7)
                for s in range(TILES):
                    yield
                    act.wait_ge(rneg_ready, n + 1)
                    act.activation(pr[:, s, :], router_out(s), ACT.Exp, bias=rmx[:, s, 1:2],
                                   accum_out=rmx[:, s, 2:3]).then_inc(rexp_ready, 1)
                for e in range(E3):
                    for u in range(3 * e, 3 * e + 3):
                        m = CHUNKS[u % 3][1]
                        yield
                        act.wait_ge(up_psum, n * UNITS + u + 1)
                        act.activation(TH[0:m, u % RING, :], up_bank(u)[0:m, 0:256], ACT.Tanh, scale=0.5)
                        copy(UC[0:m, u % RING, :], up_bank(u)[0:m, 256:512]).then_inc(silu_in, 1)

            weave(OPENING["act"], front(0), prep())
            with act.Fori(1, B) as i:
                weave(WEAVE["act"], front(i), back(i - 1))
            alone(back(B - 1))

        @block.vector
        def _(dve):
            steps = [0]
            pads = iter(range(32))

            def pad():
                k = next(pads)
                return filler[:, k:k + 1]

            def count_prep(ins):
                steps[0] += 1
                ins.then_inc(prep_steps, 1)

            def settle_prep():
                dve.wait_ge(prep_steps, steps[0])

            def masks():
                dve.wait_ge(ld_masks, 48)
                count_prep(dve.tensor_scalar(m0row[:, :, :], m0w.bitcast(U8).rearrange("p (b k) -> p b k", b=B),
                                             MASKED, None, ALU.mult))
                for dst, src in ((mneg1, m1i), (mneg2, m2i)):
                    dve.tensor_scalar(dst[:, :, :], src[:, :, :], 0.0, MASKED, ALU.is_equal,
                                      ALU.mult).then_inc(consts_ready, 1)
                settle_prep()
                dve.tensor_copy(pad()[0:1, :], m0row[0:1, 0, 0:1]).then_inc(mrows, 1)
                dve.wait_ge(ld_const, 16)
                dve.tensor_copy(ident_bf[:, :], ident).then_inc(consts_ready, 1)

            def weight_stats():
                dve.wait_ge(ld_b, 16)
                for n in range(2):
                    count_prep(dve.tensor_reduce(wstat[:, n:n + 1], wb_sb[:, 512 * n:512 * n + 512], X_AXIS, ALU.add,
                                                 apply_absolute_value=True))
                settle_prep()
                dve.tensor_copy(pad(), wstat[:, 0:1]).then_inc(wstat_ready, 1)
                dve.wait_ge(ld_d, 48)
                for n in range(2):
                    count_prep(dve.tensor_reduce(wstat[:, 2 + n:3 + n], wd_sb[:, 512 * n:512 * n + 512], X_AXIS, ALU.max,
                                                 apply_absolute_value=True))
                settle_prep()
                dve.tensor_copy(pad(), wstat[:, 2:3]).then_inc(wstat_ready, 1)

            def ternary_weights():
                dve.wait_ge(wred_ready, 1)
                count_prep(dve.tensor_scalar(wmean[:, :], wred[:, 0:2], 1.0 / (D * FF), 1e-5, ALU.mult, ALU.max))
                settle_prep()
                count_prep(dve.reciprocal(wsc[:, 0:2], wmean[:, :]))
                settle_prep()
                for n in range(2):
                    count_prep(dve.tensor_scalar(wtmp[:, 512 * n:512 * n + 512], wb_sb[:, 512 * n:512 * n + 512],
                                                 wsc[:, n:n + 1], ROUND, ALU.mult, ALU.add))
                settle_prep()
                count_prep(dve.tensor_scalar(wtmp2, wtmp, ROUND, -1.0, ALU.subtract, ALU.max))
                settle_prep()
                dve.tensor_scalar(w1q[:, :], wtmp2[:, 0:512], 1.0, None, ALU.min).then_inc(ternary_ready, 1)
                dve.tensor_scalar(w2q[:, :, :].rearrange("p c d -> p (c d)"), wtmp2[:, 512:1024], 1.0, None,
                                  ALU.min).then_inc(ternary_ready, 1)

            def int8_weights():
                dve.wait_ge(wred_ready, 2)
                count_prep(dve.tensor_scalar(wsc[:, 0:2], wred[:, 2:4], 1.0 / QMAX, None, ALU.mult))
                settle_prep()
                count_prep(dve.reciprocal(wsc[:, 2:4], wsc[:, 0:2]))
                settle_prep()
                dve.wait_ge(ternary_ready, 2)
                for n in range(2):
                    count_prep(dve.tensor_scalar(wtmp[:, 512 * n:512 * n + 512], wd_sb[:, 512 * n:512 * n + 512],
                                                 wsc[:, 2 + n:3 + n], ROUND, ALU.mult, ALU.add))
                settle_prep()
                for n in range(2):
                    count_prep(dve.tensor_scalar(wtmp2[:, 512 * n:512 * n + 512], wtmp[:, 512 * n:512 * n + 512], ROUND,
                                                 wsc[:, n:n + 1], ALU.subtract, ALU.mult))
                settle_prep()

            def read_job(n):
                kind, c, readers = JOBS[n]
                dve.wait_ge(prep_mm, n + 1)
                bank = job_bank(n)
                if kind in ("K0", "V0"):
                    bias = "bk0" if kind == "K0" else "bv0"
                    ins = dve.tensor_scalar(KVbd[64:128, c, :, CTX:P], bank[64:128, 0:256].rearrange("p (b k) -> p b k", b=B),
                                            part(cols_sb, COLS, bias)[64:128, c:c + 1], None, ALU.add)
                elif kind in ("M0", "VO"):
                    ins = dve.tensor_copy((M0 if kind == "M0" else VO0)[:, :, c, :],
                                          bank.rearrange("p (b k) -> p b k", b=B))
                elif kind == "b0":
                    v, r1, r2 = bank[:, 0:32], bres[:, 0, :], bres[:, 1, :]
                    hi, mid, lo = (bpart[:, r, :, :].rearrange("p b c -> p (b c)") for r in range(3))
                    count_prep(dve.tensor_copy(hi, v))
                    settle_prep()
                    count_prep(dve.tensor_tensor(r1, v, hi, ALU.subtract))
                    settle_prep()
                    count_prep(dve.tensor_copy(mid, r1))
                    settle_prep()
                    count_prep(dve.tensor_tensor(r2, r1, mid, ALU.subtract))
                    settle_prep()
                    ins = dve.tensor_copy(lo, r2)
                elif kind == "K1":
                    ins = dve.tensor_scalar(KT1, bank[:, 0:256], part(cols_sb, COLS, "bk1"), None, ALU.add)
                elif kind == "K3":
                    for src, dst, tab in ((bank[:, 0:256], KT3a, cosT), (bank[:, 256:512], KT3b, sinT)):
                        count_prep(dve.tensor_tensor(dst.rearrange("p (b k) -> p b k", b=B),
                                                     src.rearrange("p (b k) -> p b k", b=B),
                                                     tab[:, 0:CTX].unsqueeze(1).to_broadcast([P, B, CTX]), ALU.mult))
                    settle_prep()
                    ins = dve.tensor_tensor(KT3, KT3a, KT3b, ALU.add)
                elif kind in ("V1", "V3"):
                    dst = Vbd[1] if kind == "V1" else Vbd[2]
                    v = bank.rearrange("p (b c q d) -> p b c q d", b=B, c=NC8, q=2)
                    bv = part(rows_sb, ROWS, "bv1").rearrange("p (c q d) -> p c q d", q=2, d=8)
                    for q in range(2):
                        rows_q = slice(64 * q, 64 * q + 64)
                        for b in range(B):
                            o = dst[rows_q, b, :, 8 * q:8 * q + 8]
                            if kind == "V1":
                                ins = dve.tensor_tensor(o, v[rows_q, b, :, q, :], bv[rows_q, :, q, :], ALU.add)
                            else:
                                ins = dve.tensor_copy(o, v[rows_q, b, :, q, :])
                            if (q, b) != (1, B - 1):
                                count_prep(ins)
                elif kind == "Lfc":
                    ins = dve.scalar_tensor_tensor(wfc[:, :], bank, LORA_SCALE, wtmp2[:, 0:512], ALU.mult, ALU.add)
                elif kind == "Lpj":
                    ins = dve.scalar_tensor_tensor(wpj[:, :, :].rearrange("p c d -> p (c d)"), bank, LORA_SCALE,
                                                   wtmp2[:, 512:1024], ALU.mult, ALU.add)
                ins.then_inc(prep_dve, 1)
                if kind in ("K1", "K3"):
                    dve.wait_ge(prep_dve, read_by("d", n))
                    dve.tensor_copy(pad(), (KT1 if kind == "K1" else KT3)[:, 0:1]).then_inc(kt_ready, 1)

            dve.memset(KVbd[:, 0:NC8 // 2, :, :], 0.0).then_inc(zeros_first, 1)
            dve.wait_ge(ld_cols, 16)
            dve.wait_ge(memsets, 1)
            dve.wait_ge(zeros_first, 1)
            for n in range(FIRST_JOBS):
                if n == JOB["M0", 0]:
                    masks()
                if "d" in JOBS[n][2]:
                    read_job(n)
            dve.wait_ge(ld_rows, 16)
            dve.wait_ge(ld_x, 16)

            def prep():
                yield
                weight_stats()
                for n in range(FIRST_JOBS, JOB["K1", 0]):
                    if "d" in JOBS[n][2]:
                        yield
                        read_job(n)
                    if n == JOB["VO", 0]:
                        yield
                        ternary_weights()
                dve.wait_ge(memsets, 6)
                for v in Vbd[1:]:
                    count_prep(dve.memset(v[0:64, :, :, 16:17], 1.0))
                    count_prep(dve.memset(v[64:128, :, :, 17:18], 1.0))
                for kind in ("K1", "V1", "K3", "V3"):
                    yield
                    read_job(JOB[kind, 0])
                yield
                int8_weights()
                for kind in ("Lfc", "Lpj"):
                    yield
                    read_job(JOB[kind, 0])

            class Steps:

                def __init__(self, h, n, per):
                    self.h, self.n, self.per, self.count = h, n, per, 0

                def step(self, ins):
                    self.count += 1
                    ins.then_inc(self.h.dve_seq, 1)
                    return self.count

                def settle(self, mark=None):
                    dve.wait_ge(self.h.dve_seq, self.n * self.per + (self.count if mark is None else mark))

            def stats(c, src):
                h = c.h
                for s in range(TILES):
                    c.step(dve.bn_stats(h.st[:, s, :], src(s)))
                c.settle()
                c.step(dve.tensor_copy(h.pad[:, :], ident[:, 0:1]))
                for s in range(TILES):
                    c.step(dve.bn_aggr(h.mv[:, s, :], h.st[:, s, :]))
                c.settle()

            def layer_norm(c, l, src, sink=True):
                h, n = c.h, c.n
                stats(c, src)
                dve.tensor_scalar(h.ve[:, :], h.mv[:, :, 1], EPS, None, ALU.add).then_inc(h.var_ready, 1)
                yield
                dve.wait_ge(h.rstd_ready, n * h.n_pow + h.power[l] + 1)
                for s in range(TILES):
                    ins = dve.tensor_scalar(h.XH[:, s, :], src(s), h.mv[:, s, 0:1], h.rs[:, s:s + 1],
                                            ALU.subtract, ALU.mult)
                    if sink:
                        ins.then_inc(h.xhat_ready, 1)
                    else:
                        c.step(ins)

            def softmax(c, E, a, k0, per):
                hf, n = c.h, c.n
                top = hf.mx if CLAMPS[a] is None else hf.mxc
                for s in range(TILES):
                    for h in range(2):
                        yield
                        dve.wait_ge(hf.scores_ready, n * per + k0 + 2 * s + h + 1)
                        c.step(dve.tensor_reduce(hf.mx[:, s, 8 * h:8 * h + 8],
                                                 hf.bank(s, h).rearrange("p (n k) -> p n k", k=CTX), X_AXIS, ALU.max))
                    if CLAMPS[a] is not None:
                        c.settle()
                        c.step(dve.tensor_scalar(hf.mxc[:, s, :], hf.mx[:, s, :], CLAMPS[a], None, ALU.max))
                    c.settle()
                    for h in range(2):
                        sc = hf.bank(s, h).rearrange("p (n k) -> p n k", k=CTX)
                        e = E[:, s, 512 * h:512 * h + 512].rearrange("p (n k) -> p n k", k=CTX)
                        m = top[:, s, 8 * h:8 * h + 8].unsqueeze(2).to_broadcast([P, 8, CTX])
                        if CLAMPS[a] is not None:
                            ins = dve.scalar_tensor_tensor(e, sc, CLAMPS[a], m, ALU.max, ALU.subtract)
                        else:
                            ins = dve.tensor_tensor(e, sc, m, ALU.subtract)
                        ins.then_inc(hf.shifted, 1)

            def head_norms(c, a, k0, per):
                h, n = c.h, c.n
                marks = []
                for s in range(TILES):
                    yield
                    dve.wait_ge(h.attn_out, n * per + k0 + s + 1)
                    o = h.A(s)[:, 0:144].rearrange("p (c v) -> p c v", v=18)
                    marks.append(c.step(dve.reciprocal(h.rc[:, s, :].rearrange("p (c q) -> p c q", q=2), o[:, :, 16:18])))
                for s in range(TILES):
                    c.settle(marks[s])
                    o = h.A(s)[:, 0:144].rearrange("p (c v) -> p c v", v=18)[:, :, 0:16].rearrange(
                        "p c (q d) -> p c q d", q=2)
                    r = h.rc[:, s, :].rearrange("p (c q) -> p c q", q=2).unsqueeze(3).to_broadcast([P, 8, 2, 8])
                    dve.tensor_tensor(h.AO[:, s, :].rearrange("p (c q d) -> p c q d", q=2, d=8), o, r,
                                      ALU.mult).then_inc(h.heads_ready, 1)

            def beats(c, dst, g, n):
                groups = g.shape[1]
                for f in range(n):
                    pick = g[:, :, f:f + 1]
                    c.step(dve.tensor_tensor(dst[:, :, 0:f + 1, f], pick.to_broadcast([P, groups, f + 1]),
                                             g[:, :, 0:f + 1], ALU.is_gt))
                    if f < n - 1:
                        c.step(dve.tensor_tensor(dst[:, :, f + 1:n, f], pick.to_broadcast([P, groups, n - 1 - f]),
                                                 g[:, :, f + 1:n], ALU.is_ge))

            def rms_quant(c, which, ms_src, src, width, weight):
                h, n = c.h, c.n
                amax, am, ra, s1, deq = (q_small[:, k, :] for k in range(1, 6))
                ms_src()
                for s in range(TILES):
                    c.step(dve.tensor_reduce(amax[:, s:s + 1], src(s), X_AXIS, ALU.max, apply_absolute_value=True))
                c.settle()
                yield
                dve.wait_ge(h.rstd_ready, n * h.n_pow + h.power[which] + 1)
                c.step(dve.tensor_tensor(am, amax, h.rs[:, :], ALU.mult))
                c.settle()
                c.step(dve.tensor_scalar(am, am, 1e-5, None, ALU.max))
                c.settle()
                c.step(dve.reciprocal(ra, am))
                c.step(dve.tensor_scalar(deq, am, 1.0 / QMAX, wmean[:, weight:weight + 1], ALU.mult, ALU.mult))
                c.settle()
                c.step(dve.scalar_tensor_tensor(s1, ra, QMAX, h.rs[:, :], ALU.mult, ALU.mult))
                c.settle()
                for s in range(TILES):
                    c.step(dve.tensor_scalar(E1[:, s, 0:width], src(s), s1[:, s:s + 1], ROUND, ALU.mult, ALU.add))
                c.settle()
                for s in range(TILES):
                    dve.tensor_scalar(qbf[:, s, 0:width], E1[:, s, 0:width], ROUND, None,
                                      ALU.subtract).then_inc(quant_ready, 1)
                return deq

            def front(n):
                c = Steps(FR, n, F_STEPS)
                X = FR.X
                yield from layer_norm(c, 0, lambda s: xall[:, 2 * n + s, :])
                yield from softmax(c, E1, 0, 0, 8)
                for s in range(TILES):
                    for h in range(2):
                        yield
                        dve.wait_ge(FR.exp_ready, n * 8 + 2 * s + h + 1)
                        c.step(dve.tensor_reduce(FR.sm[:, s, 8 * h:8 * h + 8],
                                                 E1[:, s, 512 * h:512 * h + 512].rearrange("p (n k) -> p n k", k=CTX),
                                                 X_AXIS, ALU.add))
                    c.settle()
                    dve.reciprocal(FR.rc[:, s, :], FR.sm[:, s, :]).then_inc(recip_ready, 1)
                    dve.wait_ge(recip_ready, n * 2 + s + 1)
                    normalise(dve, s, 0).then_inc(norm_first, 1)
                yield
                dve.wait_ge(xb_ready, n * 4 + 1)
                for s in range(TILES):
                    if s:
                        yield
                    dve.wait_ge(FR.attn_out, n * 4 + s + 1)
                    c.step(dve.tensor_tensor(X[:, s, :], FR.A(s)[:, 0:D], XB[:, s, :], ALU.add))
                c.settle()
                yield from layer_norm(c, 1, lambda s: X[:, s, :], sink=False)
                c.settle()

                def ms_of_xhat():
                    t = q_small[:, 6, :]
                    c.step(dve.tensor_tensor(t, FR.rs[:, :], FR.rs[:, :], ALU.mult))
                    c.settle()
                    c.step(dve.tensor_tensor(t, t, FR.mv[:, :, 1], ALU.mult))
                    c.settle()
                    dve.tensor_scalar(FR.ve[:, :], t, RMS_EPS, None, ALU.add).then_inc(FR.var_ready, 1)

                deq = yield from rms_quant(c, "rms1", ms_of_xhat, lambda s: FR.XH[:, s, :], D, 0)
                for s in range(TILES):
                    yield
                    dve.wait_ge(bit_out, n * 4 + s + 1)
                    dve.scalar_tensor_tensor(E1[:, s, 0:512], FR.A(s), deq[:, s:s + 1], part(rows_sb, ROWS, "b1"),
                                             ALU.mult, ALU.add).then_inc(hid_ready, 1)

                def ms_of_hidden():
                    stats(c, lambda s: E1[:, s, 512:1024])
                    t = q_small[:, 6, :]
                    c.step(dve.tensor_tensor(t, FR.mv[:, :, 0], FR.mv[:, :, 0], ALU.mult))
                    c.settle()
                    c.step(dve.tensor_tensor(t, t, FR.mv[:, :, 1], ALU.add))
                    c.settle()
                    dve.tensor_scalar(FR.ve[:, :], t, RMS_EPS, None, ALU.add).then_inc(FR.var_ready, 1)

                yield
                dve.wait_ge(gelu_ready, n * 2 + 2)
                deq = yield from rms_quant(c, "rms2", ms_of_hidden, lambda s: E1[:, s, 512:1024], FF, 1)
                yield
                dve.wait_ge(xb_ready, n * 4 + 2)
                for s in range(TILES):
                    if s:
                        yield
                    dve.wait_ge(bit_out, n * 4 + 2 + s + 1)
                    c.step(dve.scalar_tensor_tensor(X[:, s, :], FR.A(s)[:, 0:D], deq[:, s:s + 1], XB[:, s, :],
                                                    ALU.mult, ALU.add))
                c.settle()
                yield from layer_norm(c, 2, lambda s: X[:, s, :])
                yield from softmax(c, E1, 1, 4, 8)
                yield from head_norms(c, 1, 2, 4)
                yield
                dve.wait_ge(xb_ready, n * 4 + 3)
                for s in range(TILES):
                    if s:
                        yield
                    dve.wait_ge(FR.proj_out, n * 2 + s + 1)
                    c.step(dve.tensor_tensor(X[:, s, :], FR.A(s)[:, 256:384], XB[:, s, :], ALU.add))
                c.settle()
                yield from layer_norm(c, 3, lambda s: X[:, s, :])
                yield
                dve.wait_ge(xb_ready, n * 4 + 4)
                for s in range(TILES):
                    if s:
                        yield
                    dve.wait_ge(pj_out, n * 2 + s + 1)
                    c.step(dve.tensor_tensor(X[:, s, :], FR.A(s)[:, 0:D], XB[:, s, :], ALU.add))
                c.settle()
                yield from layer_norm(c, 4, lambda s: X[:, s, :])
                for s in range(TILES):
                    yield
                    dve.wait_ge(sx_psum, n * 2 + s + 1)
                    c.step(dve.tensor_reduce(FR.mx[:, s, 0:1], FR.A(s)[:, 0:CTX], X_AXIS, ALU.max))
                    c.settle()
                    dve.tensor_scalar(FR.mxc[:, s, 0:1], FR.mx[:, s, 0:1], -SCALE_L2X, None, ALU.mult).then_inc(sx_neg, 1)
                yield
                dve.wait_ge(sx_exp, n * 2 + 2)
                c.step(dve.reciprocal(FR.rc[:, :, 0], FR.sm[:, :, 0]))
                c.settle()
                for s in range(TILES):
                    yield
                    dve.wait_ge(sx_out, n * 2 + s + 1)
                    c.step(dve.scalar_tensor_tensor(hand[:, s, :], FR.A(s)[:, 128:256], FR.rc[:, s, 0:1], X[:, s, :],
                                                    ALU.mult, ALU.add))
                c.settle()
                yield from layer_norm(c, 5, lambda s: hand[:, s, :])
                chosen = cnt[:, :, :].rearrange("p (t g) e -> p t g e", t=TILES)
                for s in range(TILES):
                    group = slice(s * G2, (s + 1) * G2)
                    yield
                    dve.wait_ge(gate_ready, n * 2 + s + 1)
                    beats(c, cmp[:, group, :, :], XG[:, s, XV:].rearrange("p (g e) -> p g e", e=E2X), E2X)
                    c.settle()
                    c.step(dve.tensor_reduce(cnt[:, group, :], cmp[:, group, :, :], X_AXIS, ALU.add))
                    yield
                    dve.wait_ge(tanh_ready, n * 2 + s + 1)
                    c.step(dve.tensor_scalar(th[:, s, :], th[:, s, :], 0.5, 0.5, ALU.mult, ALU.add))
                    c.settle()
                    dve.scalar_tensor_tensor(wv[:, s, :, :], chosen[:, s, 0:H2, :], SEL - 0.5,
                                             th[:, s, :].rearrange("p (h e) -> p h e", e=E2X),
                                             ALU.is_lt, ALU.mult).then_inc(wv_ready, 1)
                for cc in range(2):
                    yield
                    dve.wait_ge(qf_psum, n * 4 + 2 + cc + 1)
                    dve.tensor_copy(KFbd[64:128, 2 * cc:2 * cc + 2, 1, :],
                                    FR.A(cc)[64:128, :].rearrange("p (c k) -> p c k", c=2)).then_inc(kfd_ready, 1)
                assert c.count == F_STEPS, f"F_STEPS = {c.count}"

            def back(n):
                c = Steps(BA, n, B_STEPS)
                X = BA.X
                yield
                chosen = cnt[:, :, :].rearrange("p (t g) e -> p t g e", t=TILES)
                yield
                dve.wait_ge(FR.dve_seq, n * F_STEPS + F_STEPS)

                def second_values(part):
                    half, e = divmod(part, E2X)
                    if part == 0:
                        dve.wait_ge(wv_ready, n * 2 + 2)
                    elif e:
                        c.settle()
                    for h in range(4 * half, 4 * half + 4):
                        v = V[:, 1, h * DH2:(h + 1) * DH2]
                        xv = XG[:, 1, e * DH2:(e + 1) * DH2]
                        if e == 0:
                            ins = dve.tensor_scalar(v, xv, wv[:, 1, h, e:e + 1], None, ALU.mult)
                        else:
                            ins = dve.scalar_tensor_tensor(v, xv, wv[:, 1, h, e:e + 1], v, ALU.mult, ALU.add)
                        if part < 2 * E2X - 1 or h < H2 - 1:
                            c.step(ins)
                    if part == 2 * E2X - 1:
                        ins.then_inc(v_second, 1)

                for k in range(HEAD_UNITS):
                    s, cc = divmod(k, 4)
                    yield
                    dve.wait_ge(sf_psum, n * HEAD_UNITS + k + 1)
                    c.step(dve.tensor_reduce(mxf[:, s, 2 * cc:2 * cc + 2], head_bank(k).rearrange("p (h k) -> p h k", h=2),
                                             X_AXIS, ALU.max))
                    c.settle()
                    dve.tensor_scalar(nmf[:, s, 2 * cc:2 * cc + 2], mxf[:, s, 2 * cc:2 * cc + 2], -SCALE_L2F, None,
                                      ALU.mult).then_inc(nmf_ready, 1)
                    if k < E2X:
                        second_values(2 * k)
                        second_values(2 * k + 1)
                for s in range(TILES):
                    yield
                    dve.wait_ge(ef_ready, n * 16 + 8 * s + 8)
                    c.step(dve.reciprocal(rcf[:, s, :], smf[:, s, :]))
                    c.settle()
                    dve.scalar_tensor_tensor(mo[:, s, :, :], chosen[:, s, H2:G2, :], SEL - 0.5,
                                             rcf[:, s, :].unsqueeze(2).to_broadcast([P, H2, E2X]),
                                             ALU.is_lt, ALU.mult).then_inc(mo_ready, 1)
                for s in range(TILES):
                    yield
                    dve.wait_ge(ho_ready, n * 2 + s + 1)
                    if s:
                        dve.wait_ge(mix_ready, n * 2 + s)
                    dve.wait_ge(mo_ready, n * 2 + s + 1)
                    for h in range(H2 - POOL_HEADS):
                        c.step(mo_product(dve, s, h))
                    c.settle()
                    c.step(dve.tensor_tensor(prod[:, 0:640], prod[:, 0:640], prod[:, 640:1280], ALU.add))
                    c.settle()
                    c.step(dve.tensor_tensor(prod[:, 0:320], prod[:, 0:320], prod[:, 320:640], ALU.add))
                    c.settle()
                    c.step(dve.tensor_tensor(prod[:, 0:320], prod[:, 0:320], prod[:, 1280:1600], ALU.add))
                    c.settle()
                    yield
                    dve.wait_ge(mo_products, (n * 2 + s + 1) * POOL_HEADS)
                    dve.tensor_tensor(Amix[:, s, :], prod[:, 0:320], prod[:, 1600:1920], ALU.add).then_inc(mix_ready, 1)
                for s in range(TILES):
                    yield
                    dve.wait_ge(swo_out, n * 2 + s + 1)
                    c.step(dve.tensor_tensor(X[:, s, :], mix_bank(s)[:, 0:D], hand[:, s, :], ALU.add))
                c.settle()
                yield from layer_norm(c, 6, lambda s: X[:, s, :])
                yield
                dve.wait_ge(BA.qT_psum, n + 1)
                rope = BA.AO[:, :, :].rearrange("p t q -> p (t q)"), BA.AOT[:, :, :].rearrange("p t q -> p (t q)")
                for k, tab in enumerate((cosT, sinT)):
                    c.step(dve.tensor_tensor(rope[k], BA.A(0)[:, 256 * k:256 * k + 256], tab, ALU.mult))
                c.settle()
                dve.tensor_tensor(BA.QT[:, :], rope[0], rope[1], ALU.add).then_inc(BA.qT_ready, 1)
                yield from softmax(c, E2, 2, 0, 4)
                yield from head_norms(c, 2, 0, 2)
                for s in range(TILES):
                    yield
                    dve.wait_ge(BA.proj_out, n * 2 + s + 1)
                    c.step(dve.tensor_tensor(X[:, s, :], BA.A(s)[:, 256:384], X[:, s, :], ALU.add))
                c.settle()
                yield from layer_norm(c, 7, lambda s: X[:, s, :])
                yield
                dve.wait_ge(router_psum, n + 1)
                c.step(dve.tensor_reduce(rmx[:, :, 0], BA.banks[0][:, 0:TILES * E3].rearrange("p (t e) -> p t e", t=TILES),
                                         X_AXIS, ALU.max))
                c.settle()
                dve.tensor_scalar(rmx[:, :, 1], rmx[:, :, 0], -1.0, None, ALU.mult).then_inc(rneg_ready, 1)

                def router_weights():
                    yield
                    dve.wait_ge(rexp_ready, n * 2 + 2)
                    c.step(dve.reciprocal(rmx[:, :, 3], rmx[:, :, 2]))
                    c.settle()
                    c.step(dve.tensor_tensor(pr[:, :, :], pr[:, :, :],
                                             rmx[:, :, 3].unsqueeze(2).to_broadcast([P, TILES, E3]), ALU.mult))
                    c.settle()
                    beats(c, cmp3[:, :, :, :], pr[:, :, :], E3)
                    c.settle()
                    c.step(dve.tensor_scalar(pr[:, :, :], pr[:, :, :], 0.5, None, ALU.mult))
                    c.step(dve.tensor_reduce(cnt3[:, :, :], cmp3[:, :, :, :], X_AXIS, ALU.add))
                    c.settle()
                    c.step(dve.scalar_tensor_tensor(wte[:, :, :], cnt3[:, :, :], SEL - 0.5, pr[:, :, :], ALU.is_lt, ALU.mult))

                def add_expert(e):
                    yield
                    dve.wait_ge(y_psum, n * E3 + e + 1)
                    c.settle()
                    for s in range(TILES):
                        last = e == E3 - 1
                        ins = dve.scalar_tensor_tensor(xall[:, 2 * n + s, :] if last else X[:, s, :],
                                                       BA.banks[0][:, s * D:(s + 1) * D], wte[:, s, e:e + 1], X[:, s, :],
                                                       ALU.mult, ALU.add)
                        if last:
                            ins.then_inc(out_ready, 1)
                        elif s == 0:
                            c.step(ins)
                        else:
                            ins.then_inc(y_used, 1)

                for u in range(UNITS):
                    m = CHUNKS[u % 3][1]
                    yield
                    dve.wait_ge(silu_in, n * UNITS + u + 1)
                    dve.scalar_tensor_tensor(T1[0:m, u % RING, :], TH[0:m, u % RING, :], 1.0, up_bank(u)[0:m, 0:256],
                                             ALU.add, ALU.mult).then_inc(t1_ready, 1)
                    if u == 1:
                        yield from router_weights()
                    if u >= 4 and u % 3 == 1:
                        yield from add_expert((u - 4) // 3)
                yield from add_expert(E3 - 1)
                assert c.count == B_STEPS, f"B_STEPS = {c.count}"

            weave(OPENING["dve"], front(0), prep())
            settle_prep()
            with dve.Fori(1, B) as i:
                weave(WEAVE["dve"], front(i), back(i - 1))
            alone(back(B - 1))

        @block.tensor
        def _(pe):
            pe.wait_ge(ld_a, 16)
            W = {k: part(wa_sb, WA, k) for k in WA}
            ctxT = W["ctxT"]

            def product(n):
                kind, c, _ = JOBS[n]
                last = n - 8 if n < FIRST_JOBS else max(n - 4, FIRST_JOBS - 1)
                if last >= 0:
                    if read_by("a", last):
                        pe.wait_ge(prep_act, read_by("a", last))
                    if read_by("d", last):
                        pe.wait_ge(prep_dve, read_by("d", last))
                bank = job_bank(n)
                if (kind, c) == ("M0", 0):
                    pe.wait_ge(ld_wq, 16)
                if (kind, c) == ("V0", 0):
                    pe.wait_ge(ld_wv, 32)
                if kind in ("K0", "V0"):
                    w = W["WkT" if kind == "K0" else "WvT"]
                    mm = pe.matmul(bank[:, 0:256], w[:, c * P:(c + 1) * P], ctxT, start=True, stop=True)
                elif kind == "M0":
                    pe.wait_ge(prep_act, read_by("a", JOB["K0", c]))
                    pe.wait_ge(prep_dve, read_by("d", JOB["K0", c]))
                    mm = pe.matmul(bank, W["Wq"][:, c * P:(c + 1) * P], KVbd[:, c, :, :].rearrange("p b k -> p (b k)"),
                                   start=True, stop=True)
                elif kind == "b0":
                    pe.wait_ge(ld_cols, 16)
                    pe.wait_ge(prep_act, read_by("a", JOB["K0", NC8 - 1]))
                    pe.wait_ge(prep_dve, read_by("d", JOB["K0", NC8 - 1]))
                    for b in range(B):
                        for cc in range(NC8):
                            mm = pe.matmul(bank[:, b * NC8 + cc:b * NC8 + cc + 1], KVbd[:, cc, b, :],
                                           part(cols_sb, COLS, "bq0")[:, cc:cc + 1], start=True, stop=True)
                elif kind == "VO":
                    pe.wait_ge(prep_act, read_by("a", JOB["V0", c]))
                    pe.wait_ge(prep_dve, read_by("d", JOB["V0", c]))
                    for b in range(B):
                        mm = pe.matmul(bank[:, b * P:(b + 1) * P], KVbd[:, c, b, :], W["WoT"][:, c * P:(c + 1) * P],
                                       start=True, stop=True)
                elif kind == "b0T":
                    pe.wait_ge(prep_dve, read_by("d", JOB["b0", 0]))
                    pe.wait_ge(consts_ready, 3)
                    mm = pe.transpose(bank.bitcast(BF16)[0:96, 0:P],
                                      bpart[:, :, :, :].rearrange("p r b c -> p (r b c)"), ident_bf[:, :])
                elif kind == "K1":
                    pe.wait_ge(ld_c, 32)
                    mm = pe.matmul(bank[:, 0:256], wcol("Wk1"), ctxT, start=True, stop=True)
                elif kind == "K3":
                    pe.matmul(bank[:, 0:256], wcol("Wk3"), ctxT, start=True, stop=True)
                    mm = pe.matmul(bank[:, 256:512], wcol("Wk3s"), ctxT, start=True, stop=True)
                elif kind in ("V1", "V3"):
                    for b in range(B):
                        mm = pe.matmul(bank[:, b * P:(b + 1) * P], ctxT2[:, b * P:(b + 1) * P],
                                       wcol("Wv1" if kind == "V1" else "Wv3"), start=True, stop=True)
                elif kind == "Lfc":
                    pe.wait_ge(ld_d, 48)
                    mm = pe.matmul(bank, lora_sb[:, 0:128], lora_sb[:, 128:640], start=True, stop=True)
                else:
                    for cc in range(FF // P):
                        mm = pe.matmul(bank[:, cc * P:(cc + 1) * P], loraB_sb[:, cc * P:(cc + 1) * P],
                                       loraB_sb[:, 512:640], start=True, stop=True)
                mm.then_inc(prep_mm, 1)

            for n in range(FIRST_JOBS):
                product(n)

            def prep():
                for n in range(FIRST_JOBS, len(JOBS)):
                    yield
                    product(n)

            pe.wait_ge(prep_act, read_by("a", FIRST_JOBS - 1))
            pe.wait_ge(prep_dve, read_by("d", FIRST_JOBS - 1))
            pe.wait_ge(memsets, 6)

            def x_transposed(h, n, l):
                k = TILES * h.norms.index(l)
                for s in range(TILES):
                    yield
                    pe.wait_ge(h.xhat_ready, n * h.n_xt + k + s + 1)
                    pe.transpose(h.Bk(s)[:, 0:P], h.XH[:, s, :], ident).then_inc(h.xT_psum, 1)

            def xt_wait(h, n, l, s):
                pe.wait_ge(h.xT_ready, n * h.n_xt + TILES * h.norms.index(l) + s + 1)

            def xt(h, s):
                return h.XT[:, s * P:(s + 1) * P]

            def probs_transposed(hf, n, E, k0, per):
                for s in range(TILES):
                    for h in range(2):
                        if hf is FR and k0 == 0:
                            yield
                            pe.wait_ge(norm_second if h else norm_first, n * 2 + s + 1)
                        else:
                            yield
                            pe.wait_ge(hf.exp_ready, n * per + k0 + 2 * s + h + 1)
                        for c in range(4):
                            mm = pe.transpose(hf.bank(s, h)[:, c * P:(c + 1) * P],
                                              E[:, s, 512 * h + c * P:512 * h + (c + 1) * P], ident)
                        mm.then_inc(hf.pT_psum, 1)

            def small_values(hf, n, E, a, k0, per):
                for s in range(TILES):
                    yield
                    pe.wait_ge(hf.pT_ready, n * per + k0 + 2 * s + 2)
                    for c in range(NC8):
                        mm = pe.matmul(hf.A(s)[:, 18 * c:18 * c + 18], E[:, s, c * P:(c + 1) * P], Vbd[a][:, n, c, :],
                                       start=True, stop=True)
                    mm.then_inc(hf.attn_out, 1)

            def project(hf, n, w):
                for s in range(TILES):
                    yield
                    pe.wait_ge(hf.heads_ready, n * 2 + s + 1)
                    pe.transpose(hf.Bk(s)[:, 0:P], hf.AO[:, s, :], ident).then_inc(hf.headsT_psum, 1)
                for s in range(TILES):
                    yield
                    pe.wait_ge(hf.headsT_ready, n * 2 + s + 1)
                    pe.matmul(hf.A(s)[:, 256:384], hf.AOT[:, s, :], wcol(w), start=True, stop=True).then_inc(hf.proj_out, 1)

            def front(n):
                yield from x_transposed(FR, n, 0)
                yield
                pe.wait_ge(bias_rows, 16 * (B + 3))
                for s in range(TILES):
                    if s:
                        yield
                    xt_wait(FR, n, 0, s)
                    for h in range(2):
                        pe.matmul(FR.bank(s, h), xt(FR, s), M0[:, n, 4 * h:4 * h + 4, :].rearrange("p c k -> p (c k)"),
                                  start=True, stop=False)
                        pe.matmul(FR.bank(s, h), ones_bf[:, :], bias0[:, n, 512 * h:512 * h + 512], start=False,
                                  stop=True).then_inc(FR.scores_ready, 1)
                yield from probs_transposed(FR, n, E1, 0, 8)
                yield
                pe.wait_ge(prep_act, read_by("a", JOB["VO", NC8 - 1]))
                pe.wait_ge(prep_dve, read_by("d", JOB["VO", NC8 - 1]))
                for s in range(TILES):
                    if s:
                        yield
                    pe.wait_ge(FR.pT_ready, n * 8 + 2 * s + 2)
                    for c in range(NC8):
                        mm = pe.matmul(FR.A(s)[:, 0:D], E1[:, s, c * P:(c + 1) * P], VO0[:, n, c, :], start=(c == 0),
                                       stop=(c == NC8 - 1))
                    mm.then_inc(FR.attn_out, 1)
                yield
                pe.wait_ge(ternary_ready, 2)
                for s in range(TILES):
                    if s:
                        yield
                    pe.wait_ge(quant_ready, n * 4 + s + 1)
                    pe.transpose(FR.Bk(s).bitcast(BF16)[:, 0:P], qbf[:, s, 0:P], ident_bf[:, :]).then_inc(quantT_psum, 1)
                for s in range(TILES):
                    yield
                    pe.wait_ge(quantT_ready, n * 4 + s + 1)
                    pe.matmul(FR.A(s), qTbf[:, s, 0:P], w1q[:, :], start=True, stop=True).then_inc(bit_out, 1)
                for s in range(TILES):
                    yield
                    pe.wait_ge(quant_ready, n * 4 + 2 + s + 1)
                    for c in range(FF // P):
                        mm = pe.transpose(FR.Bk(s).bitcast(BF16)[:, c * P:(c + 1) * P], qbf[:, s, c * P:(c + 1) * P],
                                          ident_bf[:, :])
                    mm.then_inc(quantT_psum, 1)
                for s in range(TILES):
                    yield
                    pe.wait_ge(quantT_ready, n * 4 + 2 + s + 1)
                    for c in range(FF // P):
                        mm = pe.matmul(FR.A(s)[:, 0:D], qTbf[:, s, c * P:(c + 1) * P], w2q[:, c, :], start=(c == 0),
                                       stop=(c == FF // P - 1))
                    mm.then_inc(bit_out, 1)
                yield from x_transposed(FR, n, 2)
                yield
                pe.wait_ge(ld_c, 32)
                xt_wait(FR, n, 2, 1)
                pe.matmul(FR.A(0)[:, 0:256], wcol("Wq1"), FR.XT[:, :], start=True, stop=True).then_inc(FR.qT_psum, 1)
                yield
                pe.wait_ge(kbd1_ready, n + 1)
                pe.wait_ge(FR.qT_ready, n + 1)
                for s in range(TILES):
                    for h in range(2):
                        pe.matmul(FR.bank(s, h), FR.QT[:, s * P:(s + 1) * P],
                                  Kbd[1][:, 8 * h:8 * h + 8, :].rearrange("p n k -> p (n k)"), start=True, stop=False)
                        pe.matmul(FR.bank(s, h), ident_bf[:, :], mneg1[:, s, :].unsqueeze(1).to_broadcast([P, 8, CTX]),
                                  start=False, stop=True).then_inc(FR.scores_ready, 1)
                yield from probs_transposed(FR, n, E1, 4, 8)
                yield from small_values(FR, n, E1, 1, 4, 8)
                yield from project(FR, n, "Wo1")
                yield from x_transposed(FR, n, 3)
                yield
                pe.wait_ge(prep_dve, read_by("d", len(JOBS)))
                xt_wait(FR, n, 3, 1)
                for c in range(FF // P):
                    pe.matmul(FR.banks[c][:, 0:256], wfc[:, c * P:(c + 1) * P], FR.XT[:, :],
                              start=True, stop=True).then_inc(fc_psum, 1)
                for s in range(TILES):
                    yield
                    pe.wait_ge(fc_gelu, n * 4 + 4)
                    for c in range(FF // P):
                        mm = pe.matmul(FR.A(s)[:, 0:D], GT[:, c, s * P:(s + 1) * P], wpj[:, c, :], start=(c == 0),
                                       stop=(c == FF // P - 1))
                    mm.then_inc(pj_out, 1)
                yield from x_transposed(FR, n, 4)
                yield
                pe.wait_ge(ld_e, 80)
                for s in range(TILES):
                    if s:
                        yield
                    xt_wait(FR, n, 4, s)
                    pe.matmul(FR.A(s)[:, 0:CTX], xt(FR, s), ctxT_sb[:, n, :], start=True, stop=False)
                    pe.matmul(FR.A(s)[:, 0:CTX], ones_bf[0:1, :], mneg2[:, n, :], start=False, stop=True).then_inc(sx_psum, 1)
                for s in range(TILES):
                    yield
                    pe.wait_ge(sx_exp, n * 2 + s + 1)
                    pe.matmul(FR.Bk(s)[0:CTX, 0:P], E1[:, s, 0:CTX], ident, start=True, stop=True).then_inc(sxT_psum, 1)
                for s in range(TILES):
                    if s == 0:
                        yield
                        pe.wait_ge(ctxb_ready, n + 1)
                    pe.wait_ge(sxT_ready, n * 2 + s + 1)
                    pe.matmul(FR.A(s)[:, 128:256], E1[0:CTX, s, P:2 * P], ctxb[:, :], start=True, stop=True).then_inc(sx_out, 1)
                yield from x_transposed(FR, n, 5)
                for s in range(TILES):
                    yield
                    xt_wait(FR, n, 5, s)
                    pe.matmul(FR.A(s)[:, 0:400], xt(FR, s), part(we_sb, WE, "VSD"), start=True, stop=True).then_inc(gate_psum, 1)
                for w, name in enumerate(("Wq", "Wk")):
                    if w == 1:
                        yield
                        pe.wait_ge(gate_ready, n * 2 + 2)
                    for c in range(H2 // 2):
                        bank = (FR.Bk, FR.A)[w](c // 2)
                        mm = pe.matmul(bank[:, (c % 2) * 256:(c % 2) * 256 + 256], part(we_sb, WE, name)[:, c * P:(c + 1) * P],
                                       FR.XT[:, :], start=True, stop=True)
                        if c % 2:
                            mm.then_inc(qf_psum, 1)

            def up(n, u):
                e, c = divmod(u, 3)
                i0, m = CHUNKS[c]
                if u >= UP_BANKS:
                    yield
                    pe.wait_ge(t1_ready, n * UNITS + u - UP_BANKS + 1)
                for w in range(2):
                    mm = pe.matmul(up_bank(u)[0:m, 256 * w:256 * w + 256], gu_sb[:, w, e * I3 + i0:e * I3 + i0 + m],
                                   BA.XT[:, :], start=True, stop=True)
                mm.then_inc(up_psum, 1)

            def down_product(n, u):
                e, c = divmod(u, 3)
                m = CHUNKS[c][1]
                yield
                if c == 0:
                    if e:
                        pe.wait_ge(y_used, n * (E3 - 1) + e)
                    else:
                        pe.wait_ge(rexp_ready, n * 2 + 2)
                pe.wait_ge(h_ready, n * UNITS + u + 1)
                for s in range(TILES):
                    mm = pe.matmul(BA.banks[0][:, s * D:(s + 1) * D], HT[0:m, u % RING, s * P:(s + 1) * P],
                                   dn_sb[0:m, e, c, :], start=(c == 0 and s == 0), stop=(c == 2 and s == TILES - 1))
                if c == 2:
                    mm.then_inc(y_psum, 1)

            def back(n):
                def heads_product(j):
                    s, c = divmod(j, 4)
                    for h in (2 * c, 2 * c + 1):
                        for b in range(2):
                            mm = pe.matmul(heads_out(s)[:, h * DH2:(h + 1) * DH2], EF[:, s, h, b * P:(b + 1) * P],
                                           V[:, b, h * DH2:(h + 1) * DH2], start=(b == 0), stop=(b == 1))
                    if c == 3:
                        mm.then_inc(pv_out, 1)

                yield
                pe.wait_ge(qf_ready, n * 2 + 2)
                pe.wait_ge(kfa_ready, n * 2 + 2)
                pe.wait_ge(kfd_ready, n * 2 + 2)
                for k in range(HEAD_UNITS + 2):
                    if k >= 2:
                        j = k - 2
                        s, c = divmod(j, 4)
                        yield
                        pe.wait_ge(ef_ready, n * 16 + 2 * j + 2)
                        for g in range(2):
                            for q in range(2):
                                mm = pe.transpose(head_bank(j)[:, g * S + q * P:g * S + (q + 1) * P],
                                                  EF[:, s, 2 * c + g, q * P:(q + 1) * P], ident)
                        mm.then_inc(pf_psum, 1)
                    if k < HEAD_UNITS:
                        s, c = divmod(k, 4)
                        if k >= HEAD_BANKS:
                            yield
                            pe.wait_ge(pf_ready, n * HEAD_UNITS + k - HEAD_BANKS + 1)
                        pe.matmul(head_bank(k), QF[:, c, s * P:(s + 1) * P], KFbd[:, c, :, :].rearrange("p h k -> p (h k)"),
                                  start=True, stop=True).then_inc(sf_psum, 1)
                    if k >= PV_LAG:
                        j = k - PV_LAG
                        if j < 4:
                            yield
                            if j == 0:
                                pe.wait_ge(v_first, n + 1)
                                pe.wait_ge(v_second, n + 1)
                            pe.wait_ge(pf_ready, n * HEAD_UNITS + j + 1)
                            heads_product(j)
                for j in range(4, HEAD_UNITS):
                    yield
                    pe.wait_ge(pf_ready, n * HEAD_UNITS + HEAD_UNITS)
                    heads_product(j)
                for s in range(TILES):
                    yield
                    pe.wait_ge(mix_ready, n * 2 + s + 1)
                    pe.transpose(mix_bank(s)[:, 0:128], Amix[:, s, 0:128], ident)
                    pe.transpose(mix_bank(s)[:, 128:256], Amix[:, s, 128:256], ident)
                    pe.transpose(mix_bank(s)[0:64, 256:384], Amix[:, s, 256:320], ident).then_inc(mixT_psum, 1)
                for s in range(TILES):
                    yield
                    pe.wait_ge(mixT_ready, n * 2 + s + 1)
                    bank = mix_bank(s)[:, 0:D]
                    pe.matmul(bank, AT[:, s, 0, :], wo2_sb[:, 0, :], start=True, stop=False)
                    pe.matmul(bank, AT[:, s, 1, :], wo2_sb[:, 1, :], start=False, stop=False)
                    pe.matmul(bank, AT[0:64, s, 2, :], wo2b_sb[:, :], start=False, stop=True).then_inc(swo_out, 1)
                yield from x_transposed(BA, n, 6)
                yield
                xt_wait(BA, n, 6, 1)
                pe.matmul(BA.A(0)[:, 0:256], wcol("Wq3"), BA.XT[:, :], start=True, stop=True)
                pe.matmul(BA.A(0)[:, 256:512], wcol("Wq3s"), BA.XT[:, :], start=True, stop=True).then_inc(BA.qT_psum, 1)
                yield
                pe.wait_ge(kbd3_ready, n + 1)
                pe.wait_ge(BA.qT_ready, n + 1)
                for s in range(TILES):
                    for h in range(2):
                        pe.matmul(BA.bank(s, h), BA.QT[:, s * P:(s + 1) * P],
                                  Kbd[2][:, 8 * h:8 * h + 8, :].rearrange("p n k -> p (n k)"), start=True,
                                  stop=True).then_inc(BA.scores_ready, 1)
                yield from probs_transposed(BA, n, E2, 0, 4)
                yield from small_values(BA, n, E2, 2, 0, 4)
                yield from project(BA, n, "Wo3")
                yield from x_transposed(BA, n, 7)
                for s in range(TILES):
                    yield
                    xt_wait(BA, n, 7, s)
                    mm = pe.matmul(router_out(s), xt(BA, s), part(we_sb, WE, "router"), start=True, stop=True)
                mm.then_inc(router_psum, 1)
                yield
                pe.wait_ge(ld_moe, 64)
                for u in range(UNITS):
                    yield from up(n, u)
                    if u >= LAG and (u - LAG) % 3 == 1:
                        yield from down_product(n, u - LAG - 1)
                    if u >= LAG and (u - LAG) % 3 != 0:
                        yield from down_product(n, u - LAG)
                for u in range(UNITS - LAG - 1, UNITS):
                    yield from down_product(n, u)

            weave(OPENING["pe"], front(0), prep())
            pe.wait_ge(ld_e, 80)
            with pe.Fori(1, B) as i:
                weave(WEAVE["pe"], front(i), back(i - 1))
            alone(back(B - 1))


def rope_tables():
    inv = (1.0 / np.float32(10000.0) ** (np.arange(0, 8, 2, dtype=np.float32) / np.float32(8))).astype(np.float32)
    freqs = np.outer(np.arange(S, dtype=np.float32), inv).astype(np.float32)
    d = np.arange(P) % 8
    cos = np.cos(freqs).T[d // 2]
    sin = np.sin(freqs).T[d // 2] * np.where(d % 2 == 0, -1.0, 1.0)[:, None]
    return cos.astype(np.float32), sin.astype(np.float32)


def chunked(a):
    return a.reshape(-1, P, a.shape[1]).transpose(1, 0, 2).reshape(P, -1)


def kernel(**inputs):
    import concourse.bacc as bacc
    from concourse.bass_utils import run_bass_kernel_spmd

    a = {k: np.asarray(v) for k, v in inputs.items()}
    cat = lambda *parts: np.ascontiguousarray(np.concatenate(parts, axis=1))
    col = lambda v: v.reshape(-1, P).T
    ctx = a["ctx_1024"]
    ctxT = ctx.reshape(B * CTX, D).T
    ctxT2 = np.stack([ctx, ctx], axis=1).reshape(2 * B * CTX, D).T
    swap = np.arange(P) ^ 1
    cos, sin = rope_tables()
    block = (np.arange(P)[:, None] // 8 == np.arange(16)[None, :]).astype(np.float32)
    w3q, w3k = a["L3_xattn_Wq"], a["L3_xattn_Wk"]
    wv2 = a["L2_ffn_Wv"].transpose(1, 0, 2).reshape(D, XV)
    arrays = {
        "x": a["x"].reshape(B * S, D),
        "wa": cat(ctxT, a["L0_xattn_Wk"].T, a["L0_xattn_Wv"].T, chunked(a["L0_xattn_Wq"]), chunked(a["L0_xattn_Wo"].T)),
        "cols": cat(col(a["L0_xattn_bq"]), col(a["L0_xattn_bk"]), col(a["L0_xattn_bv"]), col(a["L1_xattn_bq"]),
                    col(a["L1_xattn_bk"]), col(a["L1_ffn_b_fc"])),
        "rows": cat(*(a[n][None, :] for n in ("L0_xattn_bo", "L0_ffn_b2", "L1_xattn_bo", "L1_ffn_b_proj", "L0_ffn_b1",
                                              "L1_xattn_bv"))),
        "wb": cat(a["L0_ffn_w1"].T, chunked(a["L0_ffn_w2"].T)),
        "wc": cat(a["L1_xattn_Wq"].T, a["L1_xattn_Wk"].T, a["L1_xattn_Wv"].T, a["L1_xattn_Wo"].T, w3q.T, w3q[swap].T,
                  w3k.T, w3k[swap].T, a["L3_xattn_Wv"].T, a["L3_xattn_Wo"].T, ctxT2),
        "wd": cat(a["L1_ffn_W_fc"].T, chunked(a["L1_ffn_W_proj"].T)),
        "lora": cat(a["L1_ffn_A_fc"], a["L1_ffn_B_fc"].T, a["L1_ffn_A_proj"], a["L1_ffn_B_proj"].T),
        "we": cat(a["L2_ffn_Wq"], a["L2_ffn_Wk"], wv2, a["L2_ffn_Ws"], a["L2_ffn_Wd"], a["L3_ffn_router_w"].T),
        "wo2": a["L2_ffn_Wo"].reshape(XV, D),
        "ctxn": ctx,
        "gateup": np.ascontiguousarray(np.stack([a["L3_ffn_gate_w"].transpose(2, 0, 1).reshape(D, -1),
                                                 a["L3_ffn_up_w"].transpose(2, 0, 1).reshape(D, -1)], axis=1)),
        "down": np.ascontiguousarray(a["L3_ffn_down_w"].transpose(0, 2, 1)),
        "const": cat(np.eye(P, dtype=np.float32), cos, sin, block),
        "mask0": a["mask_BxS2_bk0"].reshape(1, B * CTX).view(np.int32),
        "mask1": a["mask_1x1xSxS2_ik0"].reshape(S, CTX),
        "mask2": a["mask_BxS2_ik1"].reshape(1, B, CTX),
    }
    arrays = {f"in_{k}": np.ascontiguousarray(v) for k, v in arrays.items()}
    nc = bacc.Bacc("TRN2", target_bir_lowering=False, num_devices=1)
    args = [nc.dram_tensor(k, v.shape, mybir.dt.from_np(v.dtype), kind="ExternalInput").ap() for k, v in arrays.items()]
    args.append(nc.dram_tensor("out_0_dram", (B * S, D), F32, kind="ExternalOutput").ap())
    build(nc, *args)
    r = run_bass_kernel_spmd(nc, [arrays], core_ids=[0])
    return r.results[0]["out_0_dram"].reshape(B, S, D)
```
